# Optimizing a Trainium2 kernel written in Bass

```python
import numpy as np
import jax
import jax.numpy as jnp

def _softmax(x, axis=-1):
    return jax.nn.softmax(x, axis=axis)

def _gelu(x):
    return jax.nn.gelu(x, approximate=True)

def _silu(x):
    return jax.nn.silu(x)

def _sigmoid(x):
    return jax.nn.sigmoid(x)

def _layernorm(x, axis=-1, eps=1e-05):
    m = jnp.mean(x, axis=axis, keepdims=True)
    v = jnp.var(x, axis=axis, keepdims=True)
    return (x - m) / jnp.sqrt(v + eps)

def _scatter_add(tgt, idx, src, axis=0):
    return tgt.at[idx].add(src)

def _segment_sum(src, seg, n):
    return jax.ops.segment_sum(src, seg, n)
kernel_name = 'mk_gnn_resnorm_d4_gnn_r64_de523f'

def setup_inputs(seed: int=0):
    np.random.seed(seed)
    _w = jnp.asarray

    def _rec_inputs():
        import jax
        import jax.numpy as jnp
        _gk = jax.random.key(seed)
        x = -0.000202 + 1 * jax.random.normal(jax.random.fold_in(_gk, 1), (100000, 64), jnp.float32)
        src = jax.random.randint(jax.random.fold_in(_gk, 2), (50000,), 0, 100000, jnp.int32)
        dst = jnp.minimum((100000 * jax.random.uniform(jax.random.fold_in(_gk, 3), (50000,)) ** 2.0).astype(jnp.int32), 99999)
        _o = jnp.argsort(dst, stable=True)
        src = src[_o]
        dst = dst[_o]
        edge_attr_16 = 0.000254156 + 0.999948 * jax.random.normal(jax.random.fold_in(_gk, 12), (50000, 16), jnp.float32)
        return (x, src, dst, edge_attr_16)
    x, src, dst, edge_attr_16 = _rec_inputs()

    def _L0_gnn_setup():
        import jax, jax.numpy as jnp
        import numpy as np
        N_NODES = 100000
        N_EDGES = 1250000
        D = 64

        def _gcn_conv(x, W, b, src, dst, norm):
            h = x @ W
            msgs = h[src] * norm[:, None]
            out = jax.ops.segment_sum(msgs, dst, num_segments=x.shape[0])
            return out + b
        key = jax.random.key(seed)
        k1, k2, k3, k4 = jax.random.split(key, 4)
        x = jax.random.normal(k1, (N_NODES, D), dtype=jnp.float32)
        edge_index = jax.random.randint(k2, (2, N_EDGES), 0, N_NODES, dtype=jnp.int32)
        W1 = jax.random.normal(k3, (D, D), dtype=jnp.float32) * (1.0 / np.sqrt(D))
        b1 = jnp.zeros((D,), dtype=jnp.float32)
        W2 = jax.random.normal(k4, (D, D), dtype=jnp.float32) * (1.0 / np.sqrt(D))
        b2 = jnp.zeros((D,), dtype=jnp.float32)
        return {'x': x, 'edge_index': edge_index, 'W1': W1, 'b1': b1, 'W2': W2, 'b2': b2}
    _L0_gnn_all = _L0_gnn_setup()
    _L0_gnn_in = {k: v for k, v in _L0_gnn_all.items() if k in ('W1', 'b1', 'W2', 'b2')}
    del _L0_gnn_all

    def _L1_gnn_setup():
        import jax, jax.numpy as jnp
        import numpy as np
        K_LAYERS = 10
        ALPHA = 0.1
        N_NODES = 100000
        N_EDGES = 25000
        D_FEAT = 64
        key = jax.random.key(seed)
        k1, k2, k3 = jax.random.split(key, 3)
        features = jax.random.normal(k1, (N_NODES, D_FEAT), dtype=jnp.float32)
        src = jax.random.randint(k2, (N_EDGES,), 0, N_NODES, dtype=jnp.int64)
        dst = jax.random.randint(k3, (N_EDGES,), 0, N_NODES, dtype=jnp.int64)
        return {'features': features, 'src': src, 'dst': dst}
    _L1_gnn_all = _L1_gnn_setup()
    _L1_gnn_in = {k: v for k, v in _L1_gnn_all.items() if k in ()}
    del _L1_gnn_all

    def _L2_gnn_setup():
        import jax, jax.numpy as jnp
        import numpy as np
        N = 50000
        E = 12500
        D = 64
        EDGE_DIM = 16
        L = 3
        MSG_IN = 2 * D + EDGE_DIM
        UPD_IN = D + D
        key = jax.random.key(seed)
        ks = jax.random.split(key, 8)
        x = jax.random.normal(ks[0], (N, D), dtype=jnp.float32)
        edge_index = jax.random.randint(ks[1], (2, E), 0, N, dtype=jnp.int64)
        edge_attr = jax.random.normal(ks[2], (E, EDGE_DIM), dtype=jnp.float32)
        sc_m = 1.0 / np.sqrt(MSG_IN)
        sc_u = 1.0 / np.sqrt(UPD_IN)
        msg_w = jax.random.uniform(ks[3], (L, MSG_IN, D), jnp.float32, -sc_m, sc_m)
        msg_b = jax.random.uniform(ks[4], (L, D), jnp.float32, -sc_m, sc_m)
        upd_w = jax.random.uniform(ks[5], (L, UPD_IN, D), jnp.float32, -sc_u, sc_u)
        upd_b = jax.random.uniform(ks[6], (L, D), jnp.float32, -sc_u, sc_u)
        return {'x': x, 'edge_index': edge_index, 'edge_attr': edge_attr, 'msg_w': msg_w, 'msg_b': msg_b, 'upd_w': upd_w, 'upd_b': upd_b}
    _L2_gnn_all = _L2_gnn_setup()
    _L2_gnn_in = {k: v for k, v in _L2_gnn_all.items() if k in ('msg_w', 'msg_b', 'upd_w', 'upd_b')}
    del _L2_gnn_all

    def _L3_gnn_setup():
        import jax, jax.numpy as jnp
        import numpy as np
        N_NODES = 50000
        N_EDGES = 12500
        IN_C = 64
        key = jax.random.key(seed)
        ks = jax.random.split(key, 7)
        c2 = 2 * IN_C
        return {'features': jax.random.normal(ks[0], (N_NODES, IN_C), dtype=jnp.float32), 'W_lin': jax.random.normal(ks[1], (c2, c2), dtype=jnp.float32) / np.sqrt(c2), 'b_lin': jax.random.normal(ks[2], (c2,), dtype=jnp.float32) * 0.01, 'W_out': jax.random.normal(ks[3], (IN_C, c2), dtype=jnp.float32) / np.sqrt(c2), 'b_out': jax.random.normal(ks[4], (IN_C,), dtype=jnp.float32) * 0.01, 'src': jax.random.randint(ks[5], (N_EDGES,), 0, N_NODES, dtype=jnp.int32), 'dst': jax.random.randint(ks[6], (N_EDGES,), 0, N_NODES, dtype=jnp.int32)}
    _L3_gnn_all = _L3_gnn_setup()
    _L3_gnn_in = {k: v for k, v in _L3_gnn_all.items() if k in ('W_lin', 'b_lin', 'W_out', 'b_out')}
    del _L3_gnn_all
    return {'x': x, 'src': src, 'dst': dst, 'edge_attr_16': edge_attr_16, 'L0_gnn_W1': _L0_gnn_in['W1'], 'L0_gnn_b1': _L0_gnn_in['b1'], 'L0_gnn_W2': _L0_gnn_in['W2'], 'L0_gnn_b2': _L0_gnn_in['b2'], 'L2_gnn_msg_w': _L2_gnn_in['msg_w'], 'L2_gnn_msg_b': _L2_gnn_in['msg_b'], 'L2_gnn_upd_w': _L2_gnn_in['upd_w'], 'L2_gnn_upd_b': _L2_gnn_in['upd_b'], 'L3_gnn_W_lin': _L3_gnn_in['W_lin'], 'L3_gnn_b_lin': _L3_gnn_in['b_lin'], 'L3_gnn_W_out': _L3_gnn_in['W_out'], 'L3_gnn_b_out': _L3_gnn_in['b_out']}

def reference(x, src, dst, edge_attr_16, L0_gnn_W1, L0_gnn_b1, L0_gnn_W2, L0_gnn_b2, L2_gnn_msg_w, L2_gnn_msg_b, L2_gnn_upd_w, L2_gnn_upd_b, L3_gnn_W_lin, L3_gnn_b_lin, L3_gnn_W_out, L3_gnn_b_out):
    import jax
    import jax.numpy as jnp

    def _L0_gnn_ref(x, edge_index, W1, b1, W2, b2):
        import jax, jax.numpy as jnp
        import numpy as np
        N_NODES = 100000
        N_EDGES = 1250000
        D = 64

        def _gcn_conv(x, W, b, src, dst, norm):
            h = x @ W
            msgs = h[src] * norm[:, None]
            out = jax.ops.segment_sum(msgs, dst, num_segments=x.shape[0])
            return out + b
        n = x.shape[0]
        loops = jnp.arange(n, dtype=edge_index.dtype)
        src = jnp.concatenate([edge_index[0], loops])
        dst = jnp.concatenate([edge_index[1], loops])
        deg = jax.ops.segment_sum(jnp.ones_like(dst, dtype=x.dtype), dst, num_segments=n)
        dis = jnp.where(deg > 0, jax.lax.rsqrt(deg), 0.0)
        norm = dis[src] * dis[dst]
        identity = x
        h = jax.nn.relu(_gcn_conv(x, W1, b1, src, dst, norm))
        h = jax.nn.relu(_gcn_conv(h, W2, b2, src, dst, norm))
        return h + identity

    def _L1_gnn_ref(features, src, dst):
        import jax, jax.numpy as jnp
        import numpy as np
        K_LAYERS = 10
        ALPHA = 0.1
        N_NODES = 100000
        N_EDGES = 25000
        D_FEAT = 64
        n = features.shape[0]
        ones = jnp.ones((src.shape[0],), dtype=features.dtype)
        deg_out = jax.ops.segment_sum(ones, src, num_segments=n)
        deg_in = jax.ops.segment_sum(ones, dst, num_segments=n)
        norm_src = jnp.clip(deg_out, 1.0) ** (-0.5)
        norm_dst = jnp.clip(deg_in, 1.0) ** (-0.5)
        h0 = features
        h = features
        for _ in range(K_LAYERS):
            msg = (h * norm_src[:, None])[src]
            agg = jax.ops.segment_sum(msg, dst, num_segments=n)
            h = (1.0 - ALPHA) * (agg * norm_dst[:, None]) + ALPHA * h0
        return h

    def _L2_gnn_ref(x, edge_index, edge_attr, msg_w, msg_b, upd_w, upd_b):
        import jax, jax.numpy as jnp
        import numpy as np
        N = 50000
        E = 12500
        D = 64
        EDGE_DIM = 16
        L = 3
        MSG_IN = 2 * D + EDGE_DIM
        UPD_IN = D + D
        src = edge_index[0]
        dst = edge_index[1]
        n = x.shape[0]
        num_layers = msg_w.shape[0]
        for l in range(num_layers):
            x_i = x[dst]
            x_j = x[src]
            m_in = jnp.concatenate([x_i, x_j, edge_attr], axis=1)
            m = jax.nn.relu(m_in @ msg_w[l] + msg_b[l])
            agg = jax.ops.segment_sum(m, dst, num_segments=n)
            u_in = jnp.concatenate([x, agg], axis=1)
            x = jax.nn.relu(u_in @ upd_w[l] + upd_b[l])
        return x

    def _L3_gnn_ref(features, W_lin, b_lin, W_out, b_out, src, dst):
        import jax, jax.numpy as jnp
        import numpy as np
        N_NODES = 50000
        N_EDGES = 12500
        IN_C = 64
        n_nodes = features.shape[0]
        ef = jnp.concatenate([features[src], features[dst]], axis=-1)
        att = jax.nn.relu(ef @ W_lin.T + b_lin)
        mx = jax.ops.segment_max(att, dst, num_segments=n_nodes)
        ex = jnp.exp(att - mx[dst])
        den = jax.ops.segment_sum(ex, dst, num_segments=n_nodes)
        alpha = ex / den[dst]
        new_features = jax.ops.segment_sum(alpha * ef, dst, num_segments=n_nodes)
        return new_features @ W_out.T + b_out
    edge_index = jnp.stack([src, dst])
    x = _layernorm(x + _L0_gnn_ref(x, edge_index, L0_gnn_W1, L0_gnn_b1, L0_gnn_W2, L0_gnn_b2), axis=-1)
    x = _layernorm(x + _L1_gnn_ref(x, src, dst), axis=-1)
    x = _layernorm(x + _L2_gnn_ref(x, edge_index, edge_attr_16, L2_gnn_msg_w, L2_gnn_msg_b, L2_gnn_upd_w, L2_gnn_upd_b), axis=-1)
    x = _layernorm(x + _L3_gnn_ref(x, L3_gnn_W_lin, L3_gnn_b_lin, L3_gnn_W_out, L3_gnn_b_out, src, dst), axis=-1)
    return x

_drawn_inputs = setup_inputs


def setup_inputs(seed=0):
    import zlib

    import numpy as np

    out = dict(_drawn_inputs(seed))
    spreads = {'L0_gnn_b1': (0.0, 0.309), 'L0_gnn_b2': (0.0, 0.1)}
    factors = {'L2_gnn_msg_b': 6.786, 'L3_gnn_b_lin': 8.0, 'L3_gnn_b_out': 6.512}
    for name, (base, spread) in spreads.items():
        noise = np.random.default_rng([zlib.crc32(name.encode()), seed]).standard_normal(out[name].shape)
        drawn = base * np.exp(spread * noise) if base else spread * noise
        out[name] = jnp.asarray(drawn.astype(out[name].dtype))
    for name, factor in factors.items():
        out[name] = (out[name] * factor).astype(out[name].dtype)
    return out
```

```python
import concourse.bass as bass
from concourse import mybir
from contextlib import ExitStack, contextmanager

N_NODES = 100000
N_EDGES = 50000
D = 64
EDGE_DIM = 16
APPNP_STEPS = 10
ALPHA = 0.1
EPS = 1e-5

P = 128
SUP = 1024
HALF = 512
QJ = HALF // P
NS = -(-N_EDGES // (2 * SUP)) * 2
EP = NS * SUP
NQ = EP // P
LO = 1024
HI = -(-N_NODES // LO)
PAD_NODE = HI * LO - 1
CREDIT = 4


def build(nc, x, src, dst, edge_attr, W1, b1, W2, b2, msg_w, msg_b, upd_w, upd_b,
          W_lin, b_lin, W_out, b_out, out):
    f32, f16, bf16, i32 = (mybir.dt.float32, mybir.dt.float16, mybir.dt.bfloat16, mybir.dt.int32)
    ALU = mybir.AluOpType
    ACT = mybir.ActivationFunctionType
    assert PAD_NODE >= N_NODES

    ctx = ExitStack()

    def sb(name, shape, dt=f32):
        return ctx.enter_context(nc.sbuf_tensor(name, shape, dt))

    def dram(name, shape, dt=f32):
        return nc.dram_tensor(name, shape, dt).ap()

    src_pad = dram("src_pad", [EP], i32)
    dst_pad = dram("dst_pad", [EP + 2], i32)
    attr_pad = dram("attr_pad", [EP, EDGE_DIM])
    node_table = dram("node_table", [P * LO, 8])
    tab = [dram(f"tab{i}", [EP + P, D]) for i in range(2)]
    totT = [dram(f"totT{i}", [NS, D, SUP]) for i in range(2)]
    maxT = dram("maxT", [NS, P, SUP])
    mask_dram = {d: dram(f"mask{d}", [NS, SUP], bf16) for d in "FR"}
    row_names = ["dis_d", "dis_s", "nsrc_s", "ndst_d", "ndst_s"]
    rows = {r: dram(f"row_{r}", [NS, SUP]) for r in row_names}
    st = {n: dram(f"state_{n}", [NS, P, SUP]) for n in ("X0", "V0", "V1", "X1", "X2", "XA", "XB", "X3")}
    attrT = dram("attrT", [NS, EDGE_DIM, SUP])

    ident = sb("ident", [P, P])
    avg = sb("avg", [P, P])
    center = sb("center", [P, P])
    before = sb("before", [P, P])
    W1b, W2b = sb("W1b", [P, P]), sb("W2b", [P, P])
    Wm = sb("Wm", [P, 3, P])
    We = sb("We", [P, 3, P])
    Wu1, Wu2 = sb("Wu1", [P, 3, P]), sb("Wu2", [P, 3, P])
    Wl_raw, Wo_raw = sb("Wl_raw", [P, P]), sb("Wo_raw", [P, P])
    WlT, WoT = sb("WlT", [P, P]), sb("WoT", [P, P])
    bias = sb("bias", [P, 12])
    B1, B2, BL, BO, BEPS, BZ, BM, BU = 0, 1, 2, 3, 4, 5, 6, 9
    idx_src_gl = sb("idx_src_gl", [P, NQ], i32)
    idx_src_gf = sb("idx_src_gf", [P, NQ], i32)
    idx_out = sb("idx_out", [P, NQ], i32)
    a_src = sb("a_src", [P, NQ])

    begun = ctx.enter_context(nc.semaphore("begun"))
    pass_no = [0]
    wait_regs = {}
    swdge = {c: [ctx.enter_context(nc.semaphore(f"{c}{u}")) for u in range(2)] for c in ("got", "scat")}

    def hold(eng, *waits):
        values = []
        for i, (_, v) in enumerate(waits):
            if not isinstance(v, int):
                reg = wait_regs.get((eng.engine, i))
                if reg is None:
                    reg = wait_regs[eng.engine, i] = eng.alloc_register(f"wait_value{i}")
                eng.reg_mov(reg, v)
                v = reg
            values.append(v)
        eng.wait_ge(begun, 1)
        for (s, _), v in zip(waits, values):
            eng.wait_ge(s, v)

    @contextmanager
    def stage(counts, dmas=()):
        n = pass_no[0]
        pass_no[0] += 1
        with ExitStack() as s:
            sems = {c: s.enter_context(nc.semaphore(f"{c}_{n}")) for c in counts}
            for c in dmas:
                sems[c] = swdge[c] if c in swdge else [s.enter_context(nc.semaphore(f"{c}{u}_{n}")) for u in range(2)]
            for c in counts:
                nc.gpsimd.sem_inc(sems[c], CREDIT)
            nc.all_engine_barrier()
            with ExitStack() as bufs:
                with nc.Block() as block:
                    yield block, sems, lambda name, shape, dt=f32: bufs.enter_context(
                        nc.sbuf_tensor(f"{name}_{n}", shape, dt)), lambda name, shape=[P, HALF]: bufs.enter_context(
                        nc.psum_tensor(f"{name}_{n}", shape, f32))
            nc.all_engine_barrier()
            for c, own in swdge.items():
                if c in sems:
                    nc.gpsimd.dma_reset(range(own[0].num, own[1].num + 1))
            for c in sems.values():
                for one in (c if isinstance(c, list) else [c]):
                    nc.gpsimd.sem_clear(one)

    def made(t, u, h):
        return 4 * t + 2 * u + h + 1 + CREDIT

    def freed1(t, u, h):
        return 4 * t + 2 * u + h - 1 + CREDIT

    def freed2(t, u, h):
        return 4 * t + 2 * u + h - 3 + CREDIT

    with ctx:
        with ExitStack() as s:
            prep = s.enter_context(nc.semaphore("prep"))
            loaded = s.enter_context(nc.semaphore("loaded"))
            built = s.enter_context(nc.semaphore("built"))
            shaped = s.enter_context(nc.semaphore("shaped"))
            flipped = s.enter_context(nc.semaphore("flipped"))
            kept = s.enter_context(nc.semaphore("kept"))
            padi = s.enter_context(nc.sbuf_tensor("padi", [16, (EP - N_EDGES) // 16], i32))
            sentinel = s.enter_context(nc.sbuf_tensor("sentinel", [1, 2], i32))
            zeros = s.enter_context(nc.sbuf_tensor("zeros", [P, (EP - N_EDGES) * EDGE_DIM // 16], f32))
            ps = s.enter_context(nc.psum_tensor("ps_prep", [P, 2, HALF], f32))
            nw = [0]

            def load(dstap, srcap):
                nc.sync.dma_start(dstap, srcap).then_inc(loaded, 16)
                nw[0] += 1

            with nc.Block() as block:
                @block.vector
                def _(dve):
                    nc.vector.memset(padi[:], PAD_NODE)
                    nc.vector.memset(sentinel[:], -1)
                    for w in (zeros, W1b, W2b, Wm, We, Wu1, Wu2, Wl_raw, Wo_raw, bias, avg, ident):
                        nc.vector.memset(w[:], 0.0)
                    nc.vector.memset(before[:], 1.0).then_inc(prep, 1)
                    dve.wait_ge(prep, 1)
                    nc.vector.memset(bias[:, BEPS:BEPS + 1], EPS)
                    nc.vector.memset(avg[0:D, 0:D], 1.0 / D)
                    nc.vector.memset(avg[D:P, D:P], 1.0 / D).then_inc(prep, 1)
                    dve.wait_ge(shaped, 2)
                    nc.vector.tensor_tensor(center[:], ident[:], avg[:], ALU.subtract).then_inc(built, 1)
                    dve.wait_ge(flipped, 2)
                    nc.vector.tensor_copy(WlT[:], ps[:, 0, 0:P])
                    nc.vector.tensor_copy(WoT[:], ps[:, 1, 0:P]).then_inc(built, 1)

                @block.gpsimd
                def _(pool):
                    pool.wait_ge(prep, 2)
                    nc.gpsimd.affine_select(out=ident[:], in_=ident[:], compare_op=ALU.not_equal, fill=1.0,
                                            base=0, pattern=[[1, P]], channel_multiplier=-1).then_inc(shaped, 1)
                    pool.wait_ge(shaped, 1)
                    nc.gpsimd.affine_select(out=before[:], in_=before[:], compare_op=ALU.is_gt, fill=0.0,
                                            base=0, pattern=[[1, P]], channel_multiplier=-1).then_inc(shaped, 1)

                @block.sync
                def _(sp):
                    sp.wait_ge(prep, 2)
                    for k in range(2):
                        o = k * D
                        load(W1b[o:o + D, o:o + D], W1)
                        load(W2b[o:o + D, o:o + D], W2)
                        load(bias[o:o + D, B1:B1 + 1], b1.rearrange("(d a) -> d a", a=1))
                        load(bias[o:o + D, B2:B2 + 1], b2.rearrange("(d a) -> d a", a=1))
                        load(bias[o:o + D, BO:BO + 1], b_out.rearrange("(d a) -> d a", a=1))
                        r = D - o
                        load(bias[o:o + D, BL:BL + 1], b_lin[r:r + D].rearrange("(d a) -> d a", a=1))
                        load(Wo_raw[0:D, o:o + D], W_out[:, r:r + D])
                        for k2 in range(2):
                            load(Wl_raw[o:o + D, k2 * D:k2 * D + D], W_lin[r:r + D, D - k2 * D:2 * D - k2 * D])
                        for l in range(3):
                            load(Wu1[o:o + D, l, o:o + D], upd_w[l, 0:D, :])
                            load(Wu2[o:o + D, l, o:o + D], upd_w[l, D:2 * D, :])
                            load(bias[o:o + D, BU + l:BU + l + 1], upd_b[l].rearrange("(d a) -> d a", a=1))
                    for l in range(3):
                        load(Wm[:, l, D:P], msg_w[l, 0:2 * D, :])
                        load(We[0:EDGE_DIM, l, D:P], msg_w[l, 2 * D:2 * D + EDGE_DIM, :])
                        load(bias[D:P, BM + l:BM + l + 1], msg_b[l].rearrange("(d a) -> d a", a=1))
                    load(src_pad[0:N_EDGES].rearrange("(a b) -> a b", a=16), src.rearrange("(a b) -> a b", a=16))
                    load(src_pad[N_EDGES:EP].rearrange("(a b) -> a b", a=16), padi[:])
                    load(dst_pad[1:1 + N_EDGES].rearrange("(a b) -> a b", a=16), dst.rearrange("(a b) -> a b", a=16))
                    load(dst_pad[1 + N_EDGES:1 + EP].rearrange("(a b) -> a b", a=16), padi[:])
                    load(dst_pad[0:1].rearrange("(a b) -> a b", a=1), sentinel[:, 0:1])
                    load(dst_pad[EP + 1:EP + 2].rearrange("(a b) -> a b", a=1), sentinel[:, 1:2])
                    load(attr_pad[0:N_EDGES, :].rearrange("(a b) d -> a (b d)", a=16),
                         edge_attr.rearrange("(a b) d -> a (b d)", a=16))
                    load(attr_pad[N_EDGES:EP, :].rearrange("(a b) d -> a (b d)", a=16), zeros[0:16, :])
                    for k in range(2):
                        load(tab[k][EP:EP + P, :], zeros[:, 0:D])
                    sp.wait_ge(loaded, 16 * nw[0])
                    sp.sem_inc(kept, 1)

                @block.tensor
                def _(pe):
                    pe.wait_ge(kept, 1)
                    pe.wait_ge(shaped, 1)
                    nc.tensor.transpose(ps[:, 0, 0:P], Wl_raw[:], ident[:]).then_inc(flipped, 1)
                    nc.tensor.transpose(ps[:, 1, 0:P], Wo_raw[:], ident[:]).then_inc(flipped, 1)
            nc.all_engine_barrier()
            for one in (prep, loaded, built, shaped, flipped, kept):
                nc.gpsimd.sem_clear(one)
            nc.gpsimd.sem_inc(begun, 1)

        def edge_view(v, t, u, n=1):
            r = v.rearrange("(s h p j) -> p s h j", h=2, p=P, j=QJ * n)
            return r[:, bass.DynSlice(2 * t + u, 1), :, :].rearrange("p s h j -> p (s h) j")

        UNR = 4
        with stage(["onehot", "counted", "flipped", "flip_read", "attr_flipped", "attr_read", "chain"],
                   ["idx", "got", "kept", "attr", "attr_kept"]) as (block, S, sbt, pst):
            step = S["chain"]
            nodes = sbt("nodes", [P, 2, NQ], i32)
            lo_i, hi_i = sbt("lo_i", [P, 2, NQ], i32), sbt("hi_i", [P, 2, NQ], i32)
            lo, hi = sbt("lo", [P, 2, NQ]), sbt("hi", [P, 2, NQ])
            ramp_i, ramp = sbt("ramp_i", [P, LO], i32), sbt("ramp", [P, LO], f16)
            oh = sbt("oh", [P, 2, 2, LO + P], f16)
            I = sbt("I", [P, 2, 2, 2 * QJ], i32)
            G = sbt("G", [P, 2, 2 * QJ, P])
            XT = sbt("XT", [P, 2, SUP])
            AT = sbt("AT", [P, 2, 2 * QJ, EDGE_DIM])
            ATT = sbt("ATT", [EDGE_DIM, 2, SUP])
            psX = [pst(f"psX{h}") for h in range(2)]
            psH = [[pst(f"psH{k}{b}") for b in range(2)] for k in range(2)]
            psA = [pst(f"psA{h}", [P, HALF]) for h in range(2)]
            dsts = sbt("dsts", [NS, 3, SUP], i32)
            msk = sbt("msk", [NS, 2, SUP], bf16)
            de = sbt("de", [P, 2, NQ], i32)
            def_ = sbt("def_", [P, 2, NQ])
            cnt = sbt("cnt", [P, 2, LO])
            ones = sbt("ones", [P, LO])
            incl, sq = sbt("incl", [P, LO]), sbt("sq", [P, 3, LO])
            valid, first_e = sbt("valid", [P, LO]), sbt("first_e", [P, LO])
            ntab = sbt("ntab", [P, LO, 8])
            nothing = sbt("nothing", [P, HALF], f16)

            with ExitStack() as s2:
                once = s2.enter_context(nc.semaphore("once"))
                ramp_ok = s2.enter_context(nc.semaphore("ramp_ok"))
                roots = s2.enter_context(nc.semaphore("roots"))
                offset_ok = s2.enter_context(nc.semaphore("offset_ok"))
                masks_ok = s2.enter_context(nc.semaphore("masks_ok"))
                stored = s2.enter_context(nc.semaphore("stored"))
                table_ok = s2.enter_context(nc.semaphore("table_ok"))
                sums_ok = s2.enter_context(nc.semaphore("sums_ok"))
                zeroed = s2.enter_context(nc.semaphore("zeroed"))
                zeros_ok = s2.enter_context(nc.semaphore("zeros_ok"))

                @block.sync
                def _(sp):
                    sp.dma_start(nodes[:, 0, :], src_pad.rearrange("(p q) -> p q", p=P)).then_inc(once, 16)
                    sp.dma_start(nodes[:, 1, :], dst_pad[1:1 + EP].rearrange("(p q) -> p q", p=P)).then_inc(once, 16)
                    for k in range(3):
                        sp.dma_start(dsts[:, k, :], dst_pad[k:k + EP].rearrange("(r c) -> r c", r=NS)).then_inc(once, 16)
                    for k in range(2):
                        sp.dma_start(de[:, k, :].rearrange("p (s j) -> p s j", j=QJ),
                                     dst_pad[k:k + EP].rearrange("(s p j) -> p s j", p=P, j=QJ)).then_inc(once, 16)
                    with sp.Fori(0, NS // 2) as t:
                        for u in range(2):
                            hold(sp, (S["got"][u], t * (16 * 4 * QJ)))
                            sp.dma_start(I[:, u, 0, :].rearrange("p (h j) -> p h j", j=QJ),
                                         edge_view(dst_pad[1:1 + EP], t, u)).then_inc(S["idx"][u], 16)
                            sp.dma_start(I[:, u, 1, :].rearrange("p (h j) -> p h j", j=QJ),
                                         edge_view(src_pad, t, u)).then_inc(S["idx"][u], 16)
                            hold(sp, (S["attr_flipped"], freed2(t, u, 1)))
                            sp.dma_start(AT[:, u].rearrange("p (h j) d -> p h (j d)", h=2),
                                         edge_view(attr_pad.rearrange("e d -> (e d)"), t, u, EDGE_DIM)
                                         ).then_inc(S["attr"][u], 16)
                    sp.wait_ge(masks_ok, 1)
                    sp.dma_start(mask_dram["F"][:, :], msk[:, 0, :]).then_inc(stored, 16)
                    sp.dma_start(mask_dram["R"][:, :], msk[:, 1, :]).then_inc(stored, 16)
                    sp.wait_ge(table_ok, 1)
                    sp.dma_start(node_table.rearrange("(p l) f -> p (l f)", p=P),
                                 ntab[:].rearrange("p l f -> p (l f)")).then_inc(stored, 16)
                    sp.wait_ge(stored, 48)

                @block.gpsimd
                def _(pool):
                    nc.gpsimd.iota(ramp_i[:], pattern=[[1, LO]], base=0, channel_multiplier=0).then_inc(ramp_ok, 1)
                    nc.gpsimd.memset(G[:], 0.0).then_inc(zeroed, 1)
                    pool.wait_ge(zeroed, 1)
                    top = pool.to_reg(N_NODES - 1)
                    with pool.Fori(0, NS // 2) as t:
                        for u in range(2):
                            hold(pool, (S["idx"][u], t * 32 + 32), (S["flipped"], freed2(t, u, 1)))
                            for q in range(2 * QJ):
                                for k in range(2):
                                    nc.gpsimd.indirect_dma_start(
                                        out=G[:, u, q, k * D:k * D + D], out_offset=None, in_=x[:, :],
                                        in_offset=bass.IndirectOffsetOnAxis(ap=I[:, u, k, q:q + 1], axis=0),
                                        bounds_check=top, oob_is_err=False).then_inc(S["got"][u], 16)

                @block.tensor
                def _(pe):
                    pe.wait_ge(zeros_ok, 1)
                    for k in range(2):
                        for b in range(2):
                            nc.tensor.matmul(psH[k][b][:], nothing[:, 0:P], nothing[:],
                                             start=True, stop=True)
                    with pe.Fori(0, NS // 2) as t:
                        for u in range(2):
                            for h in range(2):
                                for i in range(UNR):
                                    n = 8 * t + 4 * u + 2 * h
                                    for k in range(2):
                                        hold(pe, (S["onehot"], (4 * t + 2 * u + h) * (UNR * 2) + (i * 2 + k + 1) + CREDIT))
                                        for b in range(2):
                                            last = nc.tensor.matmul(psH[k][b][:], oh[:, i % 2, k, LO:LO + P],
                                                                    oh[:, i % 2, k, b * HALF:(b + 1) * HALF],
                                                                    start=False, stop=True, skip_group_check=True)
                                        last.then_inc(S["counted"], 1)
                            for h in range(2):
                                hold(pe, (S["got"][u], t * (16 * 4 * QJ) + 16 * 4 * QJ), (S["flip_read"], freed1(t, u, h)))
                                for j in range(QJ):
                                    last = nc.tensor.transpose(psX[h][:].rearrange("f (p j) -> f j p", j=QJ)[:, j, :],
                                                               G[:, u, h * QJ + j, :], ident[:])
                                last.then_inc(S["flipped"], 1)
                                hold(pe, (S["attr"][u], t * 16 + 16), (S["attr_read"], freed1(t, u, h)))
                                for j in range(QJ):
                                    last = nc.tensor.transpose(
                                        psA[h][0:EDGE_DIM, :].rearrange("f (p j) -> f j p", j=QJ)[:, j, :],
                                        AT[:, u, h * QJ + j, :], ident[:])
                                last.then_inc(S["attr_flipped"], 1)
                    pe.wait_ge(sums_ok, 1)
                    pe.wait_ge(S["flip_read"], made(NS // 2 - 1, 1, 1))
                    nc.tensor.matmul(psX[0][:, 0:1], before[:], incl[:, LO - 1:LO], start=True, stop=True).then_inc(offset_ok, 1)

                @block.scalar
                def _(act):
                    with act.Fori(0, NS // 2) as t:
                        for u in range(2):
                            for h in range(2):
                                hold(act, (S["flipped"], made(t, u, h)), (S["kept"][u], t * 16))
                                nc.scalar.copy(XT[:, u, h * HALF:(h + 1) * HALF], psX[h][:]).then_inc(S["flip_read"], 1)
                                hold(act, (S["attr_flipped"], made(t, u, h)), (S["attr_kept"][u], t * 16))
                                nc.scalar.copy(ATT[:, u, h * HALF:(h + 1) * HALF], psA[h][0:EDGE_DIM, :]).then_inc(S["attr_read"], 1)
                            hold(act, (S["flip_read"], made(t, u, 1)), (S["attr_read"], made(t, u, 1)))
                            act.dma_start(st["X0"][bass.DynSlice(2 * t + u, 1), :, :].rearrange("s p e -> p (s e)"),
                                          XT[:, u, :]).then_inc(S["kept"][u], 16)
                            act.dma_start(attrT[bass.DynSlice(2 * t + u, 1), :, :].rearrange("s p e -> p (s e)"),
                                          ATT[:, u, :]).then_inc(S["attr_kept"][u], 16)
                    for u in range(2):
                        act.wait_ge(S["kept"][u], 16 * (NS // 2))
                        act.wait_ge(S["attr_kept"][u], 16 * (NS // 2))
                    act.wait_ge(sums_ok, 1)
                    nc.scalar.activation(sq[:], sq[:], ACT.Sqrt, bias=bias[:, BZ:BZ + 1]).then_inc(roots, 1)

                @block.vector
                def _(dve):
                    c = [CREDIT]

                    def link(ins):
                        c[0] += 1
                        ins.then_inc(step, 1)
                        dve.wait_ge(step, c[0])

                    dve.wait_ge(once, 16 * 7)
                    dve.wait_ge(ramp_ok, 1)
                    nc.vector.memset(nothing[:], 0.0).then_inc(zeros_ok, 1)
                    nc.vector.tensor_copy(ramp[:], ramp_i[:])
                    nc.vector.tensor_scalar(lo_i[:], nodes[:], LO - 1, None, ALU.bitwise_and)
                    link(nc.vector.tensor_scalar(hi_i[:], nodes[:], 10, None, ALU.logical_shift_right))
                    nc.vector.tensor_copy(lo[:], lo_i[:])
                    link(nc.vector.tensor_copy(hi[:], hi_i[:]))
                    nc.vector.tensor_tensor(msk[:, 0, :], dsts[:, 1, :], dsts[:, 0, :], ALU.is_equal)
                    nc.vector.tensor_tensor(msk[:, 1, :], dsts[:, 1, :], dsts[:, 2, :], ALU.is_equal).then_inc(masks_ok, 1)
                    link(nc.vector.tensor_copy(def_[:], de[:]))
                    link(nc.vector.tensor_tensor(def_[:, 0, :], def_[:, 0, :], def_[:, 1, :], ALU.is_equal))
                    link(nc.vector.scalar_tensor_tensor(out=def_[:, 0, :], in0=def_[:, 0, :], scalar=float(2 * N_NODES),
                                                        in1=def_[:, 1, :], op0=ALU.mult, op1=ALU.add))
                    nc.vector.tensor_copy(idx_out[:], def_[:, 0, :])
                    with dve.Fori(0, NS // 2) as t:
                        for g in range(4):
                            for i in range(UNR):
                                for k in range(2):
                                    n = t * (UNR * 8) + (g * UNR + i) * 2 + k
                                    hold(dve, (S["counted"], n + (CREDIT - 3)))
                                    col = t * (4 * UNR) + g * UNR + i
                                    nc.vector.tensor_scalar(oh[:, i % 2, k, 0:LO], ramp[:], lo[:, k, bass.DynSlice(col, 1)],
                                                            None, ALU.is_equal)
                                    nc.vector.tensor_scalar(oh[:, i % 2, k, LO:LO + P], ramp[:, 0:P],
                                                            hi[:, k, bass.DynSlice(col, 1)], None,
                                                            ALU.is_equal).then_inc(S["onehot"], 1)
                    dve.wait_ge(S["counted"], 2 * NQ + CREDIT)
                    nc.vector.memset(ones[:], 1.0)
                    nc.vector.memset(ntab[:], 0.0)
                    for k in range(2):
                        for b in range(2):
                            l = nc.vector.tensor_copy(cnt[:, k, b * HALF:(b + 1) * HALF], psH[k][b][:])
                    link(l)
                    nc.vector.tensor_scalar(sq[:, 0, :], cnt[:, 1, :], 1.0, None, ALU.add)
                    nc.vector.tensor_scalar(sq[:, 1, :], cnt[:, 0, :], 1.0, None, ALU.max)
                    nc.vector.tensor_scalar(sq[:, 2, :], cnt[:, 1, :], 1.0, None, ALU.max)
                    nc.vector.tensor_scalar(valid[:], cnt[:, 1, :], 1.0, None, ALU.min)
                    nc.vector.tensor_tensor_scan(out=incl[:], data0=ones[:], data1=cnt[:, 1, :], initial=0.0,
                                                 op0=ALU.mult, op1=ALU.add).then_inc(sums_ok, 1)
                    dve.wait_ge(offset_ok, 1)
                    dve.wait_ge(roots, 1)
                    link(nc.vector.tensor_scalar(incl[:], incl[:], psX[0][:, 0:1], None, ALU.add))
                    for k in range(3):
                        nc.vector.reciprocal(ntab[:, :, k], sq[:, k, :])
                    link(nc.vector.tensor_tensor(first_e[:], incl[:], cnt[:, 1, :], ALU.subtract))
                    link(nc.vector.tensor_tensor(incl[:], incl[:], valid[:], ALU.mult))
                    link(nc.vector.scalar_tensor_tensor(out=first_e[:], in0=first_e[:], scalar=1.0, in1=valid[:],
                                                        op0=ALU.add, op1=ALU.mult))
                    nc.vector.tensor_scalar(ntab[:, :, 3], incl[:], -1.0, None, ALU.add)
                    nc.vector.tensor_scalar(ntab[:, :, 4], first_e[:], -1.0, None, ALU.add).then_inc(table_ok, 1)

        for one in (once, ramp_ok, roots, offset_ok, masks_ok, stored, table_ok, sums_ok, zeroed, zeros_ok):
            nc.gpsimd.sem_clear(one)

        CH = SUP
        n_full = N_NODES // CH
        rest = (N_NODES - n_full * CH) // 2
        REST_P = 112
        assert n_full % 2 == 1 and rest == REST_P * 3
        LNS = ["sq", "var", "sd", "rs", "ln"]
        dense_ops = (["xin", "x0", "m1", "h1", "m2", "h2", "y1"] + ["ce1", "sq1", "va1", "sd1", "rs1", "x1"]
                     + ["ce2", "sq2", "va2", "sd2", "rs2", "x2"] + ["ma", "ha", "mb", "hb", "mc", "hc", "y3"]
                     + ["ce3", "sq3", "va3", "sd3", "rs3", "x3"] + ["y4", "ce4", "sq4", "va4", "sd4", "rs4", "x4"]
                     + ["back", "read"])
        with stage(dense_ops + ["copied"], ["nidx", "got", "nx", "nkept"]) as (block, S, sbt, pst):
            RES = sbt("RES", [P, 2, 8, NQ])
            T = sbt("T", [P, 2, 2, 2 * QJ, 8])
            I = sbt("I", [P, 2, 2, 2 * QJ], i32)
            X = sbt("X", [P, 2, 2, QJ, 2, D])
            Xt, H, Hb, Y, SQ, SD = (sbt(n, [P, 2, HALF]) for n in ("Xt", "H", "Hb", "Y", "SQ", "SD"))
            Xo = sbt("Xo", [P, 2, 2, QJ, 2, D])
            miss = sbt("miss", [P, NQ])
            zr_i, zr = sbt("zr_i", [P, 1], i32), sbt("zr", [P, 1])
            psT, psM, psV, psB = ([pst(f"{n}{h}") for h in range(2)] for n in ("psT", "psM", "psV", "psB"))
            with ExitStack() as s2:
                ramped = s2.enter_context(nc.semaphore("ramped"))
                fin = s2.enter_context(nc.semaphore("fin"))
                rows_ok = s2.enter_context(nc.semaphore("rows_ok"))
                rows_kept = s2.enter_context(nc.semaphore("rows_kept"))

                @block.gpsimd
                def _(pool):
                    nc.gpsimd.iota(zr_i[:], pattern=[[0, 1]], base=EP + 1, channel_multiplier=1).then_inc(ramped, 1)
                    with pool.Fori(0, NS // 2) as t:
                        for u in range(2):
                            hold(pool, (S["nidx"][u], t * 32 + 32), (S["copied"], 2 * t + u - 1 + CREDIT))
                            for q in range(2 * QJ):
                                for k in range(2):
                                    nc.gpsimd.indirect_dma_start(
                                        out=T[:, u, k, q, :], out_offset=None, in_=node_table[:, :],
                                        in_offset=bass.IndirectOffsetOnAxis(ap=I[:, u, k, q:q + 1], axis=0),
                                    ).then_inc(S["got"][u], 16)

                def step_sizes(full, h):
                    return (P, QJ, HALF) if full or h == 0 else (REST_P, 3, rest)

                def node_rows(v, tt, u, h, a):
                    return v[bass.DynSlice((2 * tt + u) * 2 * CH + h * CH + a * HALF, HALF), :].rearrange(
                        "(p j) d -> p j d", j=QJ)

                def last_rows(v, h, a):
                    pp, jj, ww = step_sizes(False, h)
                    at = (n_full - 1 + h) * CH + a * ww
                    return v[at:at + ww, :].rearrange("(p j) d -> p j d", j=jj)

                TT = (n_full - 1) // 4
                assert 4 * TT == n_full - 1

                @block.sync
                def _(sp):
                    def node_load(t, u):
                        hold(sp, (S["xin"], freed2(t, u, 1)))
                        for h in range(2):
                            for a in range(2):
                                sp.dma_start(X[:, u, h, :, a, :], node_rows(x, t, u, h, a)).then_inc(S["nx"][u], 16)

                    def idx_load(t, u):
                        hold(sp, (S["got"][u], t * (16 * 4 * QJ)))
                        sp.dma_start(I[:, u, 0, :].rearrange("p (h j) -> p h j", j=QJ),
                                     edge_view(dst_pad[1:1 + EP], t, u)).then_inc(S["nidx"][u], 16)
                        sp.dma_start(I[:, u, 1, :].rearrange("p (h j) -> p h j", j=QJ),
                                     edge_view(src_pad, t, u)).then_inc(S["nidx"][u], 16)

                    with sp.Fori(0, TT) as t:
                        for u in range(2):
                            idx_load(t, u)
                            node_load(t, u)
                    with sp.Fori(TT, NS // 2) as t:
                        for u in range(2):
                            idx_load(t, u)
                    sp.wait_ge(S["xin"], freed2(TT, 0, 1))
                    for h in range(2):
                        pp, jj, ww = step_sizes(False, h)
                        for a in range(2):
                            sp.dma_start(X[0:pp, 0, h, 0:jj, a, :], last_rows(x, h, a)).then_inc(S["nx"][0], 16)
                    sp.wait_ge(rows_ok, 1)
                    for name, k, f in (("dis_d", 0, 0), ("dis_s", 1, 0), ("nsrc_s", 1, 1), ("ndst_d", 0, 2), ("ndst_s", 1, 2)):
                        sp.dma_start(rows[name].rearrange("s (h p j) -> p (s h) j", h=2, j=QJ),
                                     RES[:, k, f, :].rearrange("p (s j) -> p s j", j=QJ)).then_inc(rows_kept, 16)
                    sp.wait_ge(rows_kept, 16 * 5)

                def dense_pe(pe, t, u, full=True):
                    cols = [step_sizes(full, h) for h in range(2)]

                    def mm(name, ps, w, rhs, need, more=()):
                        for h in range(2):
                            W = cols[h][2]
                            hold(pe, (S[need], made(t, u, h)), *[(S[m], freed1(t, u, h)) for m in more])
                            nc.tensor.matmul(ps[h][:, 0:W], w, rhs[:, h, 0:W], start=True, stop=True).then_inc(S[name], 1)

                    for h in range(2):
                        pp, jj, W = cols[h]
                        n_x = 64 * t + 64
                        hold(pe, (S["nx"][u], n_x), (S["x0"], freed1(t, u, h)))
                        for j in range(jj):
                            last = nc.tensor.transpose(psT[h][:, 0:W].rearrange("f (p j) -> f j p", j=jj)[:, j, :],
                                                       X[0:pp, u, h, j, :, :].rearrange("p a d -> p (a d)"), ident[0:pp, 0:pp])
                        last.then_inc(S["xin"], 1)
                    mm("m1", psM, W1b[:], Xt, "x0", ("x4",))
                    mm("m2", psM, W2b[:], H, "h1")
                    for i, y in (("1", "y1"), ("2", "x1")):
                        mm("ce" + i, psM, center[:], Y, y)
                        mm("va" + i, psV, avg[:], SQ, "sq" + i)
                    for l, (a, h_in, bin_) in enumerate((("ma", "x2", Y), ("mb", "ha", H), ("mc", "hb", Hb))):
                        mm(a, psM, Wu1[:, l, :], bin_, h_in)
                    for i, y in (("3", "y3"), ("4", "y4")):
                        mm("ce" + i, psM, center[:], Y, y)
                        mm("va" + i, psV, avg[:], SQ, "sq" + i)
                    for h in range(2):
                        pp, jj, W = cols[h]
                        hold(pe, (S["x4"], made(t, u, h)), (S["read"], freed1(t, u, h)))
                        for j in range(jj):
                            last = nc.tensor.transpose(psB[h][0:pp, j * P:(j + 1) * P],
                                                       H[:, h, 0:W].rearrange("f (p j) -> f j p", j=jj)[:, j, :], ident[:])
                        last.then_inc(S["back"], 1)

                @block.tensor
                def _(pe):
                    with pe.Fori(0, TT) as t:
                        for u in range(2):
                            dense_pe(pe, t, u)
                    dense_pe(pe, TT, 0, False)

                def dense_act(act, t, u, full=True):
                    cols = [step_sizes(full, h) for h in range(2)]

                    def ac(name, o, i, func, need, b=None, free=(), scale=1.0):
                        for h in range(2):
                            W = cols[h][2]
                            hold(act, (S[need], made(t, u, h)), *[(S[f], freed1(t, u, h)) for f in free])
                            if func is None:
                                ins = nc.scalar.copy(o[:, h, 0:W], i[h][:, 0:W])
                            else:
                                ins = nc.scalar.activation(o[:, h, 0:W], i[h][:, 0:W], func,
                                                           bias=bias[:, b:b + 1], scale=scale)
                            ins.then_inc(S[name], 1)

                    def ln(i):
                        ac("sq" + i, SQ, psM, ACT.Square, "ce" + i, BZ)
                        ac("sd" + i, SD, psV, ACT.Sqrt, "va" + i, BEPS)

                    ac("x0", Xt, psT, None, "xin", free=("y1",))
                    ac("h1", H, psM, ACT.Relu, "m1", B1, free=("back",))
                    ac("h2", Hb, psM, ACT.Relu, "m2", B2)
                    ln("1")
                    ln("2")
                    ac("ha", H, psM, ACT.Relu, "ma", BU)
                    ac("hb", Hb, psM, ACT.Relu, "mb", BU + 1)
                    ac("hc", H, psM, ACT.Relu, "mc", BU + 2)
                    ln("3")
                    ln("4")
                    for h in range(2):
                        pp, jj, W = cols[h]
                        kept = t * 64
                        hold(act, (S["back"], made(t, u, h)), (S["nkept"][u], kept))
                        nc.scalar.copy(Xo[0:pp, u, h, 0:jj].rearrange("p j a d -> p (j a d)"),
                                       psB[h][0:pp, 0:jj * P]).then_inc(S["read"], 1)
                    hold(act, (S["read"], made(t, u, 1)))
                    if full:
                        for h in range(2):
                            for a in range(2):
                                act.dma_start(node_rows(out, t, u, h, a), Xo[:, u, h, :, a, :]).then_inc(S["nkept"][u], 16)
                    else:
                        for h in range(2):
                            pp, jj, ww = cols[h]
                            for a in range(2):
                                act.dma_start(last_rows(out, h, a), Xo[0:pp, 0, h, 0:jj, a, :]).then_inc(S["nkept"][0], 16)

                @block.scalar
                def _(act):
                    with act.Fori(0, TT) as t:
                        for u in range(2):
                            dense_act(act, t, u)
                    dense_act(act, TT, 0, False)
                    act.wait_ge(S["nkept"][0], 64 * TT + 64)
                    act.wait_ge(S["nkept"][1], 64 * TT)

                def keep_scalars(dve, t, u):
                    hold(dve, (S["got"][u], t * (16 * 4 * QJ) + 16 * 4 * QJ))
                    for k in range(2):
                        last = nc.vector.tensor_copy(
                            RES[:, k, :, bass.DynSlice((2 * t + u) * 2 * QJ, 2 * QJ)],
                            T[:, u, k].rearrange("p q f -> p f q"))
                    last.then_inc(S["copied"], 1)

                def dense_dve(dve, t, u, full=True):
                    cols = [step_sizes(full, h)[2] for h in range(2)]

                    def ve(name, fn, *needs):
                        for h in range(2):
                            hold(dve, *[(S[n], made(t, u, h)) for n in needs])
                            fn(h, cols[h]).then_inc(S[name], 1)

                    def stt(o, a, sc, b, op0=ALU.mult, op1=ALU.add):
                        return lambda h, W: nc.vector.scalar_tensor_tensor(
                            out=o[:, h, 0:W], in0=a[:, h, 0:W], scalar=sc, in1=b[:, h, 0:W], op0=op0, op1=op1)

                    def ln(i, o):
                        ve("rs" + i, lambda h, W: nc.vector.reciprocal(SD[:, h, 0:W], SD[:, h, 0:W]), "sd" + i)
                        ve({"1": "x1", "2": "x2", "3": "x3", "4": "x4"}[i],
                           lambda h, W: nc.vector.tensor_tensor(o[:, h, 0:W], psM[h][:, 0:W], SD[:, h, 0:W], ALU.mult),
                           "rs" + i)

                    ve("y1", stt(Y, Xt, 2.0, Hb), "h2", "x0")
                    for h in range(2):
                        hold(dve, (S["sd1"], made(t, u, h)))
                        nc.vector.reciprocal(SD[:, h, 0:cols[h]], SD[:, h, 0:cols[h]]).then_inc(S["rs1"], 1)
                    ve("x1", lambda h, W: nc.vector.scalar_tensor_tensor(
                        out=Y[:, h, 0:W], in0=psM[h][:, 0:W], scalar=1.0 + ALPHA, in1=SD[:, h, 0:W],
                        op0=ALU.mult, op1=ALU.mult), "rs1")
                    ln("2", Y)
                    ve("y3", stt(Y, Y, 1.0, H), "hc", "x2")
                    ln("3", Y)
                    ve("y4", lambda h, W: nc.vector.tensor_scalar(Y[:, h, 0:W], Y[:, h, 0:W], bias[:, BO:BO + 1],
                                                                  None, ALU.add), "x3")
                    ln("4", H)

                @block.vector
                def _(dve):
                    dve.wait_ge(ramped, 1)
                    nc.vector.tensor_copy(zr[:], zr_i[:])
                    with dve.Fori(0, TT) as t:
                        for u in range(2):
                            keep_scalars(dve, t, u)
                            dense_dve(dve, t, u)
                    with dve.Fori(TT, NS // 2) as t:
                        for u in range(2):
                            keep_scalars(dve, t, u)
                    dense_dve(dve, TT, 0, False)
                    dve.wait_ge(S["copied"], NS + CREDIT)
                    n = 0
                    for f, o in ((3, idx_src_gl), (4, idx_src_gf)):
                        nc.vector.tensor_scalar(miss[:], RES[:, 1, f, :], 0.0, zr[:, 0:1], ALU.is_lt, ALU.mult).then_inc(fin, 1)
                        n += 1
                        dve.wait_ge(fin, n)
                        nc.vector.tensor_tensor(o[:], RES[:, 1, f, :], miss[:], ALU.add).then_inc(fin, 1)
                        n += 1
                        dve.wait_ge(fin, n)
                    nc.vector.scalar_tensor_tensor(out=a_src[:], in0=RES[:, 1, 1, :], scalar=1.0 - ALPHA,
                                                   in1=RES[:, 1, 2, :], op0=ALU.mult, op1=ALU.mult).then_inc(rows_ok, 1)

        for one in (ramped, fin, rows_ok, rows_kept):
            nc.gpsimd.sem_clear(one)

        def order(direction, t, u):
            return 2 * t + u if direction == "F" else (NS - 1 - u) - 2 * t

        def halves(direction):
            return (0, 1) if direction == "F" else (1, 0)

        def sup(v, n):
            return v[bass.DynSlice(n, 1), :, :].rearrange("s p e -> p (s e)")

        def spread(v, n, parts):
            return v[bass.DynSlice(n, 1), :].to_broadcast([parts, SUP])

        def tab_rows(v, n):
            return v[0:EP, :].rearrange("(s h p j) d -> p s h (j d)", h=2, p=P, j=QJ)[:, bass.DynSlice(n, 1), :, :] \
                .rearrange("p s h e -> p (s h) e")

        def appnp_pass(B_res, t_in, t_out, keepT=None):
            with stage(["scaled", "added", "flipped", "scanned", "back", "read"],
                       ["idx", "got", "mask", "kept", "keptT"]) as (block, S, sbt, pst):
                I = sbt("I", [P, 2, 2 * QJ], i32)
                G = sbt("G", [P, 2, 2 * QJ, D])
                M = sbt("M", [P, 2 * QJ, D])
                K = sbt("K", [D, 2, SUP], bf16)
                ST = sbt("ST", [D, 2, SUP])
                SR = sbt("SR", [P, 2, 2 * QJ, D])
                psT = [pst(f"psT{h}") for h in range(2)]
                psB = [pst(f"psB{h}") for h in range(2)]
                tin, tout = tab[t_in], tab[t_out]

                @block.sync
                def _(sp):
                    with sp.Fori(0, NS // 2) as t:
                        for u in range(2):
                            hold(sp, (S["got"][u], t * (32 * QJ)))
                            sp.dma_start(I[:, u, :], idx_src_gl[:, bass.DynSlice((2 * t + u) * 2 * QJ, 2 * QJ)]
                                         ).then_inc(S["idx"][u], 16)
                            hold(sp, (S["scanned"], freed2(t, u, 1)))
                            sp.dma_start(K[:, u, :], spread(mask_dram["F"], 2 * t + u, D)).then_inc(S["mask"][u], 16)

                @block.gpsimd
                def _(pool):
                    with pool.Fori(0, NS // 2) as t:
                        for u in range(2):
                            hold(pool, (S["idx"][u], t * 16 + 16), (S["scaled"], freed2(t, u, 1)))
                            for q in range(2 * QJ):
                                nc.gpsimd.indirect_dma_start(
                                    out=G[:, u, q, :], out_offset=None, in_=tin[:, :],
                                    in_offset=bass.IndirectOffsetOnAxis(ap=I[:, u, q:q + 1], axis=0),
                                ).then_inc(S["got"][u], 16)

                @block.vector
                def _(dve):
                    nc.vector.memset(ST[:, 1, SUP - 1:SUP], 0.0)
                    with dve.Fori(0, NS // 2) as t:
                        for u in range(2):
                            q0 = (2 * t + u) * 2 * QJ
                            for h in range(2):
                                q = slice(h * QJ, (h + 1) * QJ)
                                hold(dve, (S["got"][u], t * (32 * QJ) + 32 * QJ), (S["flipped"], freed1(t, u, h)))
                                nc.vector.tensor_tensor(
                                    M[:, q, :], G[:, u, q, :],
                                    a_src[:, bass.DynSlice(q0 + h * QJ, QJ)].unsqueeze(2).to_broadcast([P, QJ, D]),
                                    ALU.mult).then_inc(S["scaled"], 1)
                            for h in range(2):
                                q = slice(h * QJ, (h + 1) * QJ)
                                hold(dve, (S["scaled"], made(t, u, h)))
                                nc.vector.tensor_tensor(M[:, q, :], M[:, q, :], B_res[:, bass.DynSlice(q0 + h * QJ, QJ), :],
                                                        ALU.add).then_inc(S["added"], 1)
                            for h in range(2):
                                before_ = ST[:, u, HALF - 1:HALF] if h else ST[:, 1 - u, SUP - 1:SUP]
                                hold(dve, (S["mask"][u], t * 16 + 16), (S["flipped"], made(t, u, h)),
                                     (S["scanned"], made(t, u, h) - 1), (S["back"], freed2(t, u, h)),
                                     *([(S["keptT"][u], t * 16)] if keepT is not None else []))
                                nc.vector.tensor_tensor_scan(
                                    out=ST[:, u, h * HALF:(h + 1) * HALF], data0=K[:, u, h * HALF:(h + 1) * HALF],
                                    data1=psT[h][0:D, :], initial=before_, op0=ALU.mult, op1=ALU.add
                                ).then_inc(S["scanned"], 1)

                @block.tensor
                def _(pe):
                    with pe.Fori(0, NS // 2) as t:
                        for u in range(2):
                            for h in range(2):
                                hold(pe, (S["added"], made(t, u, h)), (S["scanned"], freed1(t, u, h)))
                                for j in range(QJ):
                                    last = nc.tensor.transpose(psT[h][0:D, :].rearrange("f (p j) -> f j p", j=QJ)[:, j, :],
                                                               M[:, h * QJ + j, :], ident[:])
                                last.then_inc(S["flipped"], 1)
                            for h in range(2):
                                hold(pe, (S["scanned"], made(t, u, h)), (S["read"], freed1(t, u, h)))
                                for j in range(QJ):
                                    last = nc.tensor.transpose(
                                        psB[h][:, j * D:(j + 1) * D],
                                        ST[:, u, h * HALF:(h + 1) * HALF].rearrange("f (p j) -> f j p", j=QJ)[:, j, :],
                                        ident[0:D, 0:D])
                                last.then_inc(S["back"], 1)

                @block.scalar
                def _(act):
                    with act.Fori(0, NS // 2) as t:
                        for u in range(2):
                            for h in range(2):
                                hold(act, (S["back"], made(t, u, h)), (S["kept"][u], t * 16))
                                nc.scalar.copy(SR[:, u, h * QJ:(h + 1) * QJ, :],
                                               psB[h][:, 0:QJ * D].rearrange("p (j d) -> p j d", d=D)).then_inc(S["read"], 1)
                            hold(act, (S["read"], made(t, u, 1)))
                            act.dma_start(tab_rows(tout, 2 * t + u),
                                          SR[:, u].rearrange("p (h j) d -> p h (j d)", h=2)).then_inc(S["kept"][u], 16)
                            if keepT is not None:
                                act.dma_start(sup(keepT, 2 * t + u), ST[:, u, :]).then_inc(S["keptT"][u], 16)
                    for u in range(2):
                        act.wait_ge(S["kept"][u], 16 * (NS // 2))
                        if keepT is not None:
                            act.wait_ge(S["keptT"][u], 16 * (NS // 2))

        def node_pass(kind, direction, tab_in=None, tab_out=None, tot_in=None, tot_out=None,
                      x_in=None, x_out=None, skip=None, layer=0, B_res=None):
            gather = tab_in is not None
            norm = kind in ("gcn2", "appnp_end", "attend", "finish")
            message = kind in ("appnp_end", "update")
            attention = kind in ("attend", "finish")
            scaled = kind in ("first", "gcn1", "gcn2", "appnp_end")
            idx_all = idx_src_gl if direction == "R" else idx_src_gf
            hs = halves(direction)
            z = hs[1]
            wide = slice(0, P) if attention else slice(D, P)
            low = slice(0, P) if kind == "finish" else slice(0, D)
            counts = ["carry_ok", "scanned"]
            counts += ["at_zero"] if message else []
            counts += ["flipped", "agg_s"] if gather else []
            counts += ["masked", "agg_d"] if kind != "first" else []
            counts += {"first": ["v"],
                       "gcn1": ["u1", "u", "mm", "relu", "v"],
                       "gcn2": ["u1", "u", "mm", "relu", "y", "msg", "b_flip", "b_read"],
                       "appnp_end": ["u1", "y", "msg_mm", "msg"],
                       "update": ["mm", "x", "msg_mm", "msg"],
                       "attend": ["mm", "relu", "y", "msg_mm", "msg"],
                       "finish": ["msg_mm", "msg", "diff", "ex", "wx", "summed", "rden", "nf", "mm", "y", "scattering"],
                       }[kind]
            counts += ["cent", "sq", "var", "sd", "rs", "x"] if norm else []
            counts += ["back", "read"] if kind != "attend" else []
            dmas = ["mask", "state"]
            dmas += ["idx", "got"] if gather else []
            dmas += ["tot"] if kind != "first" else []
            dmas += ["row"] if scaled else []
            dmas += ["nsrc"] if kind == "gcn2" else []
            dmas += ["skipped"] if skip else []
            dmas += ["attr"] if message else []
            dmas += ["xkept"] if x_out else []
            dmas += ["kept"] if tab_out is not None else []
            dmas += ["scat"] if kind == "finish" else []
            dmas += ["totkept"] if tot_out is not None else []
            dmas += ["oidx"] if kind == "finish" else []
            with stage(counts, dmas) as (block, S, sbt, pst):
                two = lambda n, dt=f32: sbt(n, [P, 2, SUP], dt)
                one = lambda n: sbt(n, [P, 2, HALF])
                K = two("K", bf16)
                X, XO, ST = two("X"), two("XO"), two("ST")
                if kind != "first":
                    TOT, MS, AG = two("TOT"), one("MS"), one("AG")
                if gather:
                    I = sbt("I", [P, 2, 2 * QJ], i32)
                    G = sbt("G", [P, 2, 2 * QJ, P])
                if skip:
                    XS = two("XS")
                if scaled:
                    R = two("R")
                if kind == "gcn2":
                    NSR = TOT
                if message:
                    AT = two("AT")
                if kind == "finish":
                    NUM, WX = two("NUM"), one("WX")
                    IO = sbt("IO", [P, 2, 2 * QJ], i32)
                H, Y, SQ, SD = (one(n) for n in ("H", "Y", "SQ", "SD"))
                MG = MS if kind == "gcn2" else one("MG")
                SR = sbt("SR", [P, 2, 2 * QJ, D])
                psT, psM, psV, psB = ([pst(f"{n}{h}") for h in range(2)] for n in ("psT", "psM", "psV", "psB"))
                cols = lambda h: slice(h * HALF, (h + 1) * HALF)
                end = HALF - 1 if direction == "F" else 0

                def md(t, u, h):
                    return made(t, u, hs.index(h))

                def f1(t, u, h):
                    return freed1(t, u, hs.index(h))

                def f2(t, u, h):
                    return freed2(t, u, hs.index(h))

                def along(ap):
                    return ap if direction == "F" else ap[:, ::-1]

                x_used = {"first": "v", "gcn1": "u1", "gcn2": "u1", "appnp_end": "y", "update": "mm",
                          "attend": "mm", "finish": "y"}[kind]
                ag_used = {"gcn1": "u1", "gcn2": "u1", "appnp_end": "u1", "update": "mm", "attend": "mm",
                           "finish": "diff", "first": None}[kind]

                @block.sync
                def _(sp):
                    if message:
                        sp.wait_ge(S["at_zero"], 1 + CREDIT)
                    with sp.Fori(0, NS // 2) as t:
                        for u in range(2):
                            n = order(direction, t, u)
                            if gather:
                                hold(sp, (S["got"][u], t * (32 * QJ)))
                                sp.dma_start(I[:, u, :], idx_all[:, bass.DynSlice(n * (2 * QJ), 2 * QJ)]
                                             ).then_inc(S["idx"][u], 16)
                            hold(sp, (S["summed" if kind == "finish" else "scanned"], f2(t, u, z)))
                            sp.dma_start(K[:, u, :], spread(mask_dram[direction], n, P)).then_inc(S["mask"][u], 16)
                            if kind != "first":
                                hold(sp, (S["masked"], f2(t, u, z)))
                                sp.dma_start(TOT[low, u, :], sup(maxT if kind == "finish" else totT[tot_in], n)
                                             ).then_inc(S["tot"][u], 16)
                            hold(sp, (S[x_used], f2(t, u, z)))
                            sp.dma_start(X[:, u, :], sup(st[x_in], n)).then_inc(S["state"][u], 16)
                            if skip:
                                hold(sp, (S["y"], f2(t, u, z)))
                                sp.dma_start(XS[:, u, :], sup(st[skip], n)).then_inc(S["skipped"][u], 16)
                            if scaled:
                                r = "ndst" if kind == "appnp_end" else "dis"
                                used = {"first": "v", "gcn1": "v", "gcn2": "u", "appnp_end": "u1"}[kind]
                                hold(sp, (S[used], f2(t, u, z)))
                                sp.dma_start(R[0:D, u, :], spread(rows[r + "_d"], n, D)).then_inc(S["row"][u], 16)
                                sp.dma_start(R[D:P, u, :], spread(rows[r + "_s"], n, D)).then_inc(S["row"][u], 16)
                            if kind == "gcn2":
                                hold(sp, (S["msg"], f2(t, u, z)))
                                sp.dma_start(NSR[D:P, u, :], spread(rows["nsrc_s"], n, D)).then_inc(S["nsrc"][u], 16)
                            if message:
                                hold(sp, (S["msg_mm"], f2(t, u, z)))
                                sp.dma_start(AT[0:EDGE_DIM, u, :], sup(attrT, n)).then_inc(S["attr"][u], 16)
                            if kind == "finish":
                                hold(sp, (S["scat"][u], t * (32 * QJ)))
                                sp.dma_start(IO[:, u, :], idx_out[:, bass.DynSlice(n * (2 * QJ), 2 * QJ)]
                                             ).then_inc(S["oidx"][u], 16)

                @block.gpsimd
                def _(pool):
                    if message:
                        nc.gpsimd.memset(AT[:], 0.0).then_inc(S["at_zero"], 1)
                    if gather:
                        nc.gpsimd.memset(G[:], 0.0).then_inc(S["flipped"], 1)
                        pool.wait_ge(S["flipped"], 1 + CREDIT)
                        with pool.Fori(0, NS // 2) as t:
                            for u in range(2):
                                hold(pool, (S["idx"][u], t * 16 + 16), (S["flipped"], freed2(t, u, 1) + 1))
                                for q in range(2 * QJ):
                                    nc.gpsimd.indirect_dma_start(
                                        out=G[:, u, q, D:P], out_offset=None, in_=tab[tab_in][:, :],
                                        in_offset=bass.IndirectOffsetOnAxis(ap=I[:, u, q:q + 1], axis=0),
                                    ).then_inc(S["got"][u], 16)
                    if kind == "finish":
                        top = pool.to_reg(N_NODES - 1)
                        with pool.Fori(0, NS // 2) as t:
                            for u in range(2):
                                hold(pool, (S["read"], made(t, u, 1)), (S["oidx"][u], t * 16 + 16))
                                for q in range(2 * QJ):
                                    nc.gpsimd.indirect_dma_start(
                                        out=out[:, :], out_offset=bass.IndirectOffsetOnAxis(ap=IO[:, u, q:q + 1], axis=0),
                                        in_=SR[:, u, q, :], in_offset=None,
                                        bounds_check=top, oob_is_err=False).then_inc(S["scat"][u], 16)
                        for u in range(2):
                            pool.wait_ge(S["scat"][u], 32 * QJ * (NS // 2))

                @block.tensor
                def _(pe):
                    with pe.Fori(0, NS // 2) as t:
                        for u in range(2):
                            def mm(name, ps, terms, needs, frees=(), landed=()):
                                for h in hs:
                                    hold(pe, *[(S[a], md(t, u, h)) for a in needs], *[(S[a], f1(t, u, h)) for a in frees],
                                         *[(S[a][u], t * 16 + 16) for a in landed])
                                    for i, (w, r) in enumerate(terms):
                                        last = nc.tensor.matmul(ps[h][:], w, r(h), start=(i == 0), stop=(i == len(terms) - 1))
                                    last.then_inc(S[name], 1)

                            half = lambda tile: lambda h: tile[:, h, :]
                            slot = lambda tile: lambda h: tile[:, u, cols(h)]
                            if gather:
                                tail = {"gcn2": "b_read", "gcn1": "agg_s"}.get(kind, "msg")
                                for h in hs:
                                    hold(pe, (S["got"][u], t * (32 * QJ) + 32 * QJ), (S[tail], f1(t, u, h)))
                                    for j in range(QJ):
                                        last = nc.tensor.transpose(psT[h][:].rearrange("f (p j) -> f j p", j=QJ)[:, j, :],
                                                                   G[:, u, h * QJ + j, :], ident[:])
                                    last.then_inc(S["flipped"], 1)
                            if kind == "gcn1":
                                mm("mm", psM, [(W1b[:], half(Y))], ["u"], ["relu"])
                            if kind == "gcn2":
                                mm("mm", psM, [(W2b[:], half(Y))], ["u"], ["x"])
                            if kind in ("update", "attend"):
                                mm("mm", psM, [(Wu1[:, layer, :], slot(X)), (Wu2[:, layer, :], half(AG))],
                                   ["agg_d", "agg_s"], ["x"], ["state"])
                            if kind == "finish":
                                mm("msg_mm", psT, [(WlT[:], slot(X))], [], ["msg"], ["state"])
                                mm("mm", psM, [(WoT[:], half(H))], ["nf"], ["x"])
                            if norm:
                                mm("cent", psM, [(center[:], half(Y))], ["y"], ["x"])
                                mm("var", psV, [(avg[:], half(SQ))], ["sq"], ["sd"])
                            if kind == "gcn2":
                                for h in hs:
                                    hold(pe, (S["msg"], md(t, u, h)))
                                    for j in range(QJ):
                                        last = nc.tensor.transpose(
                                            psT[h][:, j * D:(j + 1) * D],
                                            MG[D:P, h, :].rearrange("f (p j) -> f j p", j=QJ)[:, j, :], ident[D:P, D:P])
                                    last.then_inc(S["b_flip"], 1)
                            if message:
                                nxt = 0 if kind == "appnp_end" else layer + 1
                                mm("msg_mm", psT, [(Wm[:, nxt, :], slot(XO)), (We[:, nxt, :], slot(AT))], ["x"], [], ["attr"])
                            if kind == "attend":
                                mm("msg_mm", psT, [(WlT[:], slot(XO))], ["x"])
                            if kind != "attend":
                                part, what = ((slice(0, D), "x") if kind == "finish" else (slice(D, P), "scanned"))
                                tile = XO if kind == "finish" else ST
                                for h in hs:
                                    hold(pe, (S[what], md(t, u, h)), (S["read"], f1(t, u, h)))
                                    for j in range(QJ):
                                        last = nc.tensor.transpose(
                                            psB[h][:, j * D:(j + 1) * D],
                                            tile[part, u, cols(h)].rearrange("f (p j) -> f j p", j=QJ)[:, j, :],
                                            ident[part, part])
                                    last.then_inc(S["back"], 1)

                @block.scalar
                def _(act):
                    with act.Fori(0, NS // 2) as t:
                        for u in range(2):
                            n = order(direction, t, u)

                            def ac(name, o, i, func, b, needs, frees=(), extra=()):
                                for h in hs:
                                    hold(act, *[(S[a], md(t, u, h)) for a in needs], *[(S[a], f1(t, u, h)) for a in frees], *extra)
                                    nc.scalar.activation(o(h), i(h), func, bias=bias[:, b:b + 1]).then_inc(S[name], 1)

                            half = lambda tile: lambda h: tile[:, h, :]
                            slot = lambda tile: lambda h: tile[:, u, cols(h)]
                            bank = lambda ps: lambda h: ps[h][:]
                            if gather:
                                for h in hs:
                                    hold(act, (S["flipped"], md(t, u, h) + 1), (S[ag_used], f1(t, u, h)))
                                    nc.scalar.copy(AG[D:P, h, :], psT[h][D:P, :]).then_inc(S["agg_s"], 1)
                            if kind in ("gcn1", "gcn2"):
                                b = B1 if kind == "gcn1" else B2
                                ac("relu", half(H), bank(psM), ACT.Relu, b, ["mm"], ["v" if kind == "gcn1" else "y"])
                            if kind == "update":
                                ac("x", slot(XO), bank(psM), ACT.Relu, BU + layer, ["mm"], [],
                                   [(S["xkept"][u], t * 16), (S["msg_mm"], freed2(t, u, 1))])
                            if kind == "attend":
                                ac("relu", half(H), bank(psM), ACT.Relu, BU + layer, ["mm"], ["y"])
                            if kind == "finish":
                                ac("msg", half(MG), bank(psT), ACT.Relu, BL, ["msg_mm"], ["diff"])
                                ac("ex", half(H), half(Y), ACT.Exp, BZ, ["diff"], ["mm"])
                            if norm:
                                ac("sq", half(SQ), bank(psM), ACT.Square, BZ, ["cent"], ["var"])
                                ac("sd", half(SD), bank(psV), ACT.Sqrt, BEPS, ["var"], ["x"])
                            if kind == "gcn2":
                                for h in hs:
                                    hold(act, (S["b_flip"], md(t, u, h)))
                                    nc.scalar.mul(B_res[:, bass.DynSlice(n * (2 * QJ) + h * QJ, QJ), :],
                                                  psT[h][:, 0:QJ * D].rearrange("p (j d) -> p j d", d=D), ALPHA
                                                  ).then_inc(S["b_read"], 1)
                            if message:
                                nxt = 0 if kind == "appnp_end" else layer + 1
                                ac("msg", half(MG), bank(psT), ACT.Relu, BM + nxt, ["msg_mm"], ["scanned"])
                            if kind == "attend":
                                ac("msg", half(MG), bank(psT), ACT.Relu, BL, ["msg_mm"], ["scanned"])
                            if kind != "attend":
                                free = (S["scat"][u], t * (32 * QJ)) if kind == "finish" else (S["kept"][u], t * 16)
                                for h in hs:
                                    hold(act, (S["back"], md(t, u, h)), free)
                                    nc.scalar.copy(SR[:, u, h * QJ:(h + 1) * QJ, :],
                                                   psB[h][:, 0:QJ * D].rearrange("p (j d) -> p j d", d=D)).then_inc(S["read"], 1)
                            if x_out:
                                made_by = "v" if kind in ("first", "gcn1") else "x"
                                hold(act, (S[made_by], md(t, u, z)))
                                act.dma_start(sup(st[x_out], n), XO[:, u, :]).then_inc(S["xkept"][u], 16)
                            if tot_out is not None:
                                hold(act, (S["scanned"], md(t, u, z)))
                                act.dma_start(sup(maxT if kind == "attend" else totT[tot_out], n), ST[wide, u, :]
                                              ).then_inc(S["totkept"][u], 16)
                            if tab_out is not None:
                                hold(act, (S["read"], md(t, u, z)))
                                act.dma_start(tab_rows(tab[tab_out], n),
                                              SR[:, u].rearrange("p (h j) d -> p h (j d)", h=2)).then_inc(S["kept"][u], 16)
                    for u in range(2):
                        for d in ("xkept", "kept", "totkept"):
                            if d in S and kind != "finish":
                                act.wait_ge(S[d][u], 16 * (NS // 2))

                @block.vector
                def _(dve):
                    nc.vector.memset(ST[:, 1, z * HALF + end:z * HALF + end + 1], 0.0)
                    if kind == "finish":
                        nc.vector.memset(NUM[:, 1, z * HALF + end:z * HALF + end + 1], 0.0)
                    if kind != "first":
                        nc.vector.memset(AG[low, z, end:end + 1], 0.0)
                    nc.vector.memset(SQ[:, 0, 0:1], 0.0).then_inc(S["carry_ok"], 1)
                    dve.wait_ge(S["carry_ok"], 1 + CREDIT)
                    with dve.Fori(0, NS // 2) as t:
                        for u in range(2):
                            def ve(name, fn, needs, frees=(), extra=()):
                                for h in hs:
                                    hold(dve, *[(S[a], md(t, u, h)) for a in needs], *[(S[a], f1(t, u, h)) for a in frees], *extra)
                                    fn(h).then_inc(S[name], 1)

                            def landed(name):
                                return (S[name][u], t * (32 if name == "row" else 16) + (32 if name == "row" else 16))

                            def stt(o, a, sc, b, op0, op1):
                                return lambda h: nc.vector.scalar_tensor_tensor(out=o(h), in0=a(h), scalar=sc, in1=b(h),
                                                                                op0=op0, op1=op1)

                            def tt(o, a, b, op):
                                return lambda h: nc.vector.tensor_tensor(o(h), a(h), b(h), op)

                            half = lambda tile, p=slice(0, P): lambda h: tile[p, h, :]
                            slot = lambda tile, p=slice(0, P): lambda h: tile[p, u, cols(h)]
                            bank = lambda ps: lambda h: ps[h][:]

                            if kind != "first":
                                ve("masked", stt(half(MS, low), slot(K, low), 0.0, slot(TOT, low), ALU.is_equal, ALU.mult),
                                   [], ["agg_d"], [landed("mask"), landed("tot")])
                                for h in hs:
                                    other = AG[low, 1 - h, end:end + 1]
                                    hold(dve, (S["masked"], md(t, u, h)), (S["agg_d"], md(t, u, h) - 1), (S[ag_used], f1(t, u, h)))
                                    nc.vector.tensor_tensor_scan(
                                        out=along(AG[low, h, :]), data0=along(K[low, u, cols(h)]), data1=along(MS[low, h, :]),
                                        initial=other, op0=ALU.mult, op1=ALU.add).then_inc(S["agg_d"], 1)
                            if kind == "first":
                                ve("v", tt(slot(XO), slot(X), slot(R), ALU.mult), [], [],
                                   [landed("state"), landed("row"), (S["xkept"][u], t * 16)])
                            if kind in ("gcn1", "gcn2"):
                                ve("u1", tt(half(Y), half(AG), slot(X), ALU.add), ["agg_d", "agg_s"],
                                   ["cent" if norm else "mm"], [landed("state")])
                                ve("u", tt(half(Y), half(Y), slot(R), ALU.mult), ["u1"], [], [landed("row")])
                            if kind == "gcn1":
                                ve("v", tt(slot(XO), half(H), slot(R), ALU.mult), ["relu"], [], [(S["xkept"][u], t * 16)])
                            if kind == "gcn2":
                                ve("y", stt(half(Y), slot(XS), 2.0, half(H), ALU.mult, ALU.add), ["relu"], [], [landed("skipped")])
                            if kind == "appnp_end":
                                ve("u1", stt(half(Y), half(AG), 1.0 - ALPHA, slot(R), ALU.mult, ALU.mult), ["agg_d", "agg_s"],
                                   ["cent"], [landed("row")])
                                ve("y", stt(half(Y), slot(X), 1.0 + ALPHA, half(Y), ALU.mult, ALU.add), ["u1"], [], [landed("state")])
                            if kind == "attend":
                                ve("y", tt(half(Y), slot(XS), half(H), ALU.add), ["relu"], ["cent"], [landed("skipped")])
                            if kind == "finish":
                                ve("diff", tt(half(Y), half(MG), half(AG), ALU.subtract), ["msg", "agg_d"], ["cent"])
                                ve("wx", tt(half(WX), half(H), slot(X), ALU.mult), ["ex"], ["summed"], [landed("state")])
                                for name, src_, dst_ in (("scanned", H, ST), ("summed", WX, NUM)):
                                    for h in hs:
                                        prev = (dst_[:, u, (1 - h) * HALF + end:(1 - h) * HALF + end + 1] if h == z else
                                                dst_[:, 1 - u, z * HALF + end:z * HALF + end + 1])
                                        hold(dve, (S["wx"], md(t, u, h)), (S[name], md(t, u, h) - 1))
                                        nc.vector.tensor_tensor_scan(
                                            out=along(dst_[:, u, cols(h)]), data0=along(K[:, u, cols(h)]), data1=along(src_[:, h, :]),
                                            initial=prev, op0=ALU.mult, op1=ALU.add).then_inc(S[name], 1)
                                ve("rden", lambda h: nc.vector.reciprocal(WX[:, h, :], ST[:, u, cols(h)]), ["scanned", "summed"])
                                ve("nf", tt(half(H), slot(NUM), half(WX), ALU.mult), ["rden"])
                                ve("y", lambda h: nc.vector.scalar_tensor_tensor(
                                    out=Y[:, h, :], in0=psM[h][:], scalar=bias[:, BO:BO + 1], in1=X[:, u, cols(h)],
                                    op0=ALU.add, op1=ALU.add), ["mm"])
                            if norm:
                                ve("rs", lambda h: nc.vector.reciprocal(SD[:, h, :], SD[:, h, :]), ["sd"])
                                x_free = ([(S["xkept"][u], t * 16)] if x_out else [(S["back"], freed2(t, u, 1))])
                                x_free += [(S["msg_mm"], freed2(t, u, 1))] if kind in ("appnp_end", "attend") else []
                                ve("x", tt(slot(XO), bank(psM), half(SD), ALU.mult), ["rs"], [], x_free)
                            if kind == "gcn2":
                                ve("msg", tt(half(MG, wide), slot(XO, wide), slot(NSR, wide), ALU.mult), ["x"], ["b_flip"],
                                   [landed("nsrc")])
                            if kind != "finish":
                                data, need = (slot(XO, wide), "v") if kind in ("first", "gcn1") else (half(MG, wide), "msg")
                                for h in hs:
                                    prev = (ST[wide, u, (1 - h) * HALF + end:(1 - h) * HALF + end + 1] if h == z else
                                            ST[wide, 1 - u, z * HALF + end:z * HALF + end + 1])
                                    hold(dve, (S[need], md(t, u, h)), (S["scanned"], md(t, u, h) - 1), landed("mask"),
                                         *([(S["totkept"][u], t * 16)] if tot_out is not None else []),
                                         *([(S["back"], freed2(t, u, 1))] if kind != "attend" else []))
                                    nc.vector.tensor_tensor_scan(
                                        out=along(ST[wide, u, cols(h)]), data0=along(K[wide, u, cols(h)]), data1=along(data(h)),
                                        initial=prev, op0=ALU.mult, op1=ALU.max if kind == "attend" else ALU.add
                                    ).then_inc(S["scanned"], 1)

        node_pass("first", "F", tab_out=0, tot_out=0, x_in="X0", x_out="V0")
        node_pass("gcn1", "R", 0, 1, 0, 1, "V0", "V1")
        with nc.sbuf_tensor("B_res", [P, NQ, D], f32) as B_res:
            node_pass("gcn2", "F", 1, 0, 1, None, "V1", "X1", skip="X0", B_res=B_res)
            assert APPNP_STEPS % 2 == 0 and APPNP_STEPS >= 4
            with nc.Fori(0, APPNP_STEPS // 2 - 1):
                appnp_pass(B_res, 0, 1)
                appnp_pass(B_res, 1, 0)
            appnp_pass(B_res, 0, 1, totT[0])
        node_pass("appnp_end", "R", 1, 0, 0, 1, "X1", "X2")
        node_pass("update", "F", 0, 1, 1, 0, "X2", "XA", layer=0)
        node_pass("update", "R", 1, 0, 0, 1, "XA", "XB", layer=1)
        node_pass("attend", "F", 0, None, 1, 0, "XB", "X3", skip="X2", layer=2)
        node_pass("finish", "R", None, None, 0, None, "X3")


_INS = ["x", "src", "dst", "edge_attr_16", "L0_gnn_W1", "L0_gnn_b1", "L0_gnn_W2", "L0_gnn_b2",
        "L2_gnn_msg_w", "L2_gnn_msg_b", "L2_gnn_upd_w", "L2_gnn_upd_b",
        "L3_gnn_W_lin", "L3_gnn_b_lin", "L3_gnn_W_out", "L3_gnn_b_out"]


def kernel(**inputs):
    import numpy as _np
    import concourse.bacc as _bacc
    from concourse.bass_utils import run_bass_kernel_spmd as _run

    nc = _bacc.Bacc("TRN2", target_bir_lowering=False, num_devices=1)
    arrays, args = {}, []
    for name in _INS:
        a = _np.ascontiguousarray(inputs[name])
        arrays[f"in_{name}"] = a
        args.append(nc.dram_tensor(f"in_{name}", a.shape, mybir.dt.from_np(a.dtype), kind="ExternalInput").ap())
    args.append(nc.dram_tensor("out_y", (N_NODES, D), mybir.dt.float32, kind="ExternalOutput").ap())
    build(nc, *args)
    r = _run(nc, [arrays], core_ids=[0])
    return r.results[0]["out_y"]
```

```python
import concourse.bass as bass
from concourse import mybir
from contextlib import ExitStack, contextmanager

N_NODES = 100000
N_EDGES = 50000
D = 64
EDGE_DIM = 16
APPNP_STEPS = 10
ALPHA = 0.1
EPS = 1e-5

P = 128
SUP = 1024
HALF = 512
QJ = HALF // P
NS = -(-N_EDGES // (2 * SUP)) * 2
EP = NS * SUP
NQ = EP // P
LO = 1024
HI = -(-N_NODES // LO)
PAD_NODE = HI * LO - 1
CREDIT = 4


def build(nc, x, src, dst, edge_attr, W1, b1, W2, b2, msg_w, msg_b, upd_w, upd_b,
          W_lin, b_lin, W_out, b_out, out):
    f32, f16, bf16, i32 = (mybir.dt.float32, mybir.dt.float16, mybir.dt.bfloat16, mybir.dt.int32)
    ALU = mybir.AluOpType
    ACT = mybir.ActivationFunctionType
    assert PAD_NODE >= N_NODES

    ctx = ExitStack()

    def sb(name, shape, dt=f32):
        return ctx.enter_context(nc.sbuf_tensor(name, shape, dt))

    def dram(name, shape, dt=f32):
        return nc.dram_tensor(name, shape, dt).ap()

    src_pad = dram("src_pad", [EP], i32)
    dst_pad = dram("dst_pad", [EP + 2], i32)
    attr_pad = dram("attr_pad", [EP, EDGE_DIM])
    node_table = dram("node_table", [P * LO, 8])
    tab = [dram(f"tab{i}", [EP + P, D]) for i in range(2)]
    totT = [dram(f"totT{i}", [NS, D, SUP]) for i in range(2)]
    maxT = dram("maxT", [NS, P, SUP])
    mask_dram = {d: dram(f"mask{d}", [NS, SUP], bf16) for d in "FR"}
    row_names = ["dis_d", "dis_s", "nsrc_s", "ndst_d", "ndst_s"]
    rows = {r: dram(f"row_{r}", [NS, SUP]) for r in row_names}
    st = {n: dram(f"state_{n}", [NS, P, SUP]) for n in ("X0", "V0", "V1", "X1", "X2", "XA", "XB", "X3")}
    primer = dram("primer", [8, 16])
    attrT = dram("attrT", [NS, EDGE_DIM, SUP])

    ident = sb("ident", [P, P])
    avg = sb("avg", [P, P])
    center = sb("center", [P, P])
    before = sb("before", [P, P])
    W1b, W2b = sb("W1b", [P, P]), sb("W2b", [P, P])
    Wm = sb("Wm", [P, 3, P])
    We = sb("We", [P, 3, P])
    Wu1, Wu2 = sb("Wu1", [P, 3, P]), sb("Wu2", [P, 3, P])
    Wl_raw, Wo_raw = sb("Wl_raw", [P, P]), sb("Wo_raw", [P, P])
    WlT, WoT = sb("WlT", [P, P]), sb("WoT", [P, P])
    bias = sb("bias", [P, 12])
    B1, B2, BL, BO, BEPS, BZ, BM, BU = 0, 1, 2, 3, 4, 5, 6, 9
    idx_src_gl = sb("idx_src_gl", [P, NQ], i32)
    idx_src_gf = sb("idx_src_gf", [P, NQ], i32)
    idx_out = sb("idx_out", [P, NQ], i32)
    a_src = sb("a_src", [P, NQ])

    begun = ctx.enter_context(nc.semaphore("begun"))
    pass_no = [0]
    wait_regs = {}
    swdge = {c: [ctx.enter_context(nc.semaphore(f"{c}{u}")) for u in range(2)] for c in ("got", "scat")}

    def hold(eng, *waits):
        values = []
        for i, (_, v) in enumerate(waits):
            if not isinstance(v, int):
                reg = wait_regs.get((eng.engine, i))
                if reg is None:
                    reg = wait_regs[eng.engine, i] = eng.alloc_register(f"wait_value{i}")
                eng.reg_mov(reg, v)
                v = reg
            values.append(v)
        eng.wait_ge(begun, 1)
        for (s, _), v in zip(waits, values):
            eng.wait_ge(s, v)

    def kept_at(t):
        return t * 16 + 16

    @contextmanager
    def stage(counts, dmas=(), stores=()):
        n = pass_no[0]
        pass_no[0] += 1
        with ExitStack() as s:
            sems = {c: s.enter_context(nc.semaphore(f"{c}_{n}")) for c in counts}
            for c in dmas:
                sems[c] = swdge[c] if c in swdge else [s.enter_context(nc.semaphore(f"{c}{u}_{n}")) for u in range(2)]
            for k, c in enumerate(stores):
                sems[c] = swdge[c] if c in swdge else [s.enter_context(nc.semaphore(f"{c}{u}_{n}")) for u in range(2)]
                for u in range(2):
                    (nc.gpsimd if c in swdge else nc.sync).dma_start(
                        primer[2 * k + u:2 * k + u + 1, :], ident[0:1, 0:16]).then_inc(sems[c][u], 16)
            for c in counts:
                nc.gpsimd.sem_inc(sems[c], CREDIT)
            nc.all_engine_barrier()
            with ExitStack() as bufs:
                with nc.Block() as block:
                    yield block, sems, lambda name, shape, dt=f32: bufs.enter_context(
                        nc.sbuf_tensor(f"{name}_{n}", shape, dt)), lambda name, shape=[P, HALF]: bufs.enter_context(
                        nc.psum_tensor(f"{name}_{n}", shape, f32))
            nc.all_engine_barrier()
            for c, own in swdge.items():
                if c in sems:
                    nc.gpsimd.dma_reset(range(own[0].num, own[1].num + 1))
            for c in sems.values():
                for one in (c if isinstance(c, list) else [c]):
                    nc.gpsimd.sem_clear(one)

    def made(t, u, h):
        return 4 * t + 2 * u + h + 1 + CREDIT

    def freed1(t, u, h):
        return 4 * t + 2 * u + h - 1 + CREDIT

    def freed2(t, u, h):
        return 4 * t + 2 * u + h - 3 + CREDIT

    with ctx:
        with ExitStack() as s:
            prep = s.enter_context(nc.semaphore("prep"))
            loaded = s.enter_context(nc.semaphore("loaded"))
            built = s.enter_context(nc.semaphore("built"))
            shaped = s.enter_context(nc.semaphore("shaped"))
            flipped = s.enter_context(nc.semaphore("flipped"))
            kept = s.enter_context(nc.semaphore("kept"))
            padi = s.enter_context(nc.sbuf_tensor("padi", [16, (EP - N_EDGES) // 16], i32))
            sentinel = s.enter_context(nc.sbuf_tensor("sentinel", [1, 2], i32))
            zeros = s.enter_context(nc.sbuf_tensor("zeros", [P, (EP - N_EDGES) * EDGE_DIM // 16], f32))
            ps = s.enter_context(nc.psum_tensor("ps_prep", [P, 2, HALF], f32))
            nw = [0]

            def load(dstap, srcap):
                nc.sync.dma_start(dstap, srcap).then_inc(loaded, 16)
                nw[0] += 1

            with nc.Block() as block:
                @block.vector
                def _(dve):
                    nc.vector.memset(padi[:], PAD_NODE)
                    nc.vector.memset(sentinel[:], -1)
                    for w in (zeros, W1b, W2b, Wm, We, Wu1, Wu2, Wl_raw, Wo_raw, bias, avg, ident):
                        nc.vector.memset(w[:], 0.0)
                    nc.vector.memset(before[:], 1.0).then_inc(prep, 1)
                    dve.wait_ge(prep, 1)
                    nc.vector.memset(bias[:, BEPS:BEPS + 1], EPS)
                    nc.vector.memset(avg[0:D, 0:D], 1.0 / D)
                    nc.vector.memset(avg[D:P, D:P], 1.0 / D).then_inc(prep, 1)
                    dve.wait_ge(shaped, 2)
                    nc.vector.tensor_tensor(center[:], ident[:], avg[:], ALU.subtract).then_inc(built, 1)
                    dve.wait_ge(flipped, 2)
                    nc.vector.tensor_copy(WlT[:], ps[:, 0, 0:P])
                    nc.vector.tensor_copy(WoT[:], ps[:, 1, 0:P]).then_inc(built, 1)

                @block.gpsimd
                def _(pool):
                    pool.wait_ge(prep, 2)
                    nc.gpsimd.affine_select(out=ident[:], in_=ident[:], compare_op=ALU.not_equal, fill=1.0,
                                            base=0, pattern=[[1, P]], channel_multiplier=-1).then_inc(shaped, 1)
                    pool.wait_ge(shaped, 1)
                    nc.gpsimd.affine_select(out=before[:], in_=before[:], compare_op=ALU.is_gt, fill=0.0,
                                            base=0, pattern=[[1, P]], channel_multiplier=-1).then_inc(shaped, 1)

                @block.sync
                def _(sp):
                    sp.wait_ge(prep, 2)
                    for k in range(2):
                        o = k * D
                        load(W1b[o:o + D, o:o + D], W1)
                        load(W2b[o:o + D, o:o + D], W2)
                        load(bias[o:o + D, B1:B1 + 1], b1.rearrange("(d a) -> d a", a=1))
                        load(bias[o:o + D, B2:B2 + 1], b2.rearrange("(d a) -> d a", a=1))
                        load(bias[o:o + D, BO:BO + 1], b_out.rearrange("(d a) -> d a", a=1))
                        r = D - o
                        load(bias[o:o + D, BL:BL + 1], b_lin[r:r + D].rearrange("(d a) -> d a", a=1))
                        load(Wo_raw[0:D, o:o + D], W_out[:, r:r + D])
                        for k2 in range(2):
                            load(Wl_raw[o:o + D, k2 * D:k2 * D + D], W_lin[r:r + D, D - k2 * D:2 * D - k2 * D])
                        for l in range(3):
                            load(Wu1[o:o + D, l, o:o + D], upd_w[l, 0:D, :])
                            load(Wu2[o:o + D, l, o:o + D], upd_w[l, D:2 * D, :])
                            load(bias[o:o + D, BU + l:BU + l + 1], upd_b[l].rearrange("(d a) -> d a", a=1))
                    for l in range(3):
                        load(Wm[:, l, D:P], msg_w[l, 0:2 * D, :])
                        load(We[0:EDGE_DIM, l, D:P], msg_w[l, 2 * D:2 * D + EDGE_DIM, :])
                        load(bias[D:P, BM + l:BM + l + 1], msg_b[l].rearrange("(d a) -> d a", a=1))
                    load(src_pad[0:N_EDGES].rearrange("(a b) -> a b", a=16), src.rearrange("(a b) -> a b", a=16))
                    load(src_pad[N_EDGES:EP].rearrange("(a b) -> a b", a=16), padi[:])
                    load(dst_pad[1:1 + N_EDGES].rearrange("(a b) -> a b", a=16), dst.rearrange("(a b) -> a b", a=16))
                    load(dst_pad[1 + N_EDGES:1 + EP].rearrange("(a b) -> a b", a=16), padi[:])
                    load(dst_pad[0:1].rearrange("(a b) -> a b", a=1), sentinel[:, 0:1])
                    load(dst_pad[EP + 1:EP + 2].rearrange("(a b) -> a b", a=1), sentinel[:, 1:2])
                    load(attr_pad[0:N_EDGES, :].rearrange("(a b) d -> a (b d)", a=16),
                         edge_attr.rearrange("(a b) d -> a (b d)", a=16))
                    load(attr_pad[N_EDGES:EP, :].rearrange("(a b) d -> a (b d)", a=16), zeros[0:16, :])
                    for k in range(2):
                        load(tab[k][EP:EP + P, :], zeros[:, 0:D])
                    sp.wait_ge(loaded, 16 * nw[0])
                    sp.sem_inc(kept, 1)

                @block.tensor
                def _(pe):
                    pe.wait_ge(kept, 1)
                    pe.wait_ge(shaped, 1)
                    nc.tensor.transpose(ps[:, 0, 0:P], Wl_raw[:], ident[:]).then_inc(flipped, 1)
                    nc.tensor.transpose(ps[:, 1, 0:P], Wo_raw[:], ident[:]).then_inc(flipped, 1)
            nc.all_engine_barrier()
            for one in (prep, loaded, built, shaped, flipped, kept):
                nc.gpsimd.sem_clear(one)
            nc.gpsimd.sem_inc(begun, 1)

        def edge_view(v, t, u, n=1):
            r = v.rearrange("(s h p j) -> p s h j", h=2, p=P, j=QJ * n)
            return r[:, bass.DynSlice(2 * t + u, 1), :, :].rearrange("p s h j -> p (s h) j")

        UNR = 4
        with stage(["onehot", "counted", "flipped", "flip_read", "attr_flipped", "attr_read", "chain"],
                   ["idx", "got", "attr"], ["kept", "attr_kept"]) as (block, S, sbt, pst):
            step = S["chain"]
            nodes = sbt("nodes", [P, 2, NQ], i32)
            lo_i, hi_i = sbt("lo_i", [P, 2, NQ], i32), sbt("hi_i", [P, 2, NQ], i32)
            lo, hi = sbt("lo", [P, 2, NQ]), sbt("hi", [P, 2, NQ])
            ramp_i, ramp = sbt("ramp_i", [P, LO], i32), sbt("ramp", [P, LO], f16)
            oh = sbt("oh", [P, 2, 2, LO + P], f16)
            I = sbt("I", [P, 2, 2, 2 * QJ], i32)
            G = sbt("G", [P, 2, 2 * QJ, P])
            XT = sbt("XT", [P, 2, SUP])
            AT = sbt("AT", [P, 2, 2 * QJ, EDGE_DIM])
            ATT = sbt("ATT", [EDGE_DIM, 2, SUP])
            psX = [pst(f"psX{h}") for h in range(2)]
            psH = [[pst(f"psH{k}{b}") for b in range(2)] for k in range(2)]
            psA = [pst(f"psA{h}", [P, HALF]) for h in range(2)]
            dsts = sbt("dsts", [NS, 3, SUP], i32)
            msk = sbt("msk", [NS, 2, SUP], bf16)
            de = sbt("de", [P, 2, NQ], i32)
            def_ = sbt("def_", [P, 2, NQ])
            cnt = sbt("cnt", [P, 2, LO])
            ones = sbt("ones", [P, LO])
            incl, sq = sbt("incl", [P, LO]), sbt("sq", [P, 3, LO])
            valid, first_e = sbt("valid", [P, LO]), sbt("first_e", [P, LO])
            ntab = sbt("ntab", [P, LO, 8])
            nothing = sbt("nothing", [P, HALF], f16)

            with ExitStack() as s2:
                once = s2.enter_context(nc.semaphore("once"))
                ramp_ok = s2.enter_context(nc.semaphore("ramp_ok"))
                roots = s2.enter_context(nc.semaphore("roots"))
                offset_ok = s2.enter_context(nc.semaphore("offset_ok"))
                masks_ok = s2.enter_context(nc.semaphore("masks_ok"))
                stored = s2.enter_context(nc.semaphore("stored"))
                table_ok = s2.enter_context(nc.semaphore("table_ok"))
                sums_ok = s2.enter_context(nc.semaphore("sums_ok"))
                zeroed = s2.enter_context(nc.semaphore("zeroed"))
                zeros_ok = s2.enter_context(nc.semaphore("zeros_ok"))

                @block.sync
                def _(sp):
                    sp.dma_start(nodes[:, 0, :], src_pad.rearrange("(p q) -> p q", p=P)).then_inc(once, 16)
                    sp.dma_start(nodes[:, 1, :], dst_pad[1:1 + EP].rearrange("(p q) -> p q", p=P)).then_inc(once, 16)
                    for k in range(3):
                        sp.dma_start(dsts[:, k, :], dst_pad[k:k + EP].rearrange("(r c) -> r c", r=NS)).then_inc(once, 16)
                    for k in range(2):
                        sp.dma_start(de[:, k, :].rearrange("p (s j) -> p s j", j=QJ),
                                     dst_pad[k:k + EP].rearrange("(s p j) -> p s j", p=P, j=QJ)).then_inc(once, 16)
                    with sp.Fori(0, NS // 2) as t:
                        for u in range(2):
                            hold(sp, (S["flipped"], freed2(t, u, 1)))
                            sp.dma_start(I[:, u, 0, :].rearrange("p (h j) -> p h j", j=QJ),
                                         edge_view(dst_pad[1:1 + EP], t, u)).then_inc(S["idx"][u], 16)
                            sp.dma_start(I[:, u, 1, :].rearrange("p (h j) -> p h j", j=QJ),
                                         edge_view(src_pad, t, u)).then_inc(S["idx"][u], 16)
                            hold(sp, (S["attr_flipped"], freed2(t, u, 1)))
                            sp.dma_start(AT[:, u].rearrange("p (h j) d -> p h (j d)", h=2),
                                         edge_view(attr_pad.rearrange("e d -> (e d)"), t, u, EDGE_DIM)
                                         ).then_inc(S["attr"][u], 16)
                    sp.wait_ge(masks_ok, 1)
                    sp.dma_start(mask_dram["F"][:, :], msk[:, 0, :]).then_inc(stored, 16)
                    sp.dma_start(mask_dram["R"][:, :], msk[:, 1, :]).then_inc(stored, 16)
                    sp.wait_ge(table_ok, 1)
                    sp.dma_start(node_table.rearrange("(p l) f -> p (l f)", p=P),
                                 ntab[:].rearrange("p l f -> p (l f)")).then_inc(stored, 16)
                    sp.wait_ge(stored, 48)

                @block.gpsimd
                def _(pool):
                    nc.gpsimd.iota(ramp_i[:], pattern=[[1, LO]], base=0, channel_multiplier=0).then_inc(ramp_ok, 1)
                    nc.gpsimd.memset(G[:], 0.0).then_inc(zeroed, 1)
                    pool.wait_ge(zeroed, 1)
                    top = pool.to_reg(N_NODES - 1)
                    with pool.Fori(0, NS // 2) as t:
                        for u in range(2):
                            hold(pool, (S["idx"][u], t * 32 + 32), (S["flipped"], freed2(t, u, 1)))
                            for q in range(2 * QJ):
                                for k in range(2):
                                    nc.gpsimd.indirect_dma_start(
                                        out=G[:, u, q, k * D:k * D + D], out_offset=None, in_=x[:, :],
                                        in_offset=bass.IndirectOffsetOnAxis(ap=I[:, u, k, q:q + 1], axis=0),
                                        bounds_check=top, oob_is_err=False).then_inc(S["got"][u], 16)

                @block.tensor
                def _(pe):
                    pe.wait_ge(zeros_ok, 1)
                    for k in range(2):
                        for b in range(2):
                            nc.tensor.matmul(psH[k][b][:], nothing[:, 0:P], nothing[:],
                                             start=True, stop=True)
                    with pe.Fori(0, NS // 2) as t:
                        for u in range(2):
                            for h in range(2):
                                for i in range(UNR):
                                    n = 8 * t + 4 * u + 2 * h
                                    for k in range(2):
                                        hold(pe, (S["onehot"], (4 * t + 2 * u + h) * (UNR * 2) + (i * 2 + k + 1) + CREDIT))
                                        for b in range(2):
                                            last = nc.tensor.matmul(psH[k][b][:], oh[:, i % 2, k, LO:LO + P],
                                                                    oh[:, i % 2, k, b * HALF:(b + 1) * HALF],
                                                                    start=False, stop=True, skip_group_check=True)
                                        last.then_inc(S["counted"], 1)
                            for h in range(2):
                                hold(pe, (S["got"][u], t * (16 * 4 * QJ) + 16 * 4 * QJ), (S["flip_read"], freed1(t, u, h)))
                                for j in range(QJ):
                                    last = nc.tensor.transpose(psX[h][:].rearrange("f (p j) -> f j p", j=QJ)[:, j, :],
                                                               G[:, u, h * QJ + j, :], ident[:])
                                last.then_inc(S["flipped"], 1)
                                hold(pe, (S["attr"][u], t * 16 + 16), (S["attr_read"], freed1(t, u, h)))
                                for j in range(QJ):
                                    last = nc.tensor.transpose(
                                        psA[h][0:EDGE_DIM, :].rearrange("f (p j) -> f j p", j=QJ)[:, j, :],
                                        AT[:, u, h * QJ + j, :], ident[:])
                                last.then_inc(S["attr_flipped"], 1)
                    pe.wait_ge(sums_ok, 1)
                    pe.wait_ge(S["flip_read"], made(NS // 2 - 1, 1, 1))
                    nc.tensor.matmul(psX[0][:, 0:1], before[:], incl[:, LO - 1:LO], start=True, stop=True).then_inc(offset_ok, 1)

                @block.scalar
                def _(act):
                    with act.Fori(0, NS // 2) as t:
                        for u in range(2):
                            for h in range(2):
                                hold(act, (S["flipped"], made(t, u, h)), (S["kept"][u], kept_at(t)))
                                nc.scalar.copy(XT[:, u, h * HALF:(h + 1) * HALF], psX[h][:]).then_inc(S["flip_read"], 1)
                                hold(act, (S["attr_flipped"], made(t, u, h)), (S["attr_kept"][u], kept_at(t)))
                                nc.scalar.copy(ATT[:, u, h * HALF:(h + 1) * HALF], psA[h][0:EDGE_DIM, :]).then_inc(S["attr_read"], 1)
                            hold(act, (S["flip_read"], made(t, u, 1)), (S["attr_read"], made(t, u, 1)))
                            act.dma_start(st["X0"][bass.DynSlice(2 * t + u, 1), :, :].rearrange("s p e -> p (s e)"),
                                          XT[:, u, :]).then_inc(S["kept"][u], 16)
                            act.dma_start(attrT[bass.DynSlice(2 * t + u, 1), :, :].rearrange("s p e -> p (s e)"),
                                          ATT[:, u, :]).then_inc(S["attr_kept"][u], 16)
                    for u in range(2):
                        act.wait_ge(S["kept"][u], kept_at(NS // 2))
                        act.wait_ge(S["attr_kept"][u], kept_at(NS // 2))
                    act.wait_ge(sums_ok, 1)
                    nc.scalar.activation(sq[:], sq[:], ACT.Sqrt, bias=bias[:, BZ:BZ + 1]).then_inc(roots, 1)

                @block.vector
                def _(dve):
                    c = [CREDIT]

                    def link(ins):
                        c[0] += 1
                        ins.then_inc(step, 1)
                        dve.wait_ge(step, c[0])

                    dve.wait_ge(once, 16 * 7)
                    dve.wait_ge(ramp_ok, 1)
                    nc.vector.memset(nothing[:], 0.0).then_inc(zeros_ok, 1)
                    nc.vector.tensor_copy(ramp[:], ramp_i[:])
                    nc.vector.tensor_scalar(lo_i[:], nodes[:], LO - 1, None, ALU.bitwise_and)
                    link(nc.vector.tensor_scalar(hi_i[:], nodes[:], 10, None, ALU.logical_shift_right))
                    nc.vector.tensor_copy(lo[:], lo_i[:])
                    link(nc.vector.tensor_copy(hi[:], hi_i[:]))
                    nc.vector.tensor_tensor(msk[:, 0, :], dsts[:, 1, :], dsts[:, 0, :], ALU.is_equal)
                    nc.vector.tensor_tensor(msk[:, 1, :], dsts[:, 1, :], dsts[:, 2, :], ALU.is_equal).then_inc(masks_ok, 1)
                    link(nc.vector.tensor_copy(def_[:], de[:]))
                    link(nc.vector.tensor_tensor(def_[:, 0, :], def_[:, 0, :], def_[:, 1, :], ALU.is_equal))
                    link(nc.vector.scalar_tensor_tensor(out=def_[:, 0, :], in0=def_[:, 0, :], scalar=float(2 * N_NODES),
                                                        in1=def_[:, 1, :], op0=ALU.mult, op1=ALU.add))
                    nc.vector.tensor_copy(idx_out[:], def_[:, 0, :])
                    with dve.Fori(0, NS // 2) as t:
                        for g in range(4):
                            for i in range(UNR):
                                for k in range(2):
                                    n = t * (UNR * 8) + (g * UNR + i) * 2 + k
                                    hold(dve, (S["counted"], n + (CREDIT - 3)))
                                    col = t * (4 * UNR) + g * UNR + i
                                    nc.vector.tensor_scalar(oh[:, i % 2, k, 0:LO], ramp[:], lo[:, k, bass.DynSlice(col, 1)],
                                                            None, ALU.is_equal)
                                    nc.vector.tensor_scalar(oh[:, i % 2, k, LO:LO + P], ramp[:, 0:P],
                                                            hi[:, k, bass.DynSlice(col, 1)], None,
                                                            ALU.is_equal).then_inc(S["onehot"], 1)
                    dve.wait_ge(S["counted"], 2 * NQ + CREDIT)
                    nc.vector.memset(ones[:], 1.0)
                    nc.vector.memset(ntab[:], 0.0)
                    for k in range(2):
                        for b in range(2):
                            l = nc.vector.tensor_copy(cnt[:, k, b * HALF:(b + 1) * HALF], psH[k][b][:])
                    link(l)
                    nc.vector.tensor_scalar(sq[:, 0, :], cnt[:, 1, :], 1.0, None, ALU.add)
                    nc.vector.tensor_scalar(sq[:, 1, :], cnt[:, 0, :], 1.0, None, ALU.max)
                    nc.vector.tensor_scalar(sq[:, 2, :], cnt[:, 1, :], 1.0, None, ALU.max)
                    nc.vector.tensor_scalar(valid[:], cnt[:, 1, :], 1.0, None, ALU.min)
                    nc.vector.tensor_tensor_scan(out=incl[:], data0=ones[:], data1=cnt[:, 1, :], initial=0.0,
                                                 op0=ALU.mult, op1=ALU.add).then_inc(sums_ok, 1)
                    dve.wait_ge(offset_ok, 1)
                    dve.wait_ge(roots, 1)
                    link(nc.vector.tensor_scalar(incl[:], incl[:], psX[0][:, 0:1], None, ALU.add))
                    for k in range(3):
                        nc.vector.reciprocal(ntab[:, :, k], sq[:, k, :])
                    link(nc.vector.tensor_tensor(first_e[:], incl[:], cnt[:, 1, :], ALU.subtract))
                    link(nc.vector.tensor_tensor(incl[:], incl[:], valid[:], ALU.mult))
                    link(nc.vector.scalar_tensor_tensor(out=first_e[:], in0=first_e[:], scalar=1.0, in1=valid[:],
                                                        op0=ALU.add, op1=ALU.mult))
                    nc.vector.tensor_scalar(ntab[:, :, 3], incl[:], -1.0, None, ALU.add)
                    nc.vector.tensor_scalar(ntab[:, :, 4], first_e[:], -1.0, None, ALU.add).then_inc(table_ok, 1)

        for one in (once, ramp_ok, roots, offset_ok, masks_ok, stored, table_ok, sums_ok, zeroed, zeros_ok):
            nc.gpsimd.sem_clear(one)

        CH = SUP
        n_full = N_NODES // CH
        rest = (N_NODES - n_full * CH) // 2
        REST_P = 112
        assert n_full % 2 == 1 and rest == REST_P * 3
        LNS = ["sq", "var", "sd", "rs", "ln"]
        dense_ops = ["xin", "x0", "m1", "h1", "m2", "h2", "y1", "ma", "ha", "mb", "hb", "mc", "hc", "y3", "y4",
                     "back", "read"] + [f"{o}{i}" for i in "1234" for o in ("ce", "sq", "va", "ln", "rs", "x")]
        with stage(dense_ops + ["copied"], ["nidx", "got", "nx"], ["nkept"]) as (block, S, sbt, pst):
            RES = sbt("RES", [P, 2, 8, NQ])
            T = sbt("T", [P, 2, 2, 2 * QJ, 8])
            I = sbt("I", [P, 2, 2, 2 * QJ], i32)
            X = sbt("X", [P, 2, 2, QJ, 2, D])
            Xt, H, Hb, Y, SD = (sbt(n, [P, 2, 2, HALF]) for n in ("Xt", "H", "Hb", "Y", "SD"))
            Xo = sbt("Xo", [P, 2, 2, QJ, 2, D])
            miss = sbt("miss", [P, NQ])
            zr_i, zr = sbt("zr_i", [P, 1], i32), sbt("zr", [P, 1])
            psT, psM = ([[pst(f"{n}{u}{h}") for h in range(2)] for u in range(2)] for n in ("psT", "psM"))
            with ExitStack() as s2:
                ramped = s2.enter_context(nc.semaphore("ramped"))
                fin = s2.enter_context(nc.semaphore("fin"))
                rows_ok = s2.enter_context(nc.semaphore("rows_ok"))
                rows_kept = s2.enter_context(nc.semaphore("rows_kept"))

                @block.gpsimd
                def _(pool):
                    nc.gpsimd.iota(zr_i[:], pattern=[[0, 1]], base=EP + 1, channel_multiplier=1).then_inc(ramped, 1)
                    with pool.Fori(0, NS // 2) as t:
                        for u in range(2):
                            hold(pool, (S["nidx"][u], t * 32 + 32), (S["copied"], 2 * t + u - 1 + CREDIT))
                            for q in range(2 * QJ):
                                for k in range(2):
                                    nc.gpsimd.indirect_dma_start(
                                        out=T[:, u, k, q, :], out_offset=None, in_=node_table[:, :],
                                        in_offset=bass.IndirectOffsetOnAxis(ap=I[:, u, k, q:q + 1], axis=0),
                                    ).then_inc(S["got"][u], 16)

                TT = (n_full - 1) // 4
                assert 4 * TT == n_full - 1
                every = [(u, h, P, QJ, HALF) for u in range(2) for h in range(2)]
                final = [(0, 0, P, QJ, HALF), (0, 1, REST_P, 3, rest)]

                def node_rows(v, t, u, h, a):
                    return v[bass.DynSlice((4 * t + 2 * u + h) * CH + a * HALF, HALF), :].rearrange(
                        "(p j) d -> p j d", j=QJ)

                def last_rows(v, h, a):
                    jj, ww = final[h][3:]
                    at = (n_full - 1 + h) * CH + a * ww
                    return v[at:at + ww, :].rearrange("(p j) d -> p j d", j=jj)

                @block.sync
                def _(sp):
                    def idx_load(t, u):
                        hold(sp, (S["copied"], 2 * t + u - 1 + CREDIT))
                        sp.dma_start(I[:, u, 0, :].rearrange("p (h j) -> p h j", j=QJ),
                                     edge_view(dst_pad[1:1 + EP], t, u)).then_inc(S["nidx"][u], 16)
                        sp.dma_start(I[:, u, 1, :].rearrange("p (h j) -> p h j", j=QJ),
                                     edge_view(src_pad, t, u)).then_inc(S["nidx"][u], 16)

                    with sp.Fori(0, TT) as t:
                        for u in range(2):
                            idx_load(t, u)
                            hold(sp, (S["xin"], freed2(t, u, 1)))
                            for h in range(2):
                                for a in range(2):
                                    sp.dma_start(X[:, u, h, :, a, :], node_rows(x, t, u, h, a)).then_inc(S["nx"][u], 16)
                    sp.wait_ge(S["xin"], freed2(TT, 0, 1))
                    for _, h, pp, jj, ww in final:
                        for a in range(2):
                            sp.dma_start(X[0:pp, 0, h, 0:jj, a, :], last_rows(x, h, a)).then_inc(S["nx"][0], 16)
                    with sp.Fori(TT, NS // 2) as t:
                        for u in range(2):
                            idx_load(t, u)
                    sp.wait_ge(rows_ok, 1)
                    for name, k, f in (("dis_d", 0, 0), ("dis_s", 1, 0), ("nsrc_s", 1, 1), ("ndst_d", 0, 2), ("ndst_s", 1, 2)):
                        sp.dma_start(rows[name].rearrange("s (h p j) -> p (s h) j", h=2, j=QJ),
                                     RES[:, k, f, :].rearrange("p (s j) -> p s j", j=QJ)).then_inc(rows_kept, 16)
                    sp.wait_ge(rows_kept, 16 * 5)

                def dense_pe(pe, t, units):
                    def mm(name, ps, w, rhs, need, free=()):
                        for u, h, _, _, W in units:
                            hold(pe, (S[need], made(t, u, h)), *[(S[m], freed2(t, u, h)) for m in free])
                            nc.tensor.matmul(ps[u][h][:, 0:W], w, rhs[:, u, h, 0:W], start=True, stop=True
                                             ).then_inc(S[name], 1)

                    def ln(i, y):
                        mm("ce" + i, psM, center[:], Y, y)
                        mm("va" + i, psT, avg[:], Y, "sq" + i)

                    for u, h, pp, jj, W in units:
                        hold(pe, (S["nx"][u], 64 * t + 64), (S["ln4"], freed2(t, u, h)))
                        for j in range(jj):
                            last = nc.tensor.transpose(psT[u][h][:, 0:W].rearrange("f (p j) -> f j p", j=jj)[:, j, :],
                                                       X[0:pp, u, h, j, :, :].rearrange("p a d -> p (a d)"), ident[0:pp, 0:pp])
                        last.then_inc(S["xin"], 1)
                    mm("m1", psM, W1b[:], Xt, "x0", ("read",))
                    mm("m2", psM, W2b[:], H, "h1")
                    ln("1", "y1")
                    ln("2", "x1")
                    mm("ma", psM, Wu1[:, 0, :], Hb, "x2")
                    mm("mb", psM, Wu1[:, 1, :], H, "ha")
                    mm("mc", psM, Wu1[:, 2, :], Xt, "hb")
                    ln("3", "y3")
                    ln("4", "y4")
                    for u, h, pp, jj, W in units:
                        hold(pe, (S["x4"], made(t, u, h)))
                        for j in range(jj):
                            last = nc.tensor.transpose(psM[u][h][0:pp, j * P:(j + 1) * P],
                                                       H[:, u, h, 0:W].rearrange("f (p j) -> f j p", j=jj)[:, j, :], ident[:])
                        last.then_inc(S["back"], 1)

                @block.tensor
                def _(pe):
                    with pe.Fori(0, TT) as t:
                        dense_pe(pe, t, every)
                    dense_pe(pe, TT, final)

                def dense_act(act, t, units):
                    def ac(name, o, i, func, need, b, free=(), scale=1.0):
                        for u, h, _, _, W in units:
                            hold(act, (S[need], made(t, u, h)), *[(S[f], freed2(t, u, h)) for f in free])
                            src_ = i[:, u, h, 0:W] if i is SD else i[u][h][:, 0:W]
                            nc.scalar.activation(o[:, u, h, 0:W], src_, func, bias=bias[:, b:b + 1], scale=scale
                                                 ).then_inc(S[name], 1)

                    def ln(i):
                        ac("sq" + i, Y, psM, ACT.Square, "ce" + i, BZ)
                        ac("ln" + i, SD, psT, ACT.Ln, "va" + i, BEPS)
                        ac("rs" + i, SD, SD, ACT.Exp, "ln" + i, BZ, scale=-0.5)

                    for u, h, _, _, W in units:
                        hold(act, (S["xin"], made(t, u, h)), (S["mc"], freed2(t, u, h)))
                        nc.scalar.copy(Xt[:, u, h, 0:W], psT[u][h][:, 0:W]).then_inc(S["x0"], 1)
                    ac("h1", H, psM, ACT.Relu, "m1", B1, free=("back",))
                    ac("h2", Hb, psM, ACT.Relu, "m2", B2, free=("y3",))
                    ln("1")
                    ln("2")
                    ac("ha", H, psM, ACT.Relu, "ma", BU)
                    ac("hb", Xt, psM, ACT.Relu, "mb", BU + 1)
                    ac("hc", H, psM, ACT.Relu, "mc", BU + 2)
                    ln("3")
                    ln("4")
                    for u, h, pp, jj, W in units:
                        hold(act, (S["back"], made(t, u, h)), (S["nkept"][u], t * 64 + 16))
                        nc.scalar.copy(Xo[0:pp, u, h, 0:jj].rearrange("p j a d -> p (j a d)"),
                                       psM[u][h][0:pp, 0:jj * P]).then_inc(S["read"], 1)
                    for u, h, pp, jj, W in units:
                        hold(act, (S["read"], made(t, u, h)))
                        for a in range(2):
                            act.dma_start(node_rows(out, t, u, h, a) if units is every else last_rows(out, h, a),
                                          Xo[0:pp, u, h, 0:jj, a, :]).then_inc(S["nkept"][u], 16)

                @block.scalar
                def _(act):
                    with act.Fori(0, TT) as t:
                        dense_act(act, t, every)
                    dense_act(act, TT, final)
                    act.wait_ge(S["nkept"][0], 16 + 64 * TT + 64)
                    act.wait_ge(S["nkept"][1], 16 + 64 * TT)

                def keep_scalars(dve, t, u):
                    hold(dve, (S["got"][u], t * (16 * 4 * QJ) + 16 * 4 * QJ))
                    for k in range(2):
                        last = nc.vector.tensor_copy(
                            RES[:, k, :, bass.DynSlice((2 * t + u) * 2 * QJ, 2 * QJ)],
                            T[:, u, k].rearrange("p q f -> p f q"))
                    last.then_inc(S["copied"], 1)

                def dense_dve(dve, t, units):
                    def ve(name, fn, *needs):
                        for u, h, _, _, W in units:
                            hold(dve, *[(S[n], made(t, u, h)) for n in needs])
                            fn(u, h, W).then_inc(S[name], 1)

                    def stt(o, a, sc, b, op0=ALU.mult, op1=ALU.add):
                        return lambda u, h, W: nc.vector.scalar_tensor_tensor(
                            out=o[:, u, h, 0:W], in0=a[:, u, h, 0:W], scalar=sc, in1=b[:, u, h, 0:W], op0=op0, op1=op1)

                    def ln(i, o, factor=1.0):
                        ve("x" + i, lambda u, h, W: nc.vector.scalar_tensor_tensor(
                            out=o[:, u, h, 0:W], in0=psM[u][h][:, 0:W], scalar=factor, in1=SD[:, u, h, 0:W],
                            op0=ALU.mult, op1=ALU.mult), "rs" + i)

                    ve("y1", stt(Y, Xt, 2.0, Hb), "h2", "x0")
                    ln("1", Y, 1.0 + ALPHA)
                    ln("2", Hb)
                    ve("y3", stt(Y, Hb, 1.0, H), "hc", "x2")
                    ln("3", Y)
                    ve("y4", lambda u, h, W: nc.vector.tensor_scalar(
                        Y[:, u, h, 0:W], Y[:, u, h, 0:W], bias[:, BO:BO + 1], None, ALU.add), "x3")
                    ln("4", H)

                @block.vector
                def _(dve):
                    dve.wait_ge(ramped, 1)
                    nc.vector.tensor_copy(zr[:], zr_i[:])
                    with dve.Fori(0, TT) as t:
                        for u in range(2):
                            keep_scalars(dve, t, u)
                        dense_dve(dve, t, every)
                    with dve.Fori(TT, NS // 2) as t:
                        for u in range(2):
                            keep_scalars(dve, t, u)
                    dense_dve(dve, TT, final)
                    dve.wait_ge(S["copied"], NS + CREDIT)
                    n = 0
                    for f, o in ((3, idx_src_gl), (4, idx_src_gf)):
                        nc.vector.tensor_scalar(miss[:], RES[:, 1, f, :], 0.0, zr[:, 0:1], ALU.is_lt, ALU.mult).then_inc(fin, 1)
                        n += 1
                        dve.wait_ge(fin, n)
                        nc.vector.tensor_tensor(o[:], RES[:, 1, f, :], miss[:], ALU.add).then_inc(fin, 1)
                        n += 1
                        dve.wait_ge(fin, n)
                    nc.vector.scalar_tensor_tensor(out=a_src[:], in0=RES[:, 1, 1, :], scalar=1.0 - ALPHA,
                                                   in1=RES[:, 1, 2, :], op0=ALU.mult, op1=ALU.mult).then_inc(rows_ok, 1)

        for one in (ramped, fin, rows_ok, rows_kept):
            nc.gpsimd.sem_clear(one)

        def order(direction, t, u):
            return 2 * t + u if direction == "F" else (NS - 1 - u) - 2 * t

        def halves(direction):
            return (0, 1) if direction == "F" else (1, 0)

        def sup(v, n):
            return v[bass.DynSlice(n, 1), :, :].rearrange("s p e -> p (s e)")

        def spread(v, n, parts):
            return v[bass.DynSlice(n, 1), :].to_broadcast([parts, SUP])

        def tab_rows(v, n):
            return v[0:EP, :].rearrange("(s h p j) d -> p s h (j d)", h=2, p=P, j=QJ)[:, bass.DynSlice(n, 1), :, :] \
                .rearrange("p s h e -> p (s h) e")

        def appnp_pass(B_res, t_in, t_out, keepT=None):
            with stage(["scaled", "added", "flipped", "scanned", "back", "read"],
                       ["idx", "got", "mask"], ["kept"] + (["keptT"] if keepT is not None else [])) as (block, S, sbt, pst):
                I = sbt("I", [P, 2, 2 * QJ], i32)
                G = sbt("G", [P, 2, 2 * QJ, D])
                M = sbt("M", [P, 2 * QJ, D])
                K = sbt("K", [D, 2, SUP], bf16)
                ST = sbt("ST", [D, 2, SUP])
                SR = sbt("SR", [P, 2, 2 * QJ, D])
                psT = [pst(f"psT{h}") for h in range(2)]
                psB = [pst(f"psB{h}") for h in range(2)]
                tin, tout = tab[t_in], tab[t_out]

                @block.sync
                def _(sp):
                    with sp.Fori(0, NS // 2) as t:
                        for u in range(2):
                            hold(sp, (S["scaled"], freed2(t, u, 1)))
                            sp.dma_start(I[:, u, :], idx_src_gl[:, bass.DynSlice((2 * t + u) * 2 * QJ, 2 * QJ)]
                                         ).then_inc(S["idx"][u], 16)
                            hold(sp, (S["scanned"], freed2(t, u, 1)))
                            sp.dma_start(K[:, u, :], spread(mask_dram["F"], 2 * t + u, D)).then_inc(S["mask"][u], 16)

                @block.gpsimd
                def _(pool):
                    with pool.Fori(0, NS // 2) as t:
                        for u in range(2):
                            hold(pool, (S["idx"][u], t * 16 + 16), (S["scaled"], freed2(t, u, 1)))
                            for q in range(2 * QJ):
                                nc.gpsimd.indirect_dma_start(
                                    out=G[:, u, q, :], out_offset=None, in_=tin[:, :],
                                    in_offset=bass.IndirectOffsetOnAxis(ap=I[:, u, q:q + 1], axis=0),
                                ).then_inc(S["got"][u], 16)

                @block.vector
                def _(dve):
                    nc.vector.memset(ST[:, 1, SUP - 1:SUP], 0.0)
                    with dve.Fori(0, NS // 2) as t:
                        for u in range(2):
                            q0 = (2 * t + u) * 2 * QJ
                            for h in range(2):
                                q = slice(h * QJ, (h + 1) * QJ)
                                hold(dve, (S["got"][u], t * (32 * QJ) + 32 * QJ), (S["flipped"], freed1(t, u, h)))
                                nc.vector.tensor_tensor(
                                    M[:, q, :], G[:, u, q, :],
                                    a_src[:, bass.DynSlice(q0 + h * QJ, QJ)].unsqueeze(2).to_broadcast([P, QJ, D]),
                                    ALU.mult).then_inc(S["scaled"], 1)
                            for h in range(2):
                                q = slice(h * QJ, (h + 1) * QJ)
                                hold(dve, (S["scaled"], made(t, u, h)))
                                nc.vector.tensor_tensor(M[:, q, :], M[:, q, :], B_res[:, bass.DynSlice(q0 + h * QJ, QJ), :],
                                                        ALU.add).then_inc(S["added"], 1)
                            for h in range(2):
                                before_ = ST[:, u, HALF - 1:HALF] if h else ST[:, 1 - u, SUP - 1:SUP]
                                hold(dve, (S["mask"][u], t * 16 + 16), (S["flipped"], made(t, u, h)),
                                     (S["scanned"], made(t, u, h) - 1), (S["back"], freed2(t, u, h)),
                                     *([(S["keptT"][u], kept_at(t))] if keepT is not None else []))
                                nc.vector.tensor_tensor_scan(
                                    out=ST[:, u, h * HALF:(h + 1) * HALF], data0=K[:, u, h * HALF:(h + 1) * HALF],
                                    data1=psT[h][0:D, :], initial=before_, op0=ALU.mult, op1=ALU.add
                                ).then_inc(S["scanned"], 1)

                @block.tensor
                def _(pe):
                    with pe.Fori(0, NS // 2) as t:
                        for u in range(2):
                            for h in range(2):
                                hold(pe, (S["added"], made(t, u, h)), (S["scanned"], freed1(t, u, h)))
                                for j in range(QJ):
                                    last = nc.tensor.transpose(psT[h][0:D, :].rearrange("f (p j) -> f j p", j=QJ)[:, j, :],
                                                               M[:, h * QJ + j, :], ident[:])
                                last.then_inc(S["flipped"], 1)
                            for h in range(2):
                                hold(pe, (S["scanned"], made(t, u, h)), (S["read"], freed1(t, u, h)))
                                for j in range(QJ):
                                    last = nc.tensor.transpose(
                                        psB[h][:, j * D:(j + 1) * D],
                                        ST[:, u, h * HALF:(h + 1) * HALF].rearrange("f (p j) -> f j p", j=QJ)[:, j, :],
                                        ident[0:D, 0:D])
                                last.then_inc(S["back"], 1)

                @block.scalar
                def _(act):
                    with act.Fori(0, NS // 2) as t:
                        for u in range(2):
                            for h in range(2):
                                hold(act, (S["back"], made(t, u, h)), (S["kept"][u], kept_at(t)))
                                nc.scalar.copy(SR[:, u, h * QJ:(h + 1) * QJ, :],
                                               psB[h][:, 0:QJ * D].rearrange("p (j d) -> p j d", d=D)).then_inc(S["read"], 1)
                            hold(act, (S["read"], made(t, u, 1)))
                            act.dma_start(tab_rows(tout, 2 * t + u),
                                          SR[:, u].rearrange("p (h j) d -> p h (j d)", h=2)).then_inc(S["kept"][u], 16)
                            if keepT is not None:
                                act.dma_start(sup(keepT, 2 * t + u), ST[:, u, :]).then_inc(S["keptT"][u], 16)
                    for u in range(2):
                        act.wait_ge(S["kept"][u], kept_at(NS // 2))
                        if keepT is not None:
                            act.wait_ge(S["keptT"][u], kept_at(NS // 2))

        def node_pass(kind, direction, tab_in=None, tab_out=None, tot_in=None, tot_out=None,
                      x_in=None, x_out=None, skip=None, layer=0, B_res=None):
            gather = tab_in is not None
            norm = kind in ("gcn2", "appnp_end", "attend", "finish")
            message = kind in ("appnp_end", "update")
            attention = kind in ("attend", "finish")
            scaled = kind in ("first", "gcn1", "gcn2", "appnp_end")
            idx_all = idx_src_gl if direction == "R" else idx_src_gf
            hs = halves(direction)
            z = hs[1]
            units = [(u, h) for u in range(2) for h in hs]
            wide = slice(0, P) if attention else slice(D, P)
            low = slice(0, P) if kind == "finish" else slice(0, D)
            counts = ["carry_ok", "scanned"]
            counts += ["at_zero"] if message else []
            counts += ["flipped", "agg_s"] if gather else []
            counts += ["masked", "agg_d"] if kind != "first" else []
            counts += {"first": ["v"],
                       "gcn1": ["u1", "u", "mm", "relu", "v"],
                       "gcn2": ["u1", "u", "mm", "relu", "y", "msg", "b_flip", "b_read"],
                       "appnp_end": ["u1", "y", "msg_mm", "msg"],
                       "update": ["mm", "x", "msg_mm", "msg"],
                       "attend": ["mm", "relu", "y", "msg_mm", "msg"],
                       "finish": ["msg_mm", "msg", "diff", "ex", "wx", "summed", "lden", "rden", "nf", "mm", "y"],
                       }[kind]
            counts += ["cent", "sq", "var", "ln", "rs", "x"] if norm else []
            counts += ["back", "read"] if kind != "attend" else []
            dmas = ["maskw", "state"]
            dmas += ["idx", "got"] if gather else []
            dmas += ["maskl", "tot"] if kind != "first" else []
            dmas += ["row"] if scaled else []
            dmas += ["nsrc"] if kind == "gcn2" else []
            dmas += ["skipped"] if skip else []
            dmas += ["attr"] if message else []
            dmas += ["oidx"] if kind == "finish" else []
            stores = ["xkept"] if x_out else []
            stores += ["kept"] if tab_out is not None else []
            stores += ["scat"] if kind == "finish" else []
            stores += ["totkept"] if tot_out is not None else []
            with stage(counts, dmas, stores) as (block, S, sbt, pst):
                two = lambda n, dt=f32: sbt(n, [P, 2, SUP], dt)
                KW = two("KW", bf16)
                KL = two("KL", bf16) if attention else KW
                X, XO, ST = two("X"), two("XO"), two("ST")
                Y, H = two("Y"), two("H")
                TOT, MS, AG = (two("TOT"), Y, two("AG")) if kind != "first" else (None, None, None)
                if gather:
                    I = sbt("I", [P, 2, 2 * QJ], i32)
                    G = sbt("G", [P, 2, 2 * QJ, P])
                if skip:
                    XS = two("XS")
                if scaled:
                    R = two("R")
                if kind == "gcn2":
                    NSR = TOT
                if message:
                    AT = two("AT")
                if kind == "finish":
                    NUM = two("NUM")
                    IO = sbt("IO", [P, 2, 2 * QJ], i32)
                MG = H if kind == "gcn2" else two("MG") if message or attention else None
                WX = MG
                SR = sbt("SR", [P, 2, 2 * QJ, D])
                psT, psM = ([[pst(f"{n}{u}{h}") for h in range(2)] for u in range(2)] for n in ("psT", "psM"))
                end = HALF - 1 if direction == "F" else 0

                def cols(h):
                    return slice(h * HALF, (h + 1) * HALF)

                def at(tile, part=slice(0, P)):
                    return lambda u, h: tile[part, u, cols(h)]

                def bank(ps):
                    return lambda u, h: ps[u][h][:]

                def md(t, u, h):
                    return made(t, u, hs.index(h))

                def fr(t, u, h):
                    return freed2(t, u, hs.index(h))

                def along(ap):
                    return ap if direction == "F" else ap[:, ::-1]

                x_used = {"first": "v", "gcn1": "u1", "gcn2": "u1", "appnp_end": "y", "update": "mm",
                          "attend": "mm", "finish": "y"}[kind]
                ag_used = {"gcn1": "u1", "gcn2": "u1", "appnp_end": "u1", "update": "mm", "attend": "mm",
                           "finish": "diff", "first": None}[kind]
                y_used = "mm" if kind == "gcn1" else "agg_d" if kind == "update" else "var"

                @block.sync
                def _(sp):
                    if message:
                        sp.wait_ge(S["at_zero"], 1 + CREDIT)

                    def load(t, name, free, dst_of, src_of):
                        for u in range(2):
                            hold(sp, (S[free], fr(t, u, z)))
                            sp.dma_start(dst_of(u), src_of(order(direction, t, u))).then_inc(S[name][u], 16)

                    with sp.Fori(0, NS // 2) as t:
                        if gather:
                            load(t, "idx", "flipped", lambda u: I[:, u, :],
                                 lambda n: idx_all[:, bass.DynSlice(n * (2 * QJ), 2 * QJ)])
                        if kind != "first":
                            load(t, "maskl", "agg_d", lambda u: KL[low, u, :],
                                 lambda n: spread(mask_dram[direction], n, low.stop - low.start))
                            load(t, "tot", "masked", lambda u: TOT[low, u, :],
                                 lambda n: sup(maxT if kind == "finish" else totT[tot_in], n))
                        load(t, "state", x_used, lambda u: X[:, u, :], lambda n: sup(st[x_in], n))
                        if scaled:
                            r = "ndst" if kind == "appnp_end" else "dis"
                            used = {"first": "v", "gcn1": "v", "gcn2": "u", "appnp_end": "u1"}[kind]
                            load(t, "row", used, lambda u: R[0:D, u, :], lambda n: spread(rows[r + "_d"], n, D))
                            load(t, "row", used, lambda u: R[D:P, u, :], lambda n: spread(rows[r + "_s"], n, D))
                        if skip:
                            load(t, "skipped", "y", lambda u: XS[:, u, :], lambda n: sup(st[skip], n))
                        if kind == "gcn2":
                            load(t, "nsrc", "msg", lambda u: NSR[D:P, u, :], lambda n: spread(rows["nsrc_s"], n, D))
                        if message:
                            load(t, "attr", "msg_mm", lambda u: AT[0:EDGE_DIM, u, :], lambda n: sup(attrT, n))
                        load(t, "maskw", "summed" if kind == "finish" else "scanned", lambda u: KW[wide, u, :],
                             lambda n: spread(mask_dram[direction], n, wide.stop - wide.start))
                        if kind == "finish":
                            for u in range(2):
                                n = order(direction, t, u)
                                hold(sp, (S["scat"][u], t * (32 * QJ) + 16))
                                sp.dma_start(IO[:, u, :], idx_out[:, bass.DynSlice(n * (2 * QJ), 2 * QJ)]
                                             ).then_inc(S["oidx"][u], 16)

                @block.gpsimd
                def _(pool):
                    if message:
                        nc.gpsimd.memset(AT[:], 0.0).then_inc(S["at_zero"], 1)
                    if gather:
                        nc.gpsimd.memset(G[:], 0.0).then_inc(S["flipped"], 1)
                        pool.wait_ge(S["flipped"], 1 + CREDIT)
                        with pool.Fori(0, NS // 2) as t:
                            for u in range(2):
                                hold(pool, (S["idx"][u], t * 16 + 16), (S["flipped"], freed2(t, u, 1) + 1))
                                for q in range(2 * QJ):
                                    nc.gpsimd.indirect_dma_start(
                                        out=G[:, u, q, D:P], out_offset=None, in_=tab[tab_in][:, :],
                                        in_offset=bass.IndirectOffsetOnAxis(ap=I[:, u, q:q + 1], axis=0),
                                    ).then_inc(S["got"][u], 16)
                    if kind == "finish":
                        top = pool.to_reg(N_NODES - 1)
                        with pool.Fori(0, NS // 2) as t:
                            for u in range(2):
                                hold(pool, (S["read"], made(t, u, 1)), (S["oidx"][u], t * 16 + 16))
                                for q in range(2 * QJ):
                                    nc.gpsimd.indirect_dma_start(
                                        out=out[:, :], out_offset=bass.IndirectOffsetOnAxis(ap=IO[:, u, q:q + 1], axis=0),
                                        in_=SR[:, u, q, :], in_offset=None,
                                        bounds_check=top, oob_is_err=False).then_inc(S["scat"][u], 16)
                        for u in range(2):
                            pool.wait_ge(S["scat"][u], 32 * QJ * (NS // 2) + 16)

                @block.tensor
                def _(pe):
                    with pe.Fori(0, NS // 2) as t:
                        def mm(name, ps, terms, needs, frees=(), landed=()):
                            for u, h in units:
                                hold(pe, *[(S[a], md(t, u, h)) for a in needs], *[(S[a], fr(t, u, h)) for a in frees],
                                     *[(S[a][u], t * 16 + 16) for a in landed])
                                for i, (w, r) in enumerate(terms):
                                    last = nc.tensor.matmul(ps[u][h][:], w, r(u, h), start=(i == 0), stop=(i == len(terms) - 1))
                                last.then_inc(S[name], 1)

                        if gather:
                            tail = {"gcn2": "b_read", "gcn1": "agg_s"}.get(kind, "msg")
                            for u, h in units:
                                hold(pe, (S["got"][u], t * (32 * QJ) + 32 * QJ), (S[tail], fr(t, u, h)))
                                for j in range(QJ):
                                    last = nc.tensor.transpose(psT[u][h][:].rearrange("f (p j) -> f j p", j=QJ)[:, j, :],
                                                               G[:, u, h * QJ + j, :], ident[:])
                                last.then_inc(S["flipped"], 1)
                        if kind == "gcn1":
                            mm("mm", psM, [(W1b[:], at(Y))], ["u"], ["read"])
                        if kind == "gcn2":
                            mm("mm", psM, [(W2b[:], at(Y))], ["u"], ["read"])
                        if kind in ("update", "attend"):
                            mm("mm", psM, [(Wu1[:, layer, :], at(X)), (Wu2[:, layer, :], at(AG))],
                               ["agg_d", "agg_s"], ["read" if kind == "update" else "x"], ["state"])
                        if kind == "finish":
                            mm("msg_mm", psT, [(WlT[:], at(X))], [], ["ln"], ["state"])
                            mm("mm", psM, [(WoT[:], at(H))], ["nf"], ["read"])
                        if norm:
                            mm("cent", psM, [(center[:], at(Y))], ["y"], ["read"] if kind == "appnp_end" else [])
                            mm("var", psT, [(avg[:], at(Y))], ["sq"])
                        if kind == "gcn2":
                            for u, h in units:
                                hold(pe, (S["msg"], md(t, u, h)))
                                for j in range(QJ):
                                    last = nc.tensor.transpose(
                                        psT[u][h][:, j * D:(j + 1) * D],
                                        MG[D:P, u, cols(h)].rearrange("f (p j) -> f j p", j=QJ)[:, j, :], ident[D:P, D:P])
                                last.then_inc(S["b_flip"], 1)
                        if message:
                            nxt = 0 if kind == "appnp_end" else layer + 1
                            mm("msg_mm", psT, [(Wm[:, nxt, :], at(XO)), (We[:, nxt, :], at(AT))], ["x"], [], ["attr"])
                        if kind == "attend":
                            mm("msg_mm", psT, [(WlT[:], at(XO))], ["x"])
                        if kind != "attend":
                            part, what = ((slice(0, D), "x") if kind == "finish" else (slice(D, P), "scanned"))
                            tile = XO if kind == "finish" else ST
                            for u, h in units:
                                hold(pe, (S[what], md(t, u, h)), *([(S["read"], fr(t, u, h))] if kind == "first" else []))
                                for j in range(QJ):
                                    last = nc.tensor.transpose(
                                        psM[u][h][:, j * D:(j + 1) * D],
                                        tile[part, u, cols(h)].rearrange("f (p j) -> f j p", j=QJ)[:, j, :],
                                        ident[part, part])
                                last.then_inc(S["back"], 1)

                @block.scalar
                def _(act):
                    with act.Fori(0, NS // 2) as t:
                        def ac(name, o, i, func, b, needs, frees=(), store=None, scale=1.0):
                            for u, h in units:
                                hold(act, *[(S[a], md(t, u, h)) for a in needs], *[(S[a], fr(t, u, h)) for a in frees],
                                     *([(S[store][u], kept_at(t))] if store else []))
                                nc.scalar.activation(o(u, h), i(u, h), func, bias=bias[:, b:b + 1], scale=scale
                                                     ).then_inc(S[name], 1)

                        if gather:
                            for u, h in units:
                                hold(act, (S["flipped"], md(t, u, h) + 1), (S[ag_used], fr(t, u, h)))
                                nc.scalar.copy(AG[D:P, u, cols(h)], psT[u][h][D:P, :]).then_inc(S["agg_s"], 1)
                        if kind == "gcn1":
                            ac("relu", at(H), bank(psM), ACT.Relu, B1, ["mm"], ["v"])
                        if kind == "gcn2":
                            ac("relu", at(H), bank(psM), ACT.Relu, B2, ["mm"], ["b_flip", "scanned"])
                        if kind == "update":
                            ac("x", at(XO), bank(psM), ACT.Relu, BU + layer, ["mm"], ["msg_mm"], "xkept")
                        if kind == "attend":
                            ac("relu", at(H), bank(psM), ACT.Relu, BU + layer, ["mm"], ["x"])
                        if kind == "finish":
                            ac("msg", at(MG), bank(psT), ACT.Relu, BL, ["msg_mm"], ["nf"])
                            ac("ex", at(H), at(Y), ACT.Exp, BZ, ["diff"], ["x"])
                            ac("lden", at(WX), at(ST), ACT.Ln, BZ, ["scanned", "summed"])
                            ac("rden", at(WX), at(WX), ACT.Exp, BZ, ["lden"], scale=-1.0)
                        if norm:
                            ac("sq", at(Y), bank(psM), ACT.Square, BZ, ["cent"])
                            ac("ln", at(H), bank(psT), ACT.Ln, BEPS, ["var"], ["x"] if kind == "appnp_end" else [])
                            ac("rs", at(H), at(H), ACT.Exp, BZ, ["ln"], scale=-0.5)
                        if kind == "gcn2":
                            for u, h in units:
                                n = order(direction, t, u)
                                hold(act, (S["b_flip"], md(t, u, h)))
                                nc.scalar.mul(B_res[:, bass.DynSlice(n * (2 * QJ) + h * QJ, QJ), :],
                                              psT[u][h][:, 0:QJ * D].rearrange("p (j d) -> p j d", d=D), ALPHA
                                              ).then_inc(S["b_read"], 1)
                        if message:
                            nxt = 0 if kind == "appnp_end" else layer + 1
                            ac("msg", at(MG), bank(psT), ACT.Relu, BM + nxt, ["msg_mm"], ["scanned"])
                        if kind == "attend":
                            ac("msg", at(MG), bank(psT), ACT.Relu, BL, ["msg_mm"], ["scanned"])
                        if kind != "attend":
                            for u, h in units:
                                free = ((S["scat"][u], t * (32 * QJ) + 16) if kind == "finish" else
                                        (S["kept"][u], kept_at(t)))
                                hold(act, (S["back"], md(t, u, h)), free)
                                nc.scalar.copy(SR[:, u, h * QJ:(h + 1) * QJ, :],
                                               psM[u][h][:, 0:QJ * D].rearrange("p (j d) -> p j d", d=D)).then_inc(S["read"], 1)
                        for u in range(2):
                            n = order(direction, t, u)
                            if x_out:
                                made_by = "v" if kind in ("first", "gcn1") else "x"
                                hold(act, (S[made_by], md(t, u, z)))
                                act.dma_start(sup(st[x_out], n), XO[:, u, :]).then_inc(S["xkept"][u], 16)
                            if tot_out is not None:
                                hold(act, (S["scanned"], md(t, u, z)))
                                act.dma_start(sup(maxT if kind == "attend" else totT[tot_out], n), ST[wide, u, :]
                                              ).then_inc(S["totkept"][u], 16)
                            if tab_out is not None:
                                hold(act, (S["read"], md(t, u, z)))
                                act.dma_start(tab_rows(tab[tab_out], n),
                                              SR[:, u].rearrange("p (h j) d -> p h (j d)", h=2)).then_inc(S["kept"][u], 16)
                    for c in stores:
                        if c != "scat":
                            for u in range(2):
                                act.wait_ge(S[c][u], kept_at(NS // 2))

                @block.vector
                def _(dve):
                    first_cols = slice(z * HALF + end, z * HALF + end + 1)
                    for tile in [ST] + ([NUM] if kind == "finish" else []) + ([AG[low]] if kind != "first" else []):
                        last = nc.vector.memset(tile[:, 1, first_cols], 0.0)
                    last.then_inc(S["carry_ok"], 1)
                    dve.wait_ge(S["carry_ok"], 1 + CREDIT)
                    with dve.Fori(0, NS // 2) as t:
                        def ve(name, fn, needs, frees=(), loads=(), store=None):
                            for u, h in units:
                                hold(dve, *[(S[a], md(t, u, h)) for a in needs], *[(S[a], fr(t, u, h)) for a in frees],
                                     *[landed(a, u) for a in loads], *([(S[store][u], kept_at(t))] if store else []))
                                fn(u, h).then_inc(S[name], 1)

                        def landed(name, u):
                            return (S[name][u], t * 32 + 32 if name == "row" else t * 16 + 16)

                        def stt(o, a, sc, b, op0, op1):
                            return lambda u, h: nc.vector.scalar_tensor_tensor(
                                out=o(u, h), in0=a(u, h), scalar=sc, in1=b(u, h), op0=op0, op1=op1)

                        def tt(o, a, b, op):
                            return lambda u, h: nc.vector.tensor_tensor(o(u, h), a(u, h), b(u, h), op)

                        def scan(name, out_, part, mask, data, op1, needs, frees=(), loads=(), store=None):
                            for u, h in units:
                                pu, ph = (u, 1 - h) if h == z else (1 - u, z)
                                carry = out_[part, pu, ph * HALF + end:ph * HALF + end + 1]
                                hold(dve, *[(S[a], md(t, u, h)) for a in needs], (S[name], md(t, u, h) - 1),
                                     *[(S[a], fr(t, u, h)) for a in frees], *[landed(a, u) for a in loads],
                                     *([(S[store][u], kept_at(t))] if store else []))
                                nc.vector.tensor_tensor_scan(
                                    out=along(out_[part, u, cols(h)]), data0=along(mask[part, u, cols(h)]),
                                    data1=along(data(u, h)), initial=carry, op0=ALU.mult, op1=op1).then_inc(S[name], 1)

                        if kind != "first":
                            ve("masked", stt(at(MS, low), at(KL, low), 0.0, at(TOT, low), ALU.is_equal, ALU.mult),
                               [], [y_used], ["maskl", "tot"])
                            scan("agg_d", AG, low, KL, at(MS, low), ALU.add, ["masked"], [ag_used])
                        if kind == "first":
                            ve("v", tt(at(XO), at(X), at(R), ALU.mult), [], [], ["state", "row"], "xkept")
                        if kind in ("gcn1", "gcn2"):
                            ve("u1", tt(at(Y), at(AG), at(X), ALU.add), ["agg_d", "agg_s"], [], ["state"])
                            ve("u", tt(at(Y), at(Y), at(R), ALU.mult), ["u1"], [], ["row"])
                        if kind == "gcn1":
                            ve("v", tt(at(XO), at(H), at(R), ALU.mult), ["relu"], [], [], "xkept")
                        if kind == "gcn2":
                            ve("y", stt(at(Y), at(XS), 2.0, at(H), ALU.mult, ALU.add), ["relu"], [], ["skipped"])
                        if kind == "appnp_end":
                            ve("u1", stt(at(Y), at(AG), 1.0 - ALPHA, at(R), ALU.mult, ALU.mult), ["agg_d", "agg_s"], [], ["row"])
                            ve("y", stt(at(Y), at(X), 1.0 + ALPHA, at(Y), ALU.mult, ALU.add), ["u1"], [], ["state"])
                        if kind == "attend":
                            ve("y", tt(at(Y), at(XS), at(H), ALU.add), ["relu"], [], ["skipped"])
                        if kind == "finish":
                            ve("diff", tt(at(Y), at(MG), at(AG), ALU.subtract), ["msg", "agg_d"])
                            ve("wx", tt(at(WX), at(H), at(X), ALU.mult), ["ex"], [], ["state"])
                            scan("scanned", ST, wide, KW, at(H), ALU.add, ["ex"], [], ["maskw"])
                            scan("summed", NUM, wide, KW, at(WX), ALU.add, ["wx"], [], ["maskw"])
                            ve("nf", tt(at(H), at(NUM), at(WX), ALU.mult), ["rden"])
                            ve("y", lambda u, h: nc.vector.scalar_tensor_tensor(
                                out=Y[:, u, cols(h)], in0=psM[u][h][:], scalar=bias[:, BO:BO + 1], in1=X[:, u, cols(h)],
                                op0=ALU.add, op1=ALU.add), ["mm"])
                        if norm:
                            ve("x", tt(at(XO), bank(psM), at(H), ALU.mult), ["rs"],
                               ["msg_mm"] if kind in ("appnp_end", "attend") else ["back"] if kind == "finish" else [], [],
                               "xkept" if x_out else None)
                        if kind == "gcn2":
                            ve("msg", tt(at(MG, wide), at(XO, wide), at(NSR, wide), ALU.mult), ["x"], [], ["nsrc"])
                        if kind != "finish":
                            data, need = (at(XO, wide), "v") if kind in ("first", "gcn1") else (at(MG, wide), "msg")
                            scan("scanned", ST, wide, KW, data, ALU.max if kind == "attend" else ALU.add, [need],
                                 ["back"] if kind != "attend" else [], ["maskw"], "totkept" if tot_out is not None else None)

        node_pass("first", "F", tab_out=0, tot_out=0, x_in="X0", x_out="V0")
        node_pass("gcn1", "R", 0, 1, 0, 1, "V0", "V1")
        with nc.sbuf_tensor("B_res", [P, NQ, D], f32) as B_res:
            node_pass("gcn2", "F", 1, 0, 1, None, "V1", "X1", skip="X0", B_res=B_res)
            assert APPNP_STEPS % 2 == 0 and APPNP_STEPS >= 4
            with nc.Fori(0, APPNP_STEPS // 2 - 1):
                appnp_pass(B_res, 0, 1)
                appnp_pass(B_res, 1, 0)
            appnp_pass(B_res, 0, 1, totT[0])
        node_pass("appnp_end", "R", 1, 0, 0, 1, "X1", "X2")
        node_pass("update", "F", 0, 1, 1, 0, "X2", "XA", layer=0)
        node_pass("update", "R", 1, 0, 0, 1, "XA", "XB", layer=1)
        node_pass("attend", "F", 0, None, 1, 0, "XB", "X3", skip="X2", layer=2)
        node_pass("finish", "R", None, None, 0, None, "X3")


_INS = ["x", "src", "dst", "edge_attr_16", "L0_gnn_W1", "L0_gnn_b1", "L0_gnn_W2", "L0_gnn_b2",
        "L2_gnn_msg_w", "L2_gnn_msg_b", "L2_gnn_upd_w", "L2_gnn_upd_b",
        "L3_gnn_W_lin", "L3_gnn_b_lin", "L3_gnn_W_out", "L3_gnn_b_out"]


def kernel(**inputs):
    import numpy as _np
    import concourse.bacc as _bacc
    from concourse.bass_utils import run_bass_kernel_spmd as _run

    nc = _bacc.Bacc("TRN2", target_bir_lowering=False, num_devices=1)
    arrays, args = {}, []
    for name in _INS:
        a = _np.ascontiguousarray(inputs[name])
        arrays[f"in_{name}"] = a
        args.append(nc.dram_tensor(f"in_{name}", a.shape, mybir.dt.from_np(a.dtype), kind="ExternalInput").ap())
    args.append(nc.dram_tensor("out_y", (N_NODES, D), mybir.dt.float32, kind="ExternalOutput").ap())
    build(nc, *args)
    r = _run(nc, [arrays], core_ids=[0])
    return r.results[0]["out_y"]
```

```python
import concourse.bass as bass
from concourse import mybir
from contextlib import ExitStack, contextmanager

N_NODES = 100000
N_EDGES = 50000
D = 64
EDGE_DIM = 16
APPNP_STEPS = 10
ALPHA = 0.1
EPS = 1e-5

P = 128
SUP = 1024
HALF = 512
QJ = HALF // P
NS = -(-N_EDGES // (2 * SUP)) * 2
EP = NS * SUP
NQ = EP // P
LO = 1024
HI = -(-N_NODES // LO)
PAD_NODE = HI * LO - 1
CREDIT = 4


def build(nc, x, src, dst, edge_attr, W1, b1, W2, b2, msg_w, msg_b, upd_w, upd_b,
          W_lin, b_lin, W_out, b_out, out):
    f32, f16, bf16, i32 = (mybir.dt.float32, mybir.dt.float16, mybir.dt.bfloat16, mybir.dt.int32)
    ALU = mybir.AluOpType
    ACT = mybir.ActivationFunctionType
    assert PAD_NODE >= N_NODES

    ctx = ExitStack()

    def sb(name, shape, dt=f32):
        return ctx.enter_context(nc.sbuf_tensor(name, shape, dt))

    def dram(name, shape, dt=f32):
        return nc.dram_tensor(name, shape, dt).ap()

    src_pad = dram("src_pad", [EP], i32)
    dst_pad = dram("dst_pad", [EP + 2], i32)
    attr_pad = dram("attr_pad", [EP, EDGE_DIM])
    node_table = dram("node_table", [P * LO, 8])
    tab = [dram(f"tab{i}", [EP + P, D]) for i in range(2)]
    totT = [dram(f"totT{i}", [NS, D, SUP]) for i in range(2)]
    maxT = dram("maxT", [NS, P, SUP])
    mask_dram = {d: dram(f"mask{d}", [NS, SUP], bf16) for d in "FR"}
    row_names = ["dis_d", "dis_s", "nsrc_s", "ndst_d", "ndst_s"]
    rows = {r: dram(f"row_{r}", [NS, SUP]) for r in row_names}
    st = {n: dram(f"state_{n}", [NS, P, SUP]) for n in ("X0", "V1", "X1", "X2", "XA", "XB", "X3")}
    primer = dram("primer", [8, 16])
    attrT = dram("attrT", [NS, EDGE_DIM, SUP])

    ident = sb("ident", [P, P])
    avg = sb("avg", [P, P])
    center = sb("center", [P, P])
    before = sb("before", [P, P])
    W1b, W2b = sb("W1b", [P, P]), sb("W2b", [P, P])
    Wm = sb("Wm", [P, 3, P])
    We = sb("We", [P, 3, P])
    Wu1, Wu2 = sb("Wu1", [P, 3, P]), sb("Wu2", [P, 3, P])
    Wl_raw, Wo_raw = sb("Wl_raw", [P, P]), sb("Wo_raw", [P, P])
    WlT = sb("WlT", [P, P])
    bias = sb("bias", [P, 14])
    B1, B2, BL, BO, BEPS, BZ, BM, BU, BC, BEPS2 = 0, 1, 2, 3, 4, 5, 6, 9, 12, 13
    WoC = sb("WoC", [P, P])
    idx_src_gl = sb("idx_src_gl", [P, NQ], i32)
    idx_src_gf = sb("idx_src_gf", [P, NQ], i32)
    idx_out = sb("idx_out", [P, NQ], i32)
    a_src = sb("a_src", [P, NQ])

    begun = ctx.enter_context(nc.semaphore("begun"))
    pass_no = [0]
    wait_regs = {}
    swdge = {c: [ctx.enter_context(nc.semaphore(f"{c}{u}")) for u in range(2)] for c in ("got", "scat")}

    def hold(eng, *waits):
        values = []
        for i, (_, v) in enumerate(waits):
            if not isinstance(v, int):
                reg = wait_regs.get((eng.engine, i))
                if reg is None:
                    reg = wait_regs[eng.engine, i] = eng.alloc_register(f"wait_value{i}")
                eng.reg_mov(reg, v)
                v = reg
            values.append(v)
        eng.wait_ge(begun, 1)
        for (s, _), v in zip(waits, values):
            eng.wait_ge(s, v)

    def kept_at(t):
        return t * 16 + 16

    @contextmanager
    def stage(counts, dmas=(), stores=()):
        n = pass_no[0]
        pass_no[0] += 1
        with ExitStack() as s:
            sems = {c: s.enter_context(nc.semaphore(f"{c}_{n}")) for c in counts}
            for c in dmas:
                sems[c] = swdge[c] if c in swdge else [s.enter_context(nc.semaphore(f"{c}{u}_{n}")) for u in range(2)]
            for k, c in enumerate(stores):
                sems[c] = swdge[c] if c in swdge else [s.enter_context(nc.semaphore(f"{c}{u}_{n}")) for u in range(2)]
                for u in range(2):
                    (nc.gpsimd if c in swdge else nc.sync).dma_start(
                        primer[2 * k + u:2 * k + u + 1, :], ident[0:1, 0:16]).then_inc(sems[c][u], 16)
            for c in counts:
                nc.gpsimd.sem_inc(sems[c], CREDIT)
            nc.all_engine_barrier()
            with ExitStack() as bufs:
                with nc.Block() as block:
                    yield block, sems, lambda name, shape, dt=f32: bufs.enter_context(
                        nc.sbuf_tensor(f"{name}_{n}", shape, dt)), lambda name, shape=[P, HALF]: bufs.enter_context(
                        nc.psum_tensor(f"{name}_{n}", shape, f32))
            nc.all_engine_barrier()
            for c, own in swdge.items():
                if c in sems:
                    nc.gpsimd.dma_reset(range(own[0].num, own[1].num + 1))
            for c in sems.values():
                for one in (c if isinstance(c, list) else [c]):
                    nc.gpsimd.sem_clear(one)

    def made(t, u, h):
        return 4 * t + 2 * u + h + 1 + CREDIT

    def freed1(t, u, h):
        return 4 * t + 2 * u + h - 1 + CREDIT

    def freed2(t, u, h):
        return 4 * t + 2 * u + h - 3 + CREDIT

    with ctx:
        with ExitStack() as s:
            prep = s.enter_context(nc.semaphore("prep"))
            loaded = s.enter_context(nc.semaphore("loaded"))
            built = s.enter_context(nc.semaphore("built"))
            shaped = s.enter_context(nc.semaphore("shaped"))
            flipped = s.enter_context(nc.semaphore("flipped"))
            kept = s.enter_context(nc.semaphore("kept"))
            padi = s.enter_context(nc.sbuf_tensor("padi", [16, (EP - N_EDGES) // 16], i32))
            sentinel = s.enter_context(nc.sbuf_tensor("sentinel", [1, 2], i32))
            zeros = s.enter_context(nc.sbuf_tensor("zeros", [P, (EP - N_EDGES) * EDGE_DIM // 16], f32))
            ps = s.enter_context(nc.psum_tensor("ps_prep", [P, 2, HALF], f32))
            nw = [0]

            def load(dstap, srcap):
                nc.sync.dma_start(dstap, srcap).then_inc(loaded, 16)
                nw[0] += 1

            with nc.Block() as block:
                @block.vector
                def _(dve):
                    nc.vector.memset(padi[:], PAD_NODE)
                    nc.vector.memset(sentinel[:], -1)
                    for w in (zeros, W1b, W2b, Wm, We, Wu1, Wu2, Wl_raw, Wo_raw, bias, avg, ident):
                        nc.vector.memset(w[:], 0.0)
                    nc.vector.memset(before[:], 1.0).then_inc(prep, 1)
                    dve.wait_ge(prep, 1)
                    nc.vector.memset(bias[:, BEPS:BEPS + 1], EPS)
                    nc.vector.memset(bias[:, BEPS2:BEPS2 + 1], EPS * EPS)
                    nc.vector.memset(avg[0:D, 0:D], 1.0 / D)
                    nc.vector.memset(avg[D:P, D:P], 1.0 / D).then_inc(prep, 1)
                    dve.wait_ge(shaped, 2)
                    nc.vector.tensor_tensor(center[:], ident[:], avg[:], ALU.subtract).then_inc(built, 1)
                    dve.wait_ge(flipped, 1)
                    nc.vector.tensor_copy(WlT[:], ps[:, 0, 0:P]).then_inc(built, 1)
                    dve.wait_ge(flipped, 3)
                    nc.vector.tensor_copy(bias[:, BC:BC + 1], ps[:, 0, 0:1])
                    nc.vector.tensor_copy(WoC[:], ps[:, 1, 0:P]).then_inc(built, 1)

                @block.gpsimd
                def _(pool):
                    pool.wait_ge(prep, 2)
                    nc.gpsimd.affine_select(out=ident[:], in_=ident[:], compare_op=ALU.not_equal, fill=1.0,
                                            base=0, pattern=[[1, P]], channel_multiplier=-1).then_inc(shaped, 1)
                    pool.wait_ge(shaped, 1)
                    nc.gpsimd.affine_select(out=before[:], in_=before[:], compare_op=ALU.is_gt, fill=0.0,
                                            base=0, pattern=[[1, P]], channel_multiplier=-1).then_inc(shaped, 1)

                @block.sync
                def _(sp):
                    sp.wait_ge(prep, 2)
                    for k in range(2):
                        o = k * D
                        load(W1b[o:o + D, o:o + D], W1)
                        load(W2b[o:o + D, o:o + D], W2)
                        load(bias[o:o + D, B1:B1 + 1], b1.rearrange("(d a) -> d a", a=1))
                        load(bias[o:o + D, B2:B2 + 1], b2.rearrange("(d a) -> d a", a=1))
                        load(bias[o:o + D, BO:BO + 1], b_out.rearrange("(d a) -> d a", a=1))
                        r = D - o
                        load(bias[o:o + D, BL:BL + 1], b_lin[r:r + D].rearrange("(d a) -> d a", a=1))
                        load(Wo_raw[0:D, o:o + D], W_out[:, r:r + D])
                        for k2 in range(2):
                            load(Wl_raw[o:o + D, k2 * D:k2 * D + D], W_lin[r:r + D, D - k2 * D:2 * D - k2 * D])
                        for l in range(3):
                            load(Wu1[o:o + D, l, o:o + D], upd_w[l, 0:D, :])
                            load(Wu2[o:o + D, l, o:o + D], upd_w[l, D:2 * D, :])
                            load(bias[o:o + D, BU + l:BU + l + 1], upd_b[l].rearrange("(d a) -> d a", a=1))
                    for l in range(3):
                        load(Wm[:, l, D:P], msg_w[l, 0:2 * D, :])
                        load(We[0:EDGE_DIM, l, D:P], msg_w[l, 2 * D:2 * D + EDGE_DIM, :])
                        load(bias[D:P, BM + l:BM + l + 1], msg_b[l].rearrange("(d a) -> d a", a=1))
                    load(src_pad[0:N_EDGES].rearrange("(a b) -> a b", a=16), src.rearrange("(a b) -> a b", a=16))
                    load(src_pad[N_EDGES:EP].rearrange("(a b) -> a b", a=16), padi[:])
                    load(dst_pad[1:1 + N_EDGES].rearrange("(a b) -> a b", a=16), dst.rearrange("(a b) -> a b", a=16))
                    load(dst_pad[1 + N_EDGES:1 + EP].rearrange("(a b) -> a b", a=16), padi[:])
                    load(dst_pad[0:1].rearrange("(a b) -> a b", a=1), sentinel[:, 0:1])
                    load(dst_pad[EP + 1:EP + 2].rearrange("(a b) -> a b", a=1), sentinel[:, 1:2])
                    load(attr_pad[0:N_EDGES, :].rearrange("(a b) d -> a (b d)", a=16),
                         edge_attr.rearrange("(a b) d -> a (b d)", a=16))
                    load(attr_pad[N_EDGES:EP, :].rearrange("(a b) d -> a (b d)", a=16), zeros[0:16, :])
                    for k in range(2):
                        load(tab[k][EP:EP + P, :], zeros[:, 0:D])
                    sp.wait_ge(loaded, 16 * nw[0])
                    sp.sem_inc(kept, 1)

                @block.tensor
                def _(pe):
                    pe.wait_ge(kept, 1)
                    pe.wait_ge(shaped, 1)
                    nc.tensor.transpose(ps[:, 0, 0:P], Wl_raw[:], ident[:]).then_inc(flipped, 1)
                    pe.wait_ge(built, 2)
                    nc.tensor.matmul(ps[:, 0, 0:1], center[:], bias[:, BO:BO + 1], start=True, stop=True).then_inc(flipped, 1)
                    nc.tensor.matmul(ps[:, 1, 0:P], Wo_raw[:], center[:], start=True, stop=True).then_inc(flipped, 1)
            nc.all_engine_barrier()
            for one in (prep, loaded, built, shaped, flipped, kept):
                nc.gpsimd.sem_clear(one)
            nc.gpsimd.sem_inc(begun, 1)

        def edge_view(v, t, u, n=1):
            r = v.rearrange("(s h p j) -> p s h j", h=2, p=P, j=QJ * n)
            return r[:, bass.DynSlice(2 * t + u, 1), :, :].rearrange("p s h j -> p (s h) j")

        UNR = 4
        with stage(["onehot", "counted", "flipped", "flip_read", "attr_flipped", "attr_read", "chain"],
                   ["idx", "got", "attr"], ["kept", "attr_kept"]) as (block, S, sbt, pst):
            step = S["chain"]
            nodes = sbt("nodes", [P, 2, NQ], i32)
            lo_i, hi_i = sbt("lo_i", [P, 2, NQ], i32), sbt("hi_i", [P, 2, NQ], i32)
            lo, hi = sbt("lo", [P, 2, NQ]), sbt("hi", [P, 2, NQ])
            ramp_i, ramp = sbt("ramp_i", [P, LO], i32), sbt("ramp", [P, LO], f16)
            oh = sbt("oh", [P, 2, 2, LO + P], f16)
            I = sbt("I", [P, 2, 2, 2 * QJ], i32)
            G = sbt("G", [P, 2, 2 * QJ, P])
            XT = sbt("XT", [P, 2, SUP])
            AT = sbt("AT", [P, 2, 2 * QJ, EDGE_DIM])
            ATT = sbt("ATT", [EDGE_DIM, 2, SUP])
            psX = [pst(f"psX{h}") for h in range(2)]
            psH = [[pst(f"psH{k}{b}") for b in range(2)] for k in range(2)]
            psA = [pst(f"psA{h}", [P, HALF]) for h in range(2)]
            dsts = sbt("dsts", [NS, 3, SUP], i32)
            msk = sbt("msk", [NS, 2, SUP], bf16)
            de = sbt("de", [P, 2, NQ], i32)
            def_ = sbt("def_", [P, 2, NQ])
            cnt = sbt("cnt", [P, 2, LO])
            ones = sbt("ones", [P, LO])
            incl, sq = sbt("incl", [P, LO]), sbt("sq", [P, 3, LO])
            valid, first_e = sbt("valid", [P, LO]), sbt("first_e", [P, LO])
            ntab = sbt("ntab", [P, LO, 8])
            nothing = sbt("nothing", [P, HALF], f16)

            with ExitStack() as s2:
                once = s2.enter_context(nc.semaphore("once"))
                ramp_ok = s2.enter_context(nc.semaphore("ramp_ok"))
                roots = s2.enter_context(nc.semaphore("roots"))
                offset_ok = s2.enter_context(nc.semaphore("offset_ok"))
                masks_ok = s2.enter_context(nc.semaphore("masks_ok"))
                stored = s2.enter_context(nc.semaphore("stored"))
                table_ok = s2.enter_context(nc.semaphore("table_ok"))
                sums_ok = s2.enter_context(nc.semaphore("sums_ok"))
                zeroed = s2.enter_context(nc.semaphore("zeroed"))
                zeros_ok = s2.enter_context(nc.semaphore("zeros_ok"))

                @block.sync
                def _(sp):
                    sp.dma_start(nodes[:, 0, :], src_pad.rearrange("(p q) -> p q", p=P)).then_inc(once, 16)
                    sp.dma_start(nodes[:, 1, :], dst_pad[1:1 + EP].rearrange("(p q) -> p q", p=P)).then_inc(once, 16)
                    for k in range(3):
                        sp.dma_start(dsts[:, k, :], dst_pad[k:k + EP].rearrange("(r c) -> r c", r=NS)).then_inc(once, 16)
                    for k in range(2):
                        sp.dma_start(de[:, k, :].rearrange("p (s j) -> p s j", j=QJ),
                                     dst_pad[k:k + EP].rearrange("(s p j) -> p s j", p=P, j=QJ)).then_inc(once, 16)
                    with sp.Fori(0, NS // 2) as t:
                        for u in range(2):
                            hold(sp, (S["flipped"], freed2(t, u, 1)))
                            sp.dma_start(I[:, u, 0, :].rearrange("p (h j) -> p h j", j=QJ),
                                         edge_view(dst_pad[1:1 + EP], t, u)).then_inc(S["idx"][u], 16)
                            sp.dma_start(I[:, u, 1, :].rearrange("p (h j) -> p h j", j=QJ),
                                         edge_view(src_pad, t, u)).then_inc(S["idx"][u], 16)
                            hold(sp, (S["attr_flipped"], freed2(t, u, 1)))
                            sp.dma_start(AT[:, u].rearrange("p (h j) d -> p h (j d)", h=2),
                                         edge_view(attr_pad.rearrange("e d -> (e d)"), t, u, EDGE_DIM)
                                         ).then_inc(S["attr"][u], 16)
                    sp.wait_ge(masks_ok, 1)
                    sp.dma_start(mask_dram["F"][:, :], msk[:, 0, :]).then_inc(stored, 16)
                    sp.dma_start(mask_dram["R"][:, :], msk[:, 1, :]).then_inc(stored, 16)
                    sp.wait_ge(table_ok, 1)
                    sp.dma_start(node_table.rearrange("(p l) f -> p (l f)", p=P),
                                 ntab[:].rearrange("p l f -> p (l f)")).then_inc(stored, 16)
                    sp.wait_ge(stored, 48)

                @block.gpsimd
                def _(pool):
                    nc.gpsimd.iota(ramp_i[:], pattern=[[1, LO]], base=0, channel_multiplier=0).then_inc(ramp_ok, 1)
                    nc.gpsimd.memset(G[:], 0.0).then_inc(zeroed, 1)
                    pool.wait_ge(zeroed, 1)
                    top = pool.to_reg(N_NODES - 1)
                    with pool.Fori(0, NS // 2) as t:
                        for u in range(2):
                            hold(pool, (S["idx"][u], t * 32 + 32), (S["flipped"], freed2(t, u, 1)))
                            for q in range(2 * QJ):
                                for k in range(2):
                                    nc.gpsimd.indirect_dma_start(
                                        out=G[:, u, q, k * D:k * D + D], out_offset=None, in_=x[:, :],
                                        in_offset=bass.IndirectOffsetOnAxis(ap=I[:, u, k, q:q + 1], axis=0),
                                        bounds_check=top, oob_is_err=False).then_inc(S["got"][u], 16)

                @block.tensor
                def _(pe):
                    pe.wait_ge(zeros_ok, 1)
                    for k in range(2):
                        for b in range(2):
                            nc.tensor.matmul(psH[k][b][:], nothing[:, 0:P], nothing[:],
                                             start=True, stop=True)
                    with pe.Fori(0, NS // 2) as t:
                        for u in range(2):
                            for h in range(2):
                                for i in range(UNR):
                                    for k in range(2):
                                        hold(pe, (S["onehot"], (4 * t + 2 * u + h) * (UNR * 2) + (i * 2 + k + 1) + CREDIT))
                                        for b in range(2):
                                            last = nc.tensor.matmul(psH[k][b][:], oh[:, i % 2, k, LO:LO + P],
                                                                    oh[:, i % 2, k, b * HALF:(b + 1) * HALF],
                                                                    start=False, stop=True, skip_group_check=True)
                                        last.then_inc(S["counted"], 1)
                            for h in range(2):
                                hold(pe, (S["got"][u], t * (16 * 4 * QJ) + 16 * 4 * QJ), (S["flip_read"], freed1(t, u, h)))
                                for j in range(QJ):
                                    last = nc.tensor.transpose(psX[h][:].rearrange("f (p j) -> f j p", j=QJ)[:, j, :],
                                                               G[:, u, h * QJ + j, :], ident[:])
                                last.then_inc(S["flipped"], 1)
                                hold(pe, (S["attr"][u], t * 16 + 16), (S["attr_read"], freed1(t, u, h)))
                                for j in range(QJ):
                                    last = nc.tensor.transpose(
                                        psA[h][0:EDGE_DIM, :].rearrange("f (p j) -> f j p", j=QJ)[:, j, :],
                                        AT[:, u, h * QJ + j, :], ident[:])
                                last.then_inc(S["attr_flipped"], 1)
                    pe.wait_ge(sums_ok, 1)
                    pe.wait_ge(S["flip_read"], made(NS // 2 - 1, 1, 1))
                    nc.tensor.matmul(psX[0][:, 0:1], before[:], incl[:, LO - 1:LO], start=True, stop=True).then_inc(offset_ok, 1)

                @block.scalar
                def _(act):
                    with act.Fori(0, NS // 2) as t:
                        for u in range(2):
                            for h in range(2):
                                hold(act, (S["flipped"], made(t, u, h)), (S["kept"][u], kept_at(t)))
                                nc.scalar.copy(XT[:, u, h * HALF:(h + 1) * HALF], psX[h][:]).then_inc(S["flip_read"], 1)
                                hold(act, (S["attr_flipped"], made(t, u, h)), (S["attr_kept"][u], kept_at(t)))
                                nc.scalar.copy(ATT[:, u, h * HALF:(h + 1) * HALF], psA[h][0:EDGE_DIM, :]).then_inc(S["attr_read"], 1)
                            hold(act, (S["flip_read"], made(t, u, 1)), (S["attr_read"], made(t, u, 1)))
                            act.dma_start(st["X0"][bass.DynSlice(2 * t + u, 1), :, :].rearrange("s p e -> p (s e)"),
                                          XT[:, u, :]).then_inc(S["kept"][u], 16)
                            act.dma_start(attrT[bass.DynSlice(2 * t + u, 1), :, :].rearrange("s p e -> p (s e)"),
                                          ATT[:, u, :]).then_inc(S["attr_kept"][u], 16)
                    for u in range(2):
                        act.wait_ge(S["kept"][u], kept_at(NS // 2))
                        act.wait_ge(S["attr_kept"][u], kept_at(NS // 2))
                    act.wait_ge(sums_ok, 1)
                    nc.scalar.activation(sq[:], sq[:], ACT.Sqrt, bias=bias[:, BZ:BZ + 1]).then_inc(roots, 1)

                @block.vector
                def _(dve):
                    c = [CREDIT]

                    def link(ins):
                        c[0] += 1
                        ins.then_inc(step, 1)
                        dve.wait_ge(step, c[0])

                    dve.wait_ge(once, 16 * 7)
                    dve.wait_ge(ramp_ok, 1)
                    nc.vector.memset(nothing[:], 0.0).then_inc(zeros_ok, 1)
                    nc.vector.tensor_copy(ramp[:], ramp_i[:])
                    nc.vector.tensor_scalar(lo_i[:], nodes[:], LO - 1, None, ALU.bitwise_and)
                    link(nc.vector.tensor_scalar(hi_i[:], nodes[:], 10, None, ALU.logical_shift_right))
                    nc.vector.tensor_copy(lo[:], lo_i[:])
                    link(nc.vector.tensor_copy(hi[:], hi_i[:]))
                    nc.vector.tensor_tensor(msk[:, 0, :], dsts[:, 1, :], dsts[:, 0, :], ALU.is_equal)
                    nc.vector.tensor_tensor(msk[:, 1, :], dsts[:, 1, :], dsts[:, 2, :], ALU.is_equal).then_inc(masks_ok, 1)
                    link(nc.vector.tensor_copy(def_[:], de[:]))
                    link(nc.vector.tensor_tensor(def_[:, 0, :], def_[:, 0, :], def_[:, 1, :], ALU.is_equal))
                    link(nc.vector.scalar_tensor_tensor(out=def_[:, 0, :], in0=def_[:, 0, :], scalar=float(2 * N_NODES),
                                                        in1=def_[:, 1, :], op0=ALU.mult, op1=ALU.add))
                    nc.vector.tensor_copy(idx_out[:], def_[:, 0, :])
                    with dve.Fori(0, NS // 2) as t:
                        for g in range(4):
                            for i in range(UNR):
                                for k in range(2):
                                    n = t * (UNR * 8) + (g * UNR + i) * 2 + k
                                    hold(dve, (S["counted"], n + (CREDIT - 3)))
                                    col = t * (4 * UNR) + g * UNR + i
                                    nc.vector.tensor_scalar(oh[:, i % 2, k, 0:LO], ramp[:], lo[:, k, bass.DynSlice(col, 1)],
                                                            None, ALU.is_equal)
                                    nc.vector.tensor_scalar(oh[:, i % 2, k, LO:LO + P], ramp[:, 0:P],
                                                            hi[:, k, bass.DynSlice(col, 1)], None,
                                                            ALU.is_equal).then_inc(S["onehot"], 1)
                    dve.wait_ge(S["counted"], 2 * NQ + CREDIT)
                    nc.vector.memset(ones[:], 1.0)
                    nc.vector.memset(ntab[:], 0.0)
                    for k in range(2):
                        for b in range(2):
                            l = nc.vector.tensor_copy(cnt[:, k, b * HALF:(b + 1) * HALF], psH[k][b][:])
                    link(l)
                    nc.vector.tensor_scalar(sq[:, 0, :], cnt[:, 1, :], 1.0, None, ALU.add)
                    nc.vector.tensor_scalar(sq[:, 1, :], cnt[:, 0, :], 1.0, None, ALU.max)
                    nc.vector.tensor_scalar(sq[:, 2, :], cnt[:, 1, :], 1.0, None, ALU.max)
                    nc.vector.tensor_scalar(valid[:], cnt[:, 1, :], 1.0, None, ALU.min)
                    nc.vector.tensor_tensor_scan(out=incl[:], data0=ones[:], data1=cnt[:, 1, :], initial=0.0,
                                                 op0=ALU.mult, op1=ALU.add).then_inc(sums_ok, 1)
                    dve.wait_ge(offset_ok, 1)
                    dve.wait_ge(roots, 1)
                    link(nc.vector.tensor_scalar(incl[:], incl[:], psX[0][:, 0:1], None, ALU.add))
                    for k in range(3):
                        nc.vector.reciprocal(ntab[:, :, k], sq[:, k, :])
                    link(nc.vector.tensor_tensor(first_e[:], incl[:], cnt[:, 1, :], ALU.subtract))
                    link(nc.vector.tensor_tensor(incl[:], incl[:], valid[:], ALU.mult))
                    link(nc.vector.scalar_tensor_tensor(out=first_e[:], in0=first_e[:], scalar=1.0, in1=valid[:],
                                                        op0=ALU.add, op1=ALU.mult))
                    nc.vector.tensor_scalar(ntab[:, :, 3], incl[:], -1.0, None, ALU.add)
                    nc.vector.tensor_scalar(ntab[:, :, 4], first_e[:], -1.0, None, ALU.add).then_inc(table_ok, 1)

        for one in (once, ramp_ok, roots, offset_ok, masks_ok, stored, table_ok, sums_ok, zeroed, zeros_ok):
            nc.gpsimd.sem_clear(one)

        CH = SUP
        n_full = N_NODES // CH
        rest = (N_NODES - n_full * CH) // 2
        REST_P = 112
        assert n_full % 2 == 1 and rest == REST_P * 3
        dense_ops = ["xin", "x0", "m1", "h1", "m2", "h2", "y1", "ma", "ha", "mb", "hb", "mc", "hc", "y3",
                     "back", "read", "ce1", "sq1", "va1", "ln2", "rs2", "x2",
                     "ce3", "sq3", "va3", "ln3", "rs3", "x3", "sq4", "va4", "ln4", "rs4", "x4"]
        with stage(dense_ops + ["copied"], ["nidx", "got", "nx"], ["nkept"]) as (block, S, sbt, pst):
            RES = sbt("RES", [P, 2, 8, NQ])
            T = sbt("T", [P, 2, 2, 2 * QJ, 8])
            I = sbt("I", [P, 2, 2, 2 * QJ], i32)
            X = sbt("X", [P, 2, 2, QJ, 2, D])
            Xt, H, Hb, Y, SD = (sbt(n, [P, 2, 2, HALF]) for n in ("Xt", "H", "Hb", "Y", "SD"))
            Xo = sbt("Xo", [P, 2, 2, QJ, 2, D])
            miss = sbt("miss", [P, NQ])
            zr_i, zr = sbt("zr_i", [P, 1], i32), sbt("zr", [P, 1])
            psT, psM = ([[pst(f"{n}{u}{h}") for h in range(2)] for u in range(2)] for n in ("psT", "psM"))
            with ExitStack() as s2:
                ramped = s2.enter_context(nc.semaphore("ramped"))
                fin = s2.enter_context(nc.semaphore("fin"))
                rows_kept = s2.enter_context(nc.semaphore("rows_kept"))

                @block.gpsimd
                def _(pool):
                    nc.gpsimd.iota(zr_i[:], pattern=[[0, 1]], base=EP + 1, channel_multiplier=1).then_inc(ramped, 1)
                    with pool.Fori(0, NS // 2) as t:
                        for u in range(2):
                            hold(pool, (S["nidx"][u], t * 32 + 32), (S["copied"], 2 * t + u - 1 + CREDIT))
                            for q in range(2 * QJ):
                                for k in range(2):
                                    nc.gpsimd.indirect_dma_start(
                                        out=T[:, u, k, q, :], out_offset=None, in_=node_table[:, :],
                                        in_offset=bass.IndirectOffsetOnAxis(ap=I[:, u, k, q:q + 1], axis=0),
                                    ).then_inc(S["got"][u], 16)

                TT = (n_full - 1) // 4
                assert 4 * TT == n_full - 1
                every = [(u, h, P, QJ, HALF) for u in range(2) for h in range(2)]
                final = [(0, 0, P, QJ, HALF), (0, 1, REST_P, 3, rest)]

                def node_rows(v, t, u, h, a):
                    return v[bass.DynSlice((4 * t + 2 * u + h) * CH + a * HALF, HALF), :].rearrange(
                        "(p j) d -> p j d", j=QJ)

                def last_rows(v, h, a):
                    jj, ww = final[h][3:]
                    at = (n_full - 1 + h) * CH + a * ww
                    return v[at:at + ww, :].rearrange("(p j) d -> p j d", j=jj)

                @block.sync
                def _(sp):
                    def idx_load(t, u):
                        hold(sp, (S["copied"], 2 * t + u - 1 + CREDIT))
                        sp.dma_start(I[:, u, 0, :].rearrange("p (h j) -> p h j", j=QJ),
                                     edge_view(dst_pad[1:1 + EP], t, u)).then_inc(S["nidx"][u], 16)
                        sp.dma_start(I[:, u, 1, :].rearrange("p (h j) -> p h j", j=QJ),
                                     edge_view(src_pad, t, u)).then_inc(S["nidx"][u], 16)

                    def loads(t):
                        for u in range(2):
                            idx_load(t, u)
                            hold(sp, (S["xin"], freed2(t, u, 1)))
                            for h in range(2):
                                for a in range(2):
                                    sp.dma_start(X[:, u, h, :, a, :], node_rows(x, t, u, h, a)).then_inc(S["nx"][u], 16)

                    def stores_of(t, units):
                        for u, h, pp, jj, W in units:
                            hold(sp, (S["read"], made(t, u, h)))
                            for a in range(2):
                                sp.dma_start(node_rows(out, t, u, h, a) if units is every else last_rows(out, h, a),
                                             Xo[0:pp, u, h, 0:jj, a, :]).then_inc(S["nkept"][u], 16)

                    def keep_rows(s0, s1):
                        sp.wait_ge(S["copied"], s1 + CREDIT)
                        for name, k, f in (("dis_d", 0, 0), ("dis_s", 1, 0), ("nsrc_s", 1, 1), ("ndst_d", 0, 2),
                                           ("ndst_s", 1, 2)):
                            sp.dma_start(rows[name][s0:s1, :].rearrange("s (h p j) -> p (s h) j", h=2, j=QJ),
                                         RES[:, k, f, s0 * 2 * QJ:s1 * 2 * QJ].rearrange("p (s j) -> p s j", j=QJ)
                                         ).then_inc(rows_kept, 16)

                    loads(0)
                    with sp.Fori(1, TT) as t:
                        loads(t)
                        stores_of(t - 1, every)
                    sp.wait_ge(S["xin"], freed2(TT, 0, 1))
                    for _, h, pp, jj, ww in final:
                        for a in range(2):
                            sp.dma_start(X[0:pp, 0, h, 0:jj, a, :], last_rows(x, h, a)).then_inc(S["nx"][0], 16)
                    with sp.Fori(TT, NS // 2) as t:
                        for u in range(2):
                            idx_load(t, u)
                    keep_rows(0, 2 * TT)
                    stores_of(TT - 1, every)
                    stores_of(TT, final)
                    keep_rows(2 * TT, NS)
                    sp.wait_ge(rows_kept, 16 * 10)
                    sp.wait_ge(S["nkept"][0], 16 + 64 * TT + 64)
                    sp.wait_ge(S["nkept"][1], 16 + 64 * TT)

                def dense_pe(pe, t, units):
                    def mm(name, ps, w, rhs, need, free=()):
                        for u, h, _, _, W in units:
                            hold(pe, (S[need], made(t, u, h)), *[(S[m], freed2(t, u, h)) for m in free])
                            nc.tensor.matmul(ps[u][h][:, 0:W], w, rhs[:, u, h, 0:W], start=True, stop=True
                                             ).then_inc(S[name], 1)

                    for u, h, pp, jj, W in units:
                        hold(pe, (S["nx"][u], 64 * t + 64), (S["ln4"], freed2(t, u, h)))
                        for j in range(jj):
                            last = nc.tensor.transpose(psT[u][h][:, 0:W].rearrange("f (p j) -> f j p", j=jj)[:, j, :],
                                                       X[0:pp, u, h, j, :, :].rearrange("p a d -> p (a d)"), ident[0:pp, 0:pp])
                        last.then_inc(S["xin"], 1)
                    mm("m1", psM, W1b[:], Xt, "x0", ("read",))
                    mm("m2", psM, W2b[:], H, "h1")
                    mm("ce1", psM, center[:], Y, "y1")
                    mm("va1", psT, avg[:], Y, "sq1")
                    mm("ma", psM, Wu1[:, 0, :], Hb, "x2")
                    mm("mb", psM, Wu1[:, 1, :], H, "ha")
                    mm("mc", psM, Wu1[:, 2, :], Xt, "hb")
                    mm("ce3", psM, center[:], Y, "y3")
                    mm("va3", psT, avg[:], Y, "sq3")
                    mm("va4", psT, avg[:], H, "sq4")
                    for u, h, pp, jj, W in units:
                        hold(pe, (S["x4"], made(t, u, h)))
                        for j in range(jj):
                            last = nc.tensor.transpose(psM[u][h][0:pp, j * P:(j + 1) * P],
                                                       H[:, u, h, 0:W].rearrange("f (p j) -> f j p", j=jj)[:, j, :], ident[:])
                        last.then_inc(S["back"], 1)

                @block.tensor
                def _(pe):
                    with pe.Fori(0, TT) as t:
                        dense_pe(pe, t, every)
                    dense_pe(pe, TT, final)

                def dense_act(act, t, units):
                    def ac(name, o, i, func, need, b, free=(), scale=1.0, us=units):
                        for u, h, _, _, W in us:
                            hold(act, (S[need], made(t, u, h)), *[(S[f], freed2(t, u, h)) for f in free])
                            src_ = i[u][h][:, 0:W] if i in (psT, psM) else i[:, u, h, 0:W]
                            nc.scalar.activation(o[:, u, h, 0:W], src_, func, bias=bias[:, b:b + 1], scale=scale
                                                 ).then_inc(S[name], 1)

                    def root(i):
                        for one in units:
                            ac("ln" + i, SD, psT, ACT.Ln, "va" + i, BEPS, us=[one])
                            ac("rs" + i, SD, SD, ACT.Exp, "ln" + i, BZ, scale=-0.5, us=[one])

                    ac("h1", H, psM, ACT.Relu, "m1", B1, free=("back",))
                    ac("h2", Hb, psM, ACT.Relu, "m2", B2, free=("y3",))
                    ac("sq1", Y, psM, ACT.Square, "ce1", BZ)
                    for one in units:
                        ac("ln2", SD, psT, ACT.Ln, "va1", BEPS2, scale=(1.0 + ALPHA) ** 2 + EPS, us=[one])
                        ac("rs2", SD, SD, ACT.Exp, "ln2", BZ, scale=-0.5, us=[one])
                    ac("ha", H, psM, ACT.Relu, "ma", BU)
                    ac("hc", H, psM, ACT.Relu, "mc", BU + 2)
                    ac("sq3", Y, psM, ACT.Square, "ce3", BZ)
                    root("3")
                    ac("sq4", H, Y, ACT.Square, "x3", BC)
                    root("4")
                @block.scalar
                def _(act):
                    act.preload_act_table_set("natural_log_exp_and_others")
                    with act.Fori(0, TT) as t:
                        dense_act(act, t, every)
                    dense_act(act, TT, final)

                def keep_scalars(dve, t, u):
                    hold(dve, (S["got"][u], t * (16 * 4 * QJ) + 16 * 4 * QJ))
                    for k in range(2):
                        last = nc.vector.tensor_copy(
                            RES[:, k, :, bass.DynSlice((2 * t + u) * 2 * QJ, 2 * QJ)],
                            T[:, u, k].rearrange("p q f -> p f q"))
                    last.then_inc(S["copied"], 1)

                def dense_dve(dve, t, units):
                    def ve(name, fn, need, free=None):
                        for u, h, _, _, W in units:
                            hold(dve, (S[need], made(t, u, h)), *([(S[free], freed2(t, u, h))] if free else []))
                            fn(u, h, W).then_inc(S[name], 1)

                    def stt(o, a, sc, b, op0=ALU.mult, op1=ALU.add):
                        return lambda u, h, W: nc.vector.scalar_tensor_tensor(
                            out=o[:, u, h, 0:W], in0=a[:, u, h, 0:W], scalar=sc, in1=b[:, u, h, 0:W], op0=op0, op1=op1)

                    def from_bank(ps, o, factor, b):
                        return lambda u, h, W: nc.vector.scalar_tensor_tensor(
                            out=o[:, u, h, 0:W], in0=ps[u][h][:, 0:W], scalar=factor, in1=b[:, u, h, 0:W],
                            op0=ALU.mult, op1=ALU.mult)

                    ve("x0", lambda u, h, W: nc.vector.tensor_copy(Xt[:, u, h, 0:W], psT[u][h][:, 0:W]), "xin", free="mc")
                    ve("y1", stt(Y, Xt, 2.0, Hb), "h2")
                    ve("x2", from_bank(psM, Hb, 1.0 + ALPHA, SD), "rs2")
                    ve("hb", lambda u, h, W: nc.vector.tensor_scalar(
                        Xt[:, u, h, 0:W], psM[u][h][:, 0:W], bias[:, BU + 1:BU + 2], 0.0, ALU.add, ALU.max), "mb")
                    ve("y3", stt(Y, Hb, 1.0, H), "hc")
                    ve("x3", from_bank(psM, Y, 1.0, SD), "rs3")
                    ve("x4", lambda u, h, W: nc.vector.scalar_tensor_tensor(
                        out=H[:, u, h, 0:W], in0=Y[:, u, h, 0:W], scalar=bias[:, BC:BC + 1], in1=SD[:, u, h, 0:W],
                        op0=ALU.add, op1=ALU.mult), "rs4")
                    for u, h, pp, jj, W in units:
                        hold(dve, (S["back"], made(t, u, h)), (S["nkept"][u], t * 64 + 16))
                        nc.vector.tensor_copy(Xo[0:pp, u, h, 0:jj].rearrange("p j a d -> p (j a d)"),
                                              psM[u][h][0:pp, 0:jj * P]).then_inc(S["read"], 1)

                @block.vector
                def _(dve):
                    dve.wait_ge(ramped, 1)
                    nc.vector.tensor_copy(zr[:], zr_i[:])
                    with dve.Fori(0, TT) as t:
                        for u in range(2):
                            keep_scalars(dve, t, u)
                        dense_dve(dve, t, every)
                    with dve.Fori(TT, NS // 2) as t:
                        for u in range(2):
                            keep_scalars(dve, t, u)
                    dense_dve(dve, TT, final)
                    dve.wait_ge(S["copied"], NS + CREDIT)
                    n = 0
                    for f, o in ((3, idx_src_gl), (4, idx_src_gf)):
                        nc.vector.tensor_scalar(miss[:], RES[:, 1, f, :], 0.0, zr[:, 0:1], ALU.is_lt, ALU.mult).then_inc(fin, 1)
                        n += 1
                        dve.wait_ge(fin, n)
                        nc.vector.tensor_tensor(o[:], RES[:, 1, f, :], miss[:], ALU.add).then_inc(fin, 1)
                        n += 1
                        dve.wait_ge(fin, n)
                    nc.vector.scalar_tensor_tensor(out=a_src[:], in0=RES[:, 1, 1, :], scalar=1.0 - ALPHA,
                                                   in1=RES[:, 1, 2, :], op0=ALU.mult, op1=ALU.mult)

        for one in (ramped, fin, rows_kept):
            nc.gpsimd.sem_clear(one)

        def order(direction, t, u):
            return 2 * t + u if direction == "F" else (NS - 1 - u) - 2 * t

        def halves(direction):
            return (0, 1) if direction == "F" else (1, 0)

        def sup(v, n):
            return v[bass.DynSlice(n, 1), :, :].rearrange("s p e -> p (s e)")

        def spread(v, n, parts):
            return v[bass.DynSlice(n, 1), :].to_broadcast([parts, SUP])

        def tab_rows(v, n):
            return v[0:EP, :].rearrange("(s h p j) d -> p s h (j d)", h=2, p=P, j=QJ)[:, bass.DynSlice(n, 1), :, :] \
                .rearrange("p s h e -> p (s h) e")

        def appnp_pass(B_res, t_in, t_out, keepT=None):
            with stage(["scaled", "added", "flipped", "scanned", "back", "read"],
                       ["idx", "got", "mask"], ["kept"] + (["keptT"] if keepT is not None else [])) as (block, S, sbt, pst):
                I = sbt("I", [P, 2, 2 * QJ], i32)
                G = sbt("G", [P, 2, 2 * QJ, D])
                M = sbt("M", [P, 2 * QJ, D])
                K = sbt("K", [D, 2, SUP], bf16)
                ST = sbt("ST", [D, 2, SUP])
                SR = sbt("SR", [P, 2, 2 * QJ, D])
                psT = [pst(f"psT{h}") for h in range(2)]
                psB = [pst(f"psB{h}") for h in range(2)]
                tin, tout = tab[t_in], tab[t_out]

                @block.sync
                def _(sp):
                    with sp.Fori(0, NS // 2) as t:
                        for u in range(2):
                            hold(sp, (S["scaled"], freed2(t, u, 1)))
                            sp.dma_start(I[:, u, :], idx_src_gl[:, bass.DynSlice((2 * t + u) * 2 * QJ, 2 * QJ)]
                                         ).then_inc(S["idx"][u], 16)
                            hold(sp, (S["scanned"], freed2(t, u, 1)))
                            sp.dma_start(K[:, u, :], spread(mask_dram["F"], 2 * t + u, D)).then_inc(S["mask"][u], 16)

                @block.gpsimd
                def _(pool):
                    with pool.Fori(0, NS // 2) as t:
                        for u in range(2):
                            hold(pool, (S["idx"][u], t * 16 + 16), (S["scaled"], freed2(t, u, 1)))
                            for q in range(2 * QJ):
                                nc.gpsimd.indirect_dma_start(
                                    out=G[:, u, q, :], out_offset=None, in_=tin[:, :],
                                    in_offset=bass.IndirectOffsetOnAxis(ap=I[:, u, q:q + 1], axis=0),
                                ).then_inc(S["got"][u], 16)

                @block.vector
                def _(dve):
                    nc.vector.memset(ST[:, 1, SUP - 1:SUP], 0.0)
                    with dve.Fori(0, NS // 2) as t:
                        for u in range(2):
                            q0 = (2 * t + u) * 2 * QJ
                            for h in range(2):
                                q = slice(h * QJ, (h + 1) * QJ)
                                hold(dve, (S["got"][u], t * (32 * QJ) + 32 * QJ), (S["flipped"], freed1(t, u, h)))
                                nc.vector.tensor_tensor(
                                    M[:, q, :], G[:, u, q, :],
                                    a_src[:, bass.DynSlice(q0 + h * QJ, QJ)].unsqueeze(2).to_broadcast([P, QJ, D]),
                                    ALU.mult).then_inc(S["scaled"], 1)
                            for h in range(2):
                                q = slice(h * QJ, (h + 1) * QJ)
                                hold(dve, (S["scaled"], made(t, u, h)))
                                nc.vector.tensor_tensor(M[:, q, :], M[:, q, :], B_res[:, bass.DynSlice(q0 + h * QJ, QJ), :],
                                                        ALU.add).then_inc(S["added"], 1)
                            for h in range(2):
                                before_ = ST[:, u, HALF - 1:HALF] if h else ST[:, 1 - u, SUP - 1:SUP]
                                hold(dve, (S["mask"][u], t * 16 + 16), (S["flipped"], made(t, u, h)),
                                     (S["scanned"], made(t, u, h) - 1), (S["back"], freed2(t, u, h)),
                                     *([(S["keptT"][u], kept_at(t))] if keepT is not None else []))
                                nc.vector.tensor_tensor_scan(
                                    out=ST[:, u, h * HALF:(h + 1) * HALF], data0=K[:, u, h * HALF:(h + 1) * HALF],
                                    data1=psT[h][0:D, :], initial=before_, op0=ALU.mult, op1=ALU.add
                                ).then_inc(S["scanned"], 1)

                @block.tensor
                def _(pe):
                    with pe.Fori(0, NS // 2) as t:
                        for u in range(2):
                            for h in range(2):
                                hold(pe, (S["added"], made(t, u, h)), (S["scanned"], freed1(t, u, h)))
                                for j in range(QJ):
                                    last = nc.tensor.transpose(psT[h][0:D, :].rearrange("f (p j) -> f j p", j=QJ)[:, j, :],
                                                               M[:, h * QJ + j, :], ident[:])
                                last.then_inc(S["flipped"], 1)
                            for h in range(2):
                                hold(pe, (S["scanned"], made(t, u, h)), (S["read"], freed1(t, u, h)))
                                for j in range(QJ):
                                    last = nc.tensor.transpose(
                                        psB[h][:, j * D:(j + 1) * D],
                                        ST[:, u, h * HALF:(h + 1) * HALF].rearrange("f (p j) -> f j p", j=QJ)[:, j, :],
                                        ident[0:D, 0:D])
                                last.then_inc(S["back"], 1)

                @block.scalar
                def _(act):
                    with act.Fori(0, NS // 2) as t:
                        for u in range(2):
                            for h in range(2):
                                hold(act, (S["back"], made(t, u, h)), (S["kept"][u], kept_at(t)))
                                nc.scalar.copy(SR[:, u, h * QJ:(h + 1) * QJ, :],
                                               psB[h][:, 0:QJ * D].rearrange("p (j d) -> p j d", d=D)).then_inc(S["read"], 1)
                            hold(act, (S["read"], made(t, u, 1)))
                            act.dma_start(tab_rows(tout, 2 * t + u),
                                          SR[:, u].rearrange("p (h j) d -> p h (j d)", h=2)).then_inc(S["kept"][u], 16)
                            if keepT is not None:
                                act.dma_start(sup(keepT, 2 * t + u), ST[:, u, :]).then_inc(S["keptT"][u], 16)
                    for u in range(2):
                        act.wait_ge(S["kept"][u], kept_at(NS // 2))
                        if keepT is not None:
                            act.wait_ge(S["keptT"][u], kept_at(NS // 2))

        def node_pass(kind, direction, tab_in=None, tab_out=None, tot_in=None, tot_out=None,
                      x_in=None, x_out=None, skip=None, layer=0, B_res=None):
            gather = tab_in is not None
            norm = kind in ("gcn2", "appnp_end", "attend", "finish")
            message = kind in ("appnp_end", "update")
            attention = kind in ("attend", "finish")
            scaled = kind in ("first", "gcn1", "gcn2", "appnp_end")
            idx_all = idx_src_gl if direction == "R" else idx_src_gf
            hs = halves(direction)
            z = hs[1]
            units = [(u, h) for u in range(2) for h in hs]
            wide = slice(0, P) if attention else slice(D, P)
            low = slice(0, P) if kind == "finish" else slice(0, D)
            counts = ["carry_ok", "scanned"]
            counts += ["at_zero"] if message else []
            counts += ["flipped", "agg_s"] if gather else []
            counts += ["masked", "agg_d"] if kind != "first" else []
            counts += {"first": ["v"],
                       "gcn1": ["v0", "u1", "u", "mm", "relu", "v"],
                       "gcn2": ["u1", "u", "mm", "relu", "y", "msg", "b_flip", "b_read"],
                       "appnp_end": ["u1", "y", "msg_mm", "msg"],
                       "update": ["mm", "x", "msg_mm", "msg"],
                       "attend": ["mm", "relu", "y", "msg_mm", "msg"],
                       "finish": ["msg_mm", "msg", "diff", "ex", "wx", "summed", "lden", "rden", "nf", "mm", "y"],
                       }[kind]
            counts += ["cent", "sq", "var", "ln", "rs", "x"] if norm else []
            counts += ["back", "read"] if kind != "attend" else []
            dmas = ["maskw", "state"]
            dmas += ["idx", "got"] if gather else []
            dmas += ["maskl", "tot"] if kind != "first" else []
            dmas += ["row"] if scaled else []
            dmas += ["nsrc"] if kind == "gcn2" else []
            dmas += ["skipped"] if skip else []
            dmas += ["attr"] if message else []
            dmas += ["oidx"] if kind == "finish" else []
            stores = ["xkept"] if x_out else []
            stores += ["kept"] if tab_out is not None else []
            stores += ["scat"] if kind == "finish" else []
            stores += ["totkept"] if tot_out is not None else []
            with stage(counts, dmas, stores) as (block, S, sbt, pst):
                two = lambda n, dt=f32: sbt(n, [P, 2, SUP], dt)
                KW = two("KW", bf16)
                KL = two("KL", bf16) if attention else KW
                X, XO, ST = two("X"), two("XO"), two("ST")
                Y, H = two("Y"), two("H")
                TOT, AG = (two("TOT"), two("AG")) if kind != "first" else (None, None)
                if gather:
                    I = sbt("I", [P, 2, 2 * QJ], i32)
                    G = sbt("G", [P, 2, 2 * QJ, P])
                if skip:
                    XS = two("XS")
                if scaled:
                    R = two("R")
                if kind == "gcn2":
                    NSR = TOT
                if message:
                    AT = two("AT")
                if kind == "finish":
                    NUM = two("NUM")
                    IO = sbt("IO", [P, 2, 2 * QJ], i32)
                MG = H if kind == "gcn2" else two("MG") if message or attention else None
                WX = MG
                SR = sbt("SR", [P, 2, 2 * QJ, D])
                psT, psM = ([[pst(f"{n}{u}{h}") for h in range(2)] for u in range(2)] for n in ("psT", "psM"))
                end = HALF - 1 if direction == "F" else 0

                def cols(h):
                    return slice(h * HALF, (h + 1) * HALF)

                def at(tile, part=slice(0, P)):
                    return lambda u, h: tile[part, u, cols(h)]

                def bank(ps):
                    return lambda u, h: ps[u][h][:]

                def md(t, u, h):
                    return made(t, u, hs.index(h))

                def fr(t, u, h):
                    return freed2(t, u, hs.index(h))

                def along(ap):
                    return ap if direction == "F" else ap[:, ::-1]

                x_used = {"first": "v", "gcn1": "u1", "gcn2": "u1", "appnp_end": "y", "update": "mm",
                          "attend": "mm", "finish": "y"}[kind]
                ag_used = {"gcn1": "u1", "gcn2": "u1", "appnp_end": "u1", "update": "mm", "attend": "mm",
                           "finish": "diff", "first": None}[kind]

                @block.sync
                def _(sp):
                    if message:
                        sp.wait_ge(S["at_zero"], 1 + CREDIT)

                    def load(t, name, free, dst_of, src_of):
                        for u in range(2):
                            hold(sp, (S[free], fr(t, u, z)))
                            sp.dma_start(dst_of(u), src_of(order(direction, t, u))).then_inc(S[name][u], 16)

                    def loads(t):
                        if kind != "first":
                            load(t, "maskl", "agg_d", lambda u: KL[low, u, :],
                                 lambda n: spread(mask_dram[direction], n, low.stop - low.start))
                            load(t, "tot", "agg_d", lambda u: TOT[low, u, :],
                                 lambda n: sup(maxT if kind == "finish" else totT[tot_in], n))
                        load(t, "state", x_used, lambda u: X[:, u, :], lambda n: sup(st[x_in], n))
                        if scaled:
                            r = "ndst" if kind == "appnp_end" else "dis"
                            used = {"first": "v", "gcn1": "v", "gcn2": "u", "appnp_end": "u1"}[kind]
                            load(t, "row", used, lambda u: R[0:D, u, :], lambda n: spread(rows[r + "_d"], n, D))
                            load(t, "row", used, lambda u: R[D:P, u, :], lambda n: spread(rows[r + "_s"], n, D))
                        if skip:
                            load(t, "skipped", "y", lambda u: XS[:, u, :], lambda n: sup(st[skip], n))
                        if kind == "gcn2":
                            load(t, "nsrc", "msg", lambda u: NSR[D:P, u, :], lambda n: spread(rows["nsrc_s"], n, D))
                        if message:
                            load(t, "attr", "msg_mm", lambda u: AT[0:EDGE_DIM, u, :], lambda n: sup(attrT, n))
                        load(t, "maskw", "summed" if kind == "finish" else "scanned", lambda u: KW[wide, u, :],
                             lambda n: spread(mask_dram[direction], n, wide.stop - wide.start))
                        if kind == "finish":
                            for u in range(2):
                                n = order(direction, t, u)
                                hold(sp, (S["scat"][u], t * (32 * QJ) + 16))
                                sp.dma_start(IO[:, u, :], idx_out[:, bass.DynSlice(n * (2 * QJ), 2 * QJ)]
                                             ).then_inc(S["oidx"][u], 16)

                    def stores_of(t):
                        for u in range(2):
                            n = order(direction, t, u)
                            if x_out:
                                made_by = "v" if kind in ("first", "gcn1") else "x"
                                hold(sp, (S[made_by], md(t, u, z)))
                                sp.dma_start(sup(st[x_out], n), XO[:, u, :]).then_inc(S["xkept"][u], 16)
                            if tot_out is not None:
                                hold(sp, (S["scanned"], md(t, u, z)))
                                sp.dma_start(sup(maxT if kind == "attend" else totT[tot_out], n), ST[wide, u, :]
                                             ).then_inc(S["totkept"][u], 16)
                            if tab_out is not None:
                                hold(sp, (S["read"], md(t, u, z)))
                                sp.dma_start(tab_rows(tab[tab_out], n),
                                             SR[:, u].rearrange("p (h j) d -> p h (j d)", h=2)).then_inc(S["kept"][u], 16)

                    loads(0)
                    with sp.Fori(1, NS // 2) as t:
                        loads(t)
                        stores_of(t - 1)
                    stores_of(NS // 2 - 1)
                    for c in stores:
                        if c != "scat":
                            for u in range(2):
                                sp.wait_ge(S[c][u], kept_at(NS // 2))

                @block.gpsimd
                def _(pool):
                    if message:
                        nc.gpsimd.memset(AT[:], 0.0).then_inc(S["at_zero"], 1)
                    if gather:
                        nc.gpsimd.memset(G[:], 0.0).then_inc(S["flipped"], 1)
                        pool.wait_ge(S["flipped"], 1 + CREDIT)
                        with pool.Fori(0, NS // 2) as t:
                            for u in range(2):
                                hold(pool, (S["idx"][u], t * 16 + 16), (S["flipped"], freed2(t, u, 1) + 1))
                                for q in range(2 * QJ):
                                    nc.gpsimd.indirect_dma_start(
                                        out=G[:, u, q, D:P], out_offset=None, in_=tab[tab_in][:, :],
                                        in_offset=bass.IndirectOffsetOnAxis(ap=I[:, u, q:q + 1], axis=0),
                                    ).then_inc(S["got"][u], 16)
                    if kind == "finish":
                        top = pool.to_reg(N_NODES - 1)
                        with pool.Fori(0, NS // 2) as t:
                            for u in range(2):
                                hold(pool, (S["read"], made(t, u, 1)), (S["oidx"][u], t * 16 + 16))
                                for q in range(2 * QJ):
                                    nc.gpsimd.indirect_dma_start(
                                        out=out[:, :], out_offset=bass.IndirectOffsetOnAxis(ap=IO[:, u, q:q + 1], axis=0),
                                        in_=SR[:, u, q, :], in_offset=None,
                                        bounds_check=top, oob_is_err=False).then_inc(S["scat"][u], 16)
                        for u in range(2):
                            pool.wait_ge(S["scat"][u], 32 * QJ * (NS // 2) + 16)

                @block.tensor
                def _(pe):
                    with pe.Fori(0, NS // 2) as t:
                        def mm(name, ps, terms, needs, frees=(), landed=()):
                            for u, h in units:
                                hold(pe, *[(S[a], md(t, u, h)) for a in needs], *[(S[a], fr(t, u, h)) for a in frees],
                                     *[(S[a][u], t * 16 + 16) for a in landed])
                                for i, (w, r) in enumerate(terms):
                                    last = nc.tensor.matmul(ps[u][h][:], w, r(u, h), start=(i == 0), stop=(i == len(terms) - 1))
                                last.then_inc(S[name], 1)

                        if gather:
                            tail = {"gcn2": "b_read", "gcn1": "agg_s"}.get(kind, "msg")
                            for u, h in units:
                                hold(pe, (S["got"][u], t * (32 * QJ) + 32 * QJ), (S[tail], fr(t, u, h)))
                                for j in range(QJ):
                                    last = nc.tensor.transpose(psT[u][h][:].rearrange("f (p j) -> f j p", j=QJ)[:, j, :],
                                                               G[:, u, h * QJ + j, :], ident[:])
                                last.then_inc(S["flipped"], 1)
                        if kind == "gcn1":
                            mm("mm", psM, [(W1b[:], at(Y))], ["u"], ["read"])
                        if kind == "gcn2":
                            mm("mm", psM, [(W2b[:], at(Y))], ["u"], ["read"])
                        if kind in ("update", "attend"):
                            mm("mm", psM, [(Wu1[:, layer, :], at(X)), (Wu2[:, layer, :], at(AG))],
                               ["agg_d", "agg_s"], ["read" if kind == "update" else "x"], ["state"])
                        if kind == "finish":
                            mm("msg_mm", psT, [(WlT[:], at(X))], [], ["ln"], ["state"])
                            mm("mm", psM, [(WoC[:], at(H))], ["nf"], ["read"])
                        if norm:
                            if kind != "finish":
                                mm("cent", psM, [(center[:], at(Y))], ["y"], ["read"] if kind == "appnp_end" else [])
                            mm("var", psT, [(avg[:], at(H if kind == "finish" else Y))], ["sq"])
                        if kind == "gcn2":
                            for u, h in units:
                                hold(pe, (S["msg"], md(t, u, h)))
                                for j in range(QJ):
                                    last = nc.tensor.transpose(
                                        psT[u][h][:, j * D:(j + 1) * D],
                                        MG[D:P, u, cols(h)].rearrange("f (p j) -> f j p", j=QJ)[:, j, :], ident[D:P, D:P])
                                last.then_inc(S["b_flip"], 1)
                        if message:
                            nxt = 0 if kind == "appnp_end" else layer + 1
                            mm("msg_mm", psT, [(Wm[:, nxt, :], at(XO)), (We[:, nxt, :], at(AT))], ["x"], [], ["attr"])
                        if kind == "attend":
                            mm("msg_mm", psT, [(WlT[:], at(XO))], ["x"])
                        if kind != "attend":
                            part, what = ((slice(0, D), "x") if kind == "finish" else (slice(D, P), "scanned"))
                            tile = XO if kind == "finish" else ST
                            for u, h in units:
                                hold(pe, (S[what], md(t, u, h)), *([(S["read"], fr(t, u, h))] if kind == "first" else []))
                                for j in range(QJ):
                                    last = nc.tensor.transpose(
                                        psM[u][h][:, j * D:(j + 1) * D],
                                        tile[part, u, cols(h)].rearrange("f (p j) -> f j p", j=QJ)[:, j, :],
                                        ident[part, part])
                                last.then_inc(S["back"], 1)

                @block.scalar
                def _(act):
                    act.preload_act_table_set("natural_log_exp_and_others")

                    def idx_load(t, u):
                        act.dma_start(I[:, u, :], idx_all[:, bass.DynSlice(order(direction, t, u) * (2 * QJ), 2 * QJ)]
                                      ).then_inc(S["idx"][u], 16)

                    def iteration(t, more):
                        def ac(name, o, i, func, b, needs, frees=(), store=None, scale=1.0, us=units):
                            for u, h in us:
                                hold(act, *[(S[a], md(t, u, h)) for a in needs], *[(S[a], fr(t, u, h)) for a in frees],
                                     *([(S[store][u], kept_at(t))] if store else []))
                                nc.scalar.activation(o(u, h), i(u, h), func, bias=bias[:, b:b + 1], scale=scale
                                                     ).then_inc(S[name], 1)

                        if more:
                            for u in range(2):
                                hold(act, (S["got"][u], t * (32 * QJ) + 32 * QJ))
                                idx_load(t + 1, u)
                        if gather:
                            for u, h in units:
                                hold(act, (S["flipped"], md(t, u, h) + 1), (S[ag_used], fr(t, u, h)))
                                nc.scalar.copy(AG[D:P, u, cols(h)], psT[u][h][D:P, :]).then_inc(S["agg_s"], 1)
                        if kind == "gcn1":
                            ac("relu", at(H), bank(psM), ACT.Relu, B1, ["mm"], ["v"])
                        if kind == "gcn2":
                            ac("relu", at(H), bank(psM), ACT.Relu, B2, ["mm"], ["b_flip", "scanned"])
                        if kind == "update":
                            ac("x", at(XO), bank(psM), ACT.Relu, BU + layer, ["mm"], ["msg_mm"], "xkept")
                        if kind == "attend":
                            ac("relu", at(H), bank(psM), ACT.Relu, BU + layer, ["mm"], ["x"])
                        if kind == "finish":
                            ac("msg", at(MG), bank(psT), ACT.Relu, BL, ["msg_mm"], ["nf"])
                            ac("ex", at(H), at(Y), ACT.Exp, BZ, ["diff"], ["x"])
                            for one in units:
                                ac("lden", at(WX), at(ST), ACT.Ln, BZ, ["scanned", "summed"], us=[one])
                                ac("rden", at(WX), at(WX), ACT.Exp, BZ, ["lden"], scale=-1.0, us=[one])
                        if norm:
                            if kind == "finish":
                                ac("sq", at(H), at(Y), ACT.Square, BZ, ["y"])
                            else:
                                ac("sq", at(Y), bank(psM), ACT.Square, BZ, ["cent"])
                            for one in units:
                                ac("ln", at(H), bank(psT), ACT.Ln, BEPS, ["var"], ["x"] if kind == "appnp_end" else [],
                                   us=[one])
                                ac("rs", at(H), at(H), ACT.Exp, BZ, ["ln"], scale=-0.5, us=[one])
                        if kind == "gcn2":
                            for u, h in units:
                                n = order(direction, t, u)
                                hold(act, (S["b_flip"], md(t, u, h)))
                                nc.scalar.mul(B_res[:, bass.DynSlice(n * (2 * QJ) + h * QJ, QJ), :],
                                              psT[u][h][:, 0:QJ * D].rearrange("p (j d) -> p j d", d=D), ALPHA
                                              ).then_inc(S["b_read"], 1)
                        if message:
                            nxt = 0 if kind == "appnp_end" else layer + 1
                            ac("msg", at(MG), bank(psT), ACT.Relu, BM + nxt, ["msg_mm"], ["scanned"])
                        if kind == "attend":
                            ac("msg", at(MG), bank(psT), ACT.Relu, BL, ["msg_mm"], ["scanned"])
                        if kind != "attend":
                            for u, h in units:
                                free = ((S["scat"][u], t * (32 * QJ) + 16) if kind == "finish" else
                                        (S["kept"][u], kept_at(t)))
                                hold(act, (S["back"], md(t, u, h)), free)
                                nc.scalar.copy(SR[:, u, h * QJ:(h + 1) * QJ, :],
                                               psM[u][h][:, 0:QJ * D].rearrange("p (j d) -> p j d", d=D)).then_inc(S["read"], 1)

                    if gather:
                        for u in range(2):
                            idx_load(0, u)
                    with act.Fori(0, NS // 2 - 1) as t:
                        iteration(t, gather)
                    iteration(NS // 2 - 1, False)

                @block.vector
                def _(dve):
                    first_cols = slice(z * HALF + end, z * HALF + end + 1)
                    for tile in [ST] + ([NUM] if kind == "finish" else []) + ([AG[low]] if kind != "first" else []):
                        last = nc.vector.memset(tile[:, 1, first_cols], 0.0)
                    last.then_inc(S["carry_ok"], 1)
                    dve.wait_ge(S["carry_ok"], 1 + CREDIT)

                    def carry_of(out_, part, u, h):
                        pu, ph = (u, 1 - h) if h == z else (1 - u, z)
                        return out_[part, pu, ph * HALF + end:ph * HALF + end + 1]

                    def spread_totals(t):
                        for i in range(len(units) + 1):
                            if i < len(units):
                                u, h = units[i]
                                here = TOT[low, u, cols(h)]
                                hold(dve, (S["maskl"][u], t * 16 + 16), (S["tot"][u], t * 16 + 16))
                                nc.vector.scalar_tensor_tensor(out=here, in0=KL[low, u, cols(h)], scalar=0.0, in1=here,
                                                               op0=ALU.is_equal, op1=ALU.mult).then_inc(S["masked"], 1)
                            if i > 0:
                                u, h = units[i - 1]
                                hold(dve, (S["masked"], md(t, u, h)), (S["agg_d"], md(t, u, h) - 1),
                                     (S[ag_used], fr(t, u, h)))
                                nc.vector.tensor_tensor_scan(
                                    out=along(AG[low, u, cols(h)]), data0=along(KL[low, u, cols(h)]),
                                    data1=along(TOT[low, u, cols(h)]), initial=carry_of(AG, low, u, h),
                                    op0=ALU.mult, op1=ALU.add).then_inc(S["agg_d"], 1)

                    def iteration(t, more):
                        def ve(name, fn, needs, frees=(), loads=(), store=None, us=units):
                            for u, h in us:
                                hold(dve, *[(S[a], md(t, u, h)) for a in needs], *[(S[a], fr(t, u, h)) for a in frees],
                                     *[landed(a, u) for a in loads], *([(S[store][u], kept_at(t))] if store else []))
                                fn(u, h).then_inc(S[name], 1)

                        def landed(name, u):
                            return (S[name][u], t * 32 + 32 if name == "row" else t * 16 + 16)

                        def stt(o, a, sc, b, op0, op1):
                            return lambda u, h: nc.vector.scalar_tensor_tensor(
                                out=o(u, h), in0=a(u, h), scalar=sc, in1=b(u, h), op0=op0, op1=op1)

                        def tt(o, a, b, op):
                            return lambda u, h: nc.vector.tensor_tensor(o(u, h), a(u, h), b(u, h), op)

                        def scan(name, out_, part, mask, data, op1, needs, frees=(), loads=(), store=None, us=units):
                            for u, h in us:
                                hold(dve, *[(S[a], md(t, u, h)) for a in needs], (S[name], md(t, u, h) - 1),
                                     *[(S[a], fr(t, u, h)) for a in frees], *[landed(a, u) for a in loads],
                                     *([(S[store][u], kept_at(t))] if store else []))
                                nc.vector.tensor_tensor_scan(
                                    out=along(out_[part, u, cols(h)]), data0=along(mask[part, u, cols(h)]),
                                    data1=along(data(u, h)), initial=carry_of(out_, part, u, h), op0=ALU.mult, op1=op1).then_inc(S[name], 1)

                        if kind == "gcn1":
                            ve("v0", tt(at(X), at(X), at(R), ALU.mult), [], [], ["state", "row"])
                        if kind in ("gcn1", "gcn2"):
                            for one in units:
                                ve("u1", tt(at(Y), at(AG), at(X), ALU.add),
                                   ["agg_d", "agg_s"] + (["v0"] if kind == "gcn1" else []), [], ["state"], us=[one])
                                ve("u", tt(at(Y), at(Y), at(R), ALU.mult), ["u1"], [], ["row"], us=[one])
                        if kind == "appnp_end":
                            for one in units:
                                ve("u1", stt(at(Y), at(AG), 1.0 - ALPHA, at(R), ALU.mult, ALU.mult), ["agg_d", "agg_s"],
                                   [], ["row"], us=[one])
                                ve("y", stt(at(Y), at(X), 1.0 + ALPHA, at(Y), ALU.mult, ALU.add), ["u1"], [], ["state"],
                                   us=[one])
                        if more and kind == "update":
                            spread_totals(t + 1)
                        if kind == "first":
                            ve("v", tt(at(XO), at(X), at(R), ALU.mult), [], ["scanned"], ["state", "row"])
                        if kind == "gcn1":
                            ve("v", tt(at(XO), at(H), at(R), ALU.mult), ["relu"], [], [], "xkept")
                        if kind == "gcn2":
                            ve("y", stt(at(Y), at(XS), 2.0, at(H), ALU.mult, ALU.add), ["relu"], [], ["skipped"])
                        if kind == "attend":
                            ve("y", tt(at(Y), at(XS), at(H), ALU.add), ["relu"], [], ["skipped"])
                        if kind == "finish":
                            ve("diff", tt(at(Y), at(MG), at(AG), ALU.subtract), ["msg", "agg_d"])
                            for one in units:
                                ve("wx", tt(at(WX), at(H), at(X), ALU.mult), ["ex"], [], ["state"], us=[one])
                                scan("scanned", ST, wide, KW, at(H), ALU.add, ["ex"], [], ["maskw"], us=[one])
                                scan("summed", NUM, wide, KW, at(WX), ALU.add, ["wx"], [], ["maskw"], us=[one])
                            ve("nf", tt(at(H), at(NUM), at(WX), ALU.mult), ["rden"])
                            ve("y", lambda u, h: nc.vector.scalar_tensor_tensor(
                                out=Y[:, u, cols(h)], in0=psM[u][h][:], scalar=bias[:, BC:BC + 1], in1=X[:, u, cols(h)],
                                op0=ALU.add, op1=ALU.add), ["mm"])
                        if more and kind in ("gcn2", "attend"):
                            spread_totals(t + 1)

                        def x_made(us):
                            ve("x", tt(at(XO), at(Y) if kind == "finish" else bank(psM), at(H), ALU.mult), ["rs"],
                               ["msg_mm"] if kind in ("appnp_end", "attend") else ["back"] if kind == "finish" else [], [],
                               "xkept" if x_out else None, us=us)

                        def sums(us):
                            data, need = (at(XO, wide), "v") if kind in ("first", "gcn1") else (at(MG, wide), "msg")
                            scan("scanned", ST, wide, KW, data, ALU.max if kind == "attend" else ALU.add, [need],
                                 ["back"] if kind != "attend" else [], ["maskw"], "totkept" if tot_out is not None else None,
                                 us=us)

                        if kind == "gcn2":
                            for i in range(len(units) + 2):
                                if i < len(units):
                                    x_made(units[i:i + 1])
                                if 0 < i <= len(units):
                                    ve("msg", tt(at(MG, wide), at(XO, wide), at(NSR, wide), ALU.mult), ["x"], [], ["nsrc"],
                                       us=units[i - 1:i])
                                if i > 1:
                                    sums(units[i - 2:i - 1])
                        else:
                            if norm:
                                x_made(units)
                            if kind != "finish":
                                sums(units)
                            if more and kind in ("gcn1", "appnp_end", "finish"):
                                spread_totals(t + 1)

                    if kind != "first":
                        spread_totals(0)
                    with dve.Fori(0, NS // 2 - 1) as t:
                        iteration(t, kind != "first")
                    iteration(NS // 2 - 1, False)

        node_pass("first", "F", tab_out=0, tot_out=0, x_in="X0")
        node_pass("gcn1", "R", 0, 1, 0, 1, "X0", "V1")
        with nc.sbuf_tensor("B_res", [P, NQ, D], f32) as B_res:
            node_pass("gcn2", "F", 1, 0, 1, None, "V1", "X1", skip="X0", B_res=B_res)
            assert APPNP_STEPS % 2 == 0 and APPNP_STEPS >= 4
            with nc.Fori(0, APPNP_STEPS // 2 - 1):
                appnp_pass(B_res, 0, 1)
                appnp_pass(B_res, 1, 0)
            appnp_pass(B_res, 0, 1, totT[0])
        node_pass("appnp_end", "R", 1, 0, 0, 1, "X1", "X2")
        node_pass("update", "F", 0, 1, 1, 0, "X2", "XA", layer=0)
        node_pass("update", "R", 1, 0, 0, 1, "XA", "XB", layer=1)
        node_pass("attend", "F", 0, None, 1, 0, "XB", "X3", skip="X2", layer=2)
        node_pass("finish", "R", None, None, 0, None, "X3")


_INS = ["x", "src", "dst", "edge_attr_16", "L0_gnn_W1", "L0_gnn_b1", "L0_gnn_W2", "L0_gnn_b2",
        "L2_gnn_msg_w", "L2_gnn_msg_b", "L2_gnn_upd_w", "L2_gnn_upd_b",
        "L3_gnn_W_lin", "L3_gnn_b_lin", "L3_gnn_W_out", "L3_gnn_b_out"]


def kernel(**inputs):
    import numpy as _np
    import concourse.bacc as _bacc
    from concourse.bass_utils import run_bass_kernel_spmd as _run

    nc = _bacc.Bacc("TRN2", target_bir_lowering=False, num_devices=1)
    arrays, args = {}, []
    for name in _INS:
        a = _np.ascontiguousarray(inputs[name])
        arrays[f"in_{name}"] = a
        args.append(nc.dram_tensor(f"in_{name}", a.shape, mybir.dt.from_np(a.dtype), kind="ExternalInput").ap())
    args.append(nc.dram_tensor("out_y", (N_NODES, D), mybir.dt.float32, kind="ExternalOutput").ap())
    build(nc, *args)
    r = _run(nc, [arrays], core_ids=[0])
    return r.results[0]["out_y"]
```
